# Optimizing a Trainium2 kernel written in Bass

```python
import numpy as np
import jax
import jax.numpy as jnp

def _softmax(x, axis=-1):
    return jax.nn.softmax(x, axis=axis)

def _gelu(x):
    return jax.nn.gelu(x, approximate=True)

def _silu(x):
    return jax.nn.silu(x)

def _sigmoid(x):
    return jax.nn.sigmoid(x)

def _layernorm(x, axis=-1, eps=1e-05):
    m = jnp.mean(x, axis=axis, keepdims=True)
    v = jnp.var(x, axis=axis, keepdims=True)
    return (x - m) / jnp.sqrt(v + eps)

def _scatter_add(tgt, idx, src, axis=0):
    return tgt.at[idx].add(src)

def _segment_sum(src, seg, n):
    return jax.ops.segment_sum(src, seg, n)
kernel_name = 'mk_prb_d2_jaxref_r8_a8e5d1'

def setup_inputs(seed: int=0):
    np.random.seed(seed)
    _w = jnp.asarray

    def _L0_attn_setup():
        import jax, jax.numpy as jnp
        import numpy as np
        B, N, DIM = (2, 256, 256)
        H, DH = (16, 128)
        SOFTCAP = 50.0
        SCALE = DH ** (-0.5)
        key = jax.random.key(seed)
        k1, k2, k3, k4 = jax.random.split(key, 4)
        s = 1.0 / np.sqrt(DIM)
        x = jax.random.normal(k1, (B, N, DIM), dtype=jnp.float32)
        w_qkv = jax.random.normal(k2, (DIM, 3 * H * DH), dtype=jnp.float32) * s
        w_gates = jax.random.normal(k3, (DIM, H), dtype=jnp.float32) * s
        w_out = jax.random.normal(k4, (H * DH, DIM), dtype=jnp.float32) * s
        return {'x': x, 'w_qkv': w_qkv, 'w_gates': w_gates, 'w_out': w_out}
    _L0_attn_in = _L0_attn_setup()

    def _L0_ffn_setup():
        import jax, jax.numpy as jnp
        import numpy as np
        HIDDEN = 256
        MOE_INTER = 128
        SHARED_INTER = 512
        N_EXPERTS = 16
        TOP_K = 2
        N_GROUP = 4
        TOPK_GROUP = 2
        NORM_TOPK_PROB = True
        ROUTED_SCALING = 1.0

        def relu2(x):
            r = jax.nn.relu(x)
            return r * r

        def _get_topk_indices(scores, e_bias):
            T, E = scores.shape
            s = scores + e_bias[None, :]
            gsz = E // N_GROUP
            group_scores = jax.lax.top_k(s.reshape(T, N_GROUP, gsz), 2)[0].sum(-1)
            group_idx = jax.lax.top_k(group_scores, TOPK_GROUP)[1]
            group_mask = jnp.zeros((T, N_GROUP), dtype=bool).at[jnp.arange(T)[:, None], group_idx].set(True)
            score_mask = jnp.repeat(group_mask, gsz, axis=1)
            masked = jnp.where(score_mask, s, 0.0)
            topk_indices = jax.lax.top_k(masked, TOP_K)[1]
            return jax.lax.stop_gradient(topk_indices)

        def _router(x_flat, router_weight, e_bias):
            logits = jnp.einsum('th,eh->te', x_flat.astype(jnp.float32), router_weight.astype(jnp.float32))
            scores = jax.nn.sigmoid(logits)
            topk_indices = _get_topk_indices(scores, e_bias)
            topk_weights = jnp.take_along_axis(scores, topk_indices, axis=1)
            if NORM_TOPK_PROB:
                topk_weights = topk_weights / (topk_weights.sum(-1, keepdims=True) + 1e-20)
            return (topk_indices, topk_weights * ROUTED_SCALING)
        key = jax.random.key(seed)
        ks = jax.random.split(key, 6)
        s = 0.02
        hidden_states = jax.random.normal(ks[0], (1, 256, HIDDEN), dtype=jnp.float32)
        router_weight = jax.random.normal(ks[1], (N_EXPERTS, HIDDEN), dtype=jnp.float32) * s
        e_bias = jnp.zeros((N_EXPERTS,), dtype=jnp.float32)
        w_up = jax.random.normal(ks[2], (N_EXPERTS, HIDDEN, MOE_INTER), dtype=jnp.float32) * s
        w_down = jax.random.normal(ks[3], (N_EXPERTS, MOE_INTER, HIDDEN), dtype=jnp.float32) * s
        shared_up = jax.random.normal(ks[4], (HIDDEN, SHARED_INTER), dtype=jnp.float32) * s
        shared_down = jax.random.normal(ks[5], (SHARED_INTER, HIDDEN), dtype=jnp.float32) * s
        return {'hidden_states': hidden_states, 'router_weight': router_weight, 'e_bias': e_bias, 'w_up': w_up, 'w_down': w_down, 'shared_up': shared_up, 'shared_down': shared_down}
    _L0_ffn_in = _L0_ffn_setup()

    def _L1_attn_setup():
        import math
        import jax, jax.numpy as jnp
        import numpy as np
        B, S, D, H, DH = (2, 256, 256, 16, 128)

        def _alibi_slopes(n):

            def pow2(m):
                start = 2 ** (-2 ** (-(math.log2(m) - 3)))
                return [start * start ** i for i in range(m)]
            if math.log2(n).is_integer():
                return pow2(n)
            c = 2 ** math.floor(math.log2(n))
            return pow2(c) + _alibi_slopes(2 * c)[0::2][:n - c]

        def _alibi_mask(n_heads, q_len, kv_len):
            slopes = jnp.asarray(np.array(_alibi_slopes(n_heads), dtype=np.float32))
            bias = slopes[:, None, None] * jnp.arange(kv_len, dtype=jnp.float32)[None, None, :]
            i = jnp.arange(q_len)[:, None]
            j = jnp.arange(kv_len)[None, :]
            causal = jnp.where(j > i, -jnp.inf, 0.0).astype(jnp.float32)
            return causal[None, :, :] + bias
        key = jax.random.key(seed)
        k1, k2, k3, k4, k5 = jax.random.split(key, 5)
        scale = 1.0 / math.sqrt(D)
        return {'resid_pre': jax.random.normal(k1, (B, S, D), dtype=jnp.float32), 'Wq': jax.random.normal(k2, (H * DH, D), dtype=jnp.float32) * scale, 'Wk': jax.random.normal(k3, (H * DH, D), dtype=jnp.float32) * scale, 'Wv': jax.random.normal(k4, (H * DH, D), dtype=jnp.float32) * scale, 'Wo': jax.random.normal(k5, (D, H * DH), dtype=jnp.float32) * scale}
    _L1_attn_in = _L1_attn_setup()

    def _L1_ffn_setup():
        import jax, jax.numpy as jnp
        import numpy as np
        B, S, H = (2, 256, 256)
        E, K, I = (8, 2, 704)
        key = jax.random.key(seed)
        ks = jax.random.split(key, 5)
        scale_h = 1.0 / np.sqrt(H)
        scale_i = 1.0 / np.sqrt(I)
        return {'hidden_states': jax.random.normal(ks[0], (B, S, H), dtype=jnp.float32), 'router_w': jax.random.normal(ks[1], (E, H), dtype=jnp.float32) * scale_h, 'gate_w': jax.random.normal(ks[2], (E, I, H), dtype=jnp.float32) * scale_h, 'up_w': jax.random.normal(ks[3], (E, I, H), dtype=jnp.float32) * scale_h, 'down_w': jax.random.normal(ks[4], (E, H, I), dtype=jnp.float32) * scale_i}
    _L1_ffn_in = _L1_ffn_setup()
    _d = {'L0_attn_x': _L0_attn_in['x'], 'L0_attn_w_qkv': _L0_attn_in['w_qkv'], 'L0_attn_w_gates': _L0_attn_in['w_gates'], 'L0_attn_w_out': _L0_attn_in['w_out'], 'L0_ffn_router_weight': _L0_ffn_in['router_weight'], 'L0_ffn_e_bias': _L0_ffn_in['e_bias'], 'L0_ffn_w_up': _L0_ffn_in['w_up'], 'L0_ffn_w_down': _L0_ffn_in['w_down'], 'L0_ffn_shared_up': _L0_ffn_in['shared_up'], 'L0_ffn_shared_down': _L0_ffn_in['shared_down'], 'L1_attn_Wq': _L1_attn_in['Wq'], 'L1_attn_Wk': _L1_attn_in['Wk'], 'L1_attn_Wv': _L1_attn_in['Wv'], 'L1_attn_Wo': _L1_attn_in['Wo'], 'L1_ffn_router_w': _L1_ffn_in['router_w'], 'L1_ffn_gate_w': _L1_ffn_in['gate_w'], 'L1_ffn_up_w': _L1_ffn_in['up_w'], 'L1_ffn_down_w': _L1_ffn_in['down_w']}
    _x0 = _d['L0_attn_x']
    _d['L0_attn_x'] = jax.random.normal(jax.random.fold_in(jax.random.key(seed), 1), (4, 256, 256), dtype=_x0.dtype)
    del _x0
    return _d

def reference(L0_attn_x, L0_attn_w_qkv, L0_attn_w_gates, L0_attn_w_out, L0_ffn_router_weight, L0_ffn_e_bias, L0_ffn_w_up, L0_ffn_w_down, L0_ffn_shared_up, L0_ffn_shared_down, L1_attn_Wq, L1_attn_Wk, L1_attn_Wv, L1_attn_Wo, L1_ffn_router_w, L1_ffn_gate_w, L1_ffn_up_w, L1_ffn_down_w):

    def _L0_attn_ref(x, w_qkv, w_gates, w_out):
        import jax, jax.numpy as jnp
        import numpy as np
        B, N, DIM = (2, 256, 256)
        H, DH = (16, 128)
        SOFTCAP = 50.0
        SCALE = DH ** (-0.5)
        b, n, _ = x.shape
        qkv = (x @ w_qkv).reshape(b, n, 3, H, DH).transpose(2, 0, 3, 1, 4)
        q, k, v = (qkv[0], qkv[1], qkv[2])
        q = q * SCALE
        sim = jnp.einsum('bhid,bhjd->bhij', q, k)
        sim = jnp.tanh(sim / SOFTCAP) * SOFTCAP
        mask_value = -jnp.finfo(sim.dtype).max
        causal_mask = jnp.triu(jnp.ones((n, n), dtype=bool), 1)
        sim = jnp.where(causal_mask, mask_value, sim)
        attn = jax.nn.softmax(sim, axis=-1)
        out = jnp.einsum('bhij,bhjd->bhid', attn, v)
        gates = jax.nn.sigmoid(x @ w_gates)
        out = out * gates.transpose(0, 2, 1)[..., None]
        out = out.transpose(0, 2, 1, 3).reshape(b, n, H * DH) @ w_out
        return out

    def _L0_ffn_ref(hidden_states, router_weight, e_bias, w_up, w_down, shared_up, shared_down):
        import jax, jax.numpy as jnp
        import numpy as np
        HIDDEN = 256
        MOE_INTER = 128
        SHARED_INTER = 512
        N_EXPERTS = 16
        TOP_K = 2
        N_GROUP = 4
        TOPK_GROUP = 2
        NORM_TOPK_PROB = True
        ROUTED_SCALING = 1.0

        def relu2(x):
            r = jax.nn.relu(x)
            return r * r

        def _get_topk_indices(scores, e_bias):
            T, E = scores.shape
            s = scores + e_bias[None, :]
            gsz = E // N_GROUP
            group_scores = jax.lax.top_k(s.reshape(T, N_GROUP, gsz), 2)[0].sum(-1)
            group_idx = jax.lax.top_k(group_scores, TOPK_GROUP)[1]
            group_mask = jnp.zeros((T, N_GROUP), dtype=bool).at[jnp.arange(T)[:, None], group_idx].set(True)
            score_mask = jnp.repeat(group_mask, gsz, axis=1)
            masked = jnp.where(score_mask, s, 0.0)
            topk_indices = jax.lax.top_k(masked, TOP_K)[1]
            return jax.lax.stop_gradient(topk_indices)

        def _router(x_flat, router_weight, e_bias):
            logits = jnp.einsum('th,eh->te', x_flat.astype(jnp.float32), router_weight.astype(jnp.float32))
            scores = jax.nn.sigmoid(logits)
            topk_indices = _get_topk_indices(scores, e_bias)
            topk_weights = jnp.take_along_axis(scores, topk_indices, axis=1)
            if NORM_TOPK_PROB:
                topk_weights = topk_weights / (topk_weights.sum(-1, keepdims=True) + 1e-20)
            return (topk_indices, topk_weights * ROUTED_SCALING)
        orig_shape = hidden_states.shape
        x = hidden_states.reshape(-1, HIDDEN)
        T = x.shape[0]
        topk_indices, topk_weights = _router(x, router_weight, e_bias)
        combine = jnp.zeros((T, N_EXPERTS), dtype=topk_weights.dtype).at[jnp.arange(T)[:, None], topk_indices].add(topk_weights)
        h1 = jnp.einsum('th,ehi->tei', x, w_up)
        a = relu2(h1) * combine[:, :, None]
        routed = jnp.einsum('tei,eih->th', a, w_down)
        shared = relu2(hidden_states @ shared_up) @ shared_down
        return routed.reshape(orig_shape) + shared

    def _L1_attn_ref(resid_pre, Wq, Wk, Wv, Wo):
        import math
        import jax, jax.numpy as jnp
        import numpy as np
        B, S, D, H, DH = (2, 256, 256, 16, 128)

        def _alibi_slopes(n):

            def pow2(m):
                start = 2 ** (-2 ** (-(math.log2(m) - 3)))
                return [start * start ** i for i in range(m)]
            if math.log2(n).is_integer():
                return pow2(n)
            c = 2 ** math.floor(math.log2(n))
            return pow2(c) + _alibi_slopes(2 * c)[0::2][:n - c]

        def _alibi_mask(n_heads, q_len, kv_len):
            slopes = jnp.asarray(np.array(_alibi_slopes(n_heads), dtype=np.float32))
            bias = slopes[:, None, None] * jnp.arange(kv_len, dtype=jnp.float32)[None, None, :]
            i = jnp.arange(q_len)[:, None]
            j = jnp.arange(kv_len)[None, :]
            causal = jnp.where(j > i, -jnp.inf, 0.0).astype(jnp.float32)
            return causal[None, :, :] + bias
        b, s, d = resid_pre.shape
        q = (resid_pre @ Wq.T).reshape(b, s, H, DH)
        k = (resid_pre @ Wk.T).reshape(b, s, H, DH)
        v = (resid_pre @ Wv.T).reshape(b, s, H, DH)
        scores = jnp.einsum('bqhd,bkhd->bhqk', q, k) / math.sqrt(DH)
        scores = jnp.clip(scores, -1024.0, 1024.0)
        scores = scores + _alibi_mask(H, s, s)[None]
        attn = jax.nn.softmax(scores.astype(jnp.float32), axis=-1).astype(q.dtype)
        z = jnp.einsum('bhqk,bkhd->bqhd', attn, v)
        out = jnp.einsum('bqhd,ohd->bqo', z, Wo.reshape(d, H, DH))
        return out

    def _L1_ffn_ref(hidden_states, router_w, gate_w, up_w, down_w):
        import jax, jax.numpy as jnp
        import numpy as np
        B, S, H = (2, 256, 256)
        E, K, I = (8, 2, 704)
        b, s, h = hidden_states.shape
        x = hidden_states.reshape(-1, h)
        logits = x @ router_w.T
        probs = jax.nn.softmax(logits, axis=-1)
        topk_w, topk_idx = jax.lax.top_k(probs, K)
        coef = jnp.sum(jax.nn.one_hot(topk_idx, E, dtype=x.dtype) * topk_w[..., None], axis=1)
        out = jnp.zeros_like(x)
        for e in range(E):
            g = x @ gate_w[e].T
            u = x @ up_w[e].T
            y = jax.nn.silu(g) * u @ down_w[e].T
            out = out + coef[:, e, None] * y
        return out.reshape(b, s, h)
    x = L0_attn_x
    xn = _layernorm(x, axis=-1)
    x = x + _L0_attn_ref(xn, L0_attn_w_qkv, L0_attn_w_gates, L0_attn_w_out) + _L0_ffn_ref(xn, L0_ffn_router_weight, L0_ffn_e_bias, L0_ffn_w_up, L0_ffn_w_down, L0_ffn_shared_up, L0_ffn_shared_down)
    xn = _layernorm(x, axis=-1)
    x = x + _L1_attn_ref(xn, L1_attn_Wq, L1_attn_Wk, L1_attn_Wv, L1_attn_Wo) + _L1_ffn_ref(xn, L1_ffn_router_w, L1_ffn_gate_w, L1_ffn_up_w, L1_ffn_down_w)
    return x

_drawn_inputs = setup_inputs


def setup_inputs(seed=0):
    import zlib

    import numpy as np

    out = dict(_drawn_inputs(seed))
    spreads = {'L0_ffn_e_bias': (0.0, 0.1)}
    factors = {}
    for name, (base, spread) in spreads.items():
        noise = np.random.default_rng([zlib.crc32(name.encode()), seed]).standard_normal(out[name].shape)
        drawn = base * np.exp(spread * noise) if base else spread * noise
        out[name] = jnp.asarray(drawn.astype(out[name].dtype))
    for name, factor in factors.items():
        out[name] = (out[name] * factor).astype(out[name].dtype)
    return out
```

```python
from contextlib import ExitStack

import concourse.bass as bass
from concourse import mybir

F32 = mybir.dt.float32
F32R = mybir.dt.float32r
ALU = mybir.AluOpType
ACT = mybir.ActivationFunctionType
X_AXIS = mybir.AxisListType.X

P = 128
D = 256
KC = D // P
SEQS = 4
TILES = 8
TOK = TILES * P
HALF = TOK // 2
HEADS = 16
PAIRS = HEADS // 2
E0, SHARED, E1 = 16, 4, 8
UNITS = E0 + SHARED
FULL, TAIL = 5, 64
CH = FULL + 1
GU = FULL * KC * 2 * P + KC * P
CAP = 50.0
SCALE = float(P) ** -0.5
CLIP = 1024.0
NEG = -1e30
EPS = 1e-5


def bass_two_layers(nc, x_d, const_d, alibi_d, qk_d, v_d, o_d, router_d, up_d, down_d, gu_d, down1_d, out_d):
    with ExitStack() as ctx:
        def sb(name, shape, dt=F32):
            return ctx.enter_context(nc.sbuf_tensor(name, shape, dt))

        def sem(name):
            return ctx.enter_context(nc.semaphore(name))

        H1 = 2 * 2 * CH * HALF
        parts = sb("parts", [P, H1 + 2 * GU + 2 * CH * D], F32R)

        def region(at, *dims):
            n = 1
            for d in dims:
                n *= d
            names = " ".join(f"a{i}" for i in range(len(dims)))
            sizes = {f"a{i}": d for i, d in enumerate(dims)}
            return parts[:, at:at + n].rearrange(f"p ({names}) -> p {names}", **sizes)

        qk_w = region(0, 2, 2, KC, 2 * P)
        v_w = region(2048, 2, KC, 2 * P)
        o_w = region(3072, 2, 2, D)
        z_p = region(4096, 2, 2, TOK)
        h0_p = region(8192, 2, 2, TOK)
        h1_p = region(0, 2, 2, CH, HALF)
        gu_w = region(H1, 2, GU)
        down1_w = region(H1 + 2 * GU, 2, CH, D)
        up_w = region(H1, 2, 2, KC, P)
        down_w = region(H1 + 1024, 2, 2, D)
        xn_t = sb("xn_t", [P, 2, KC, TOK], F32R)
        router_w = sb("router_w", [P, 2, KC, 32], F32R)

        x_sb = sb("x_sb", [P, TILES, D])
        qk = sb("qk", [P, 2, 2, TOK])
        xn = qk[:, :, :, :].rearrange("p a b t -> p (a b t)")[:, 0:TILES * D].rearrange("p (t d) -> p t d", t=TILES)
        v_sb = sb("v_sb", [P, TILES, 2 * P])
        sc = sb("sc", [P, SEQS, 3 * P])
        pr = sb("pr", [P, SEQS, 3 * P])
        pr_t = sb("pr_t", [P, SEQS, 3 * P])
        qk_raw = sb("qk_raw", [P, 2, KC * 2 * P])
        v_raw = sb("v_raw", [P, KC * 2 * P])
        o_raw = sb("o_raw", [P, 2 * D])
        alibi = sb("alibi", [P, 2, 3 * P])
        up_raw = sb("up_raw", [P, 2, KC * P])
        down_raw = sb("down_raw", [P, 2, D])
        gu_raw = sb("gu_raw", [P, GU])
        down1_raw = sb("down1_raw", [P, CH * D])
        router_raw = sb("router_raw", [P, KC, 32])
        const = sb("const", [P, 608])
        ident = const[:, 0:128]
        future = const[:, 480:608]
        e_bias = const[:, 128:144]
        tri16 = const[:, 144:400].rearrange("p (a b) -> p a b", a=16)
        tri4 = const[:, 400:416].rearrange("p (a b) -> p a b", a=4)
        tri8 = const[:, 416:480].rearrange("p (a b) -> p a b", a=8)
        gate_act = sc[:, :, :].rearrange("p b c -> p (b c)")[:, 0:2 * HALF].rearrange("p (s t) -> p s t", s=2)
        hid = pr[:, :, :].rearrange("p b c -> p (b c)")[:, 0:2 * HALF].rearrange("p (s t) -> p s t", s=2)
        row_sum = sb("row_sum", [P, SEQS, 2])
        row_max = sb("row_max", [P, SEQS, 2])
        neg_max = sb("neg_max", [P, SEQS, 2])
        row_scale = sb("row_scale", [P, SEQS, 2])
        stats = sb("stats", [P, TILES, 6])
        mean_var = sb("mean_var", [P, TILES, 2])
        var_eps = sb("var_eps", [P, TILES])
        std = sb("std", [P, TILES])
        rstd = sb("rstd", [P, TILES])
        newton = sb("newton", [P, TILES])
        logits = sb("logits", [P, TILES, 32])
        sig = sb("sig", [P, TILES, 32])
        coef = sb("coef", [P, TILES, UNITS])
        small = sb("small", [P, 8, 32])
        groups = sb("groups", [P, TILES, 4])
        choice = sb("choice", [P, TILES, 16])
        rank = sb("rank", [P, TILES, 16])
        per_tile = sb("per_tile", [P, 2, TILES])
        beats = gu_raw[:, 0:1024]
        ties = gu_raw[:, 1024:2048]
        beats1 = sc[:, :, :].rearrange("p b c -> p (b c)")[:, 0:512]
        ties1 = sc[:, :, :].rearrange("p b c -> p (b c)")[:, 512:1024]

        psum = ctx.enter_context(nc.psum_tensor("psum", [P, 8, 512], F32))
        proj_bank, score_bank, prt_bank, z_bank = (0, 1), (2, 3), (4, 5), (6, 7)
        up_bank, down_bank = (0, 1, 2, 3), (4, 5, 6, 7)

        x_loaded, const_loaded = sem("x_loaded"), sem("const_loaded")
        router_loaded = sem("router_loaded")
        qk_loaded = [sem(f"qk_loaded{s}") for s in range(2)]
        alibi_loaded = [sem(f"alibi_loaded{s}") for s in range(2)]
        v_loaded, o_loaded = sem("v_loaded"), sem("o_loaded")
        up_loaded = [sem(f"up_loaded{s}") for s in range(2)]
        down_loaded = [sem(f"down_loaded{s}") for s in range(2)]
        gu_loaded, down1_loaded = sem("gu_loaded"), sem("down1_loaded")
        qk_w_hi, qk_w_split = sem("qk_w_hi"), sem("qk_w_split")
        v_w_hi, v_w_split = sem("v_w_hi"), sem("v_w_split")
        o_w_hi, o_w_split = sem("o_w_hi"), sem("o_w_split")
        up_w_hi, up_w_split = sem("up_w_hi"), sem("up_w_split")
        down_w_hi, down_w_split = sem("down_w_hi"), sem("down_w_split")
        gu_w_hi, gu_w_split = sem("gu_w_hi"), sem("gu_w_split")
        down1_w_hi, down1_w_split = sem("down1_w_hi"), sem("down1_w_split")
        router_hi, router_split = sem("router_hi"), sem("router_split")
        dve_chain = sem("dve_chain")
        var_ready, std_ready = sem("var_ready"), sem("std_ready")
        xn_ready, xn_turned, xn_hi, xn_split = sem("xn_ready"), sem("xn_turned"), sem("xn_hi"), sem("xn_split")
        logits_done, logits_copied, logits_exp = sem("logits_done"), sem("logits_copied"), sem("logits_exp")
        qk_done, qk_copied = sem("qk_done"), sem("qk_copied")
        v_done, v_copied = sem("v_done"), sem("v_copied")
        o_done, o_added = sem("o_done"), sem("o_added")
        scores_done, scores_read = sem("scores_done"), sem("scores_read")
        masked, max_ready, negmax_ready = sem("masked"), sem("max_ready"), sem("negmax_ready")
        exp_done, recip_done, row_scaled, probs_ready = (sem("exp_done"), sem("recip_done"), sem("row_scaled"),
                                                         sem("probs_ready"))
        turned, turned_copied = sem("turned"), sem("turned_copied")
        z_done, z_hi, z_split = sem("z_done"), sem("z_hi"), sem("z_split")
        up_done, relu_done, square_done, hid_hi, hid_split = (sem("up_done"), sem("relu_done"), sem("square_done"),
                                                              sem("hid_hi"), sem("hid_split"))
        down_done, y_added = sem("down_done"), sem("y_added")
        gu_done, silu_done, mul_done, hid1_hi, hid1_split = (sem("gu_done"), sem("silu_done"), sem("mul_done"),
                                                             sem("hid1_hi"), sem("hid1_split"))
        down1_done, y1_added = sem("down1_done"), sem("y1_added")
        pad_zero = sem("pad_zero")
        stored = sem("stored")

        block = ctx.enter_context(nc.Block())

        @block.sync
        def _(sp):
            sp.dma_start(x_sb[:, :, :], x_d).then_inc(x_loaded, 16)
            sp.dma_start(const[:, :], const_d).then_inc(const_loaded, 16)
            for L in range(2):
                W = 32 if L == 0 else E1
                if L == 1:
                    sp.wait_ge(router_split, 1)
                sp.dma_start(router_raw[:, :, 0:W], router_d[L]).then_inc(router_loaded, 16)

                def load_qk(h, s):
                    sp.dma_start(qk_raw[:, s, :], qk_d[L][h]).then_inc(qk_loaded[s], 16)

                def load_v(p):
                    sp.dma_start(v_raw[:, :], v_d[L][p]).then_inc(v_loaded, 16)

                def load_o(p):
                    sp.dma_start(o_raw[:, :], o_d[L][p]).then_inc(o_loaded, 16)

                def load_alibi(h, s):
                    sp.dma_start(alibi[:, s, :], alibi_d[h]).then_inc(alibi_loaded[s], 16)

                if L == 1:
                    sp.wait_ge(qk_w_split, HEADS)
                    sp.wait_ge(v_w_split, PAIRS)
                load_qk(0, 0)
                load_v(0)
                load_qk(1, 1)
                if L == 1:
                    sp.wait_ge(o_w_split, PAIRS)
                    load_alibi(0, 0)
                    load_alibi(1, 1)
                load_o(0)
                if L == 0:
                    for u in range(2):
                        sp.dma_start(up_raw[:, u, :], up_d[u]).then_inc(up_loaded[u], 16)
                        sp.dma_start(down_raw[:, u, :], down_d[u]).then_inc(down_loaded[u], 16)
                else:
                    sp.dma_start(gu_raw[:, :], gu_d[0]).then_inc(gu_loaded, 16)
                    sp.dma_start(down1_raw[:, :], down1_d[0]).then_inc(down1_loaded, 16)

                def next_pair(p, first=False):
                    sp.wait_ge(qk_w_split, 2 * p + (L * HEADS + 1))
                    load_qk(2 * p + 2, 0)
                    sp.wait_ge(v_w_split, p + (L * PAIRS + 1))
                    load_v(p + 1)
                    sp.wait_ge(qk_w_split, 2 * p + (L * HEADS + 2))
                    load_qk(2 * p + 3, 1)
                    if not first:
                        sp.wait_ge(o_w_split, p + L * PAIRS)
                        load_o(p)
                    if L == 1:
                        sp.wait_ge(max_ready, 16 * p + 8)
                        load_alibi(2 * p + 2, 0)
                        sp.wait_ge(max_ready, 16 * p + 16)
                        load_alibi(2 * p + 3, 1)

                next_pair(0, first=True)
                with sp.Fori(1, PAIRS - 1) as p:
                    next_pair(p)
                sp.wait_ge(o_w_split, L * PAIRS + PAIRS - 1)
                load_o(PAIRS - 1)
                if L == 0:
                    with sp.Fori(0, UNITS // 2 - 1) as i:
                        for s in range(2):
                            sp.wait_ge(up_w_split, 2 * i + (s + 1))
                            sp.dma_start(up_raw[:, s, :], up_d[2 * i + (2 + s)]).then_inc(up_loaded[s], 16)
                            sp.wait_ge(down_w_split, 2 * i + (s + 1))
                            sp.dma_start(down_raw[:, s, :], down_d[2 * i + (2 + s)]).then_inc(down_loaded[s], 16)
                else:
                    with sp.Fori(0, E1 - 1) as e:
                        sp.wait_ge(gu_w_split, CH * e + CH)
                        sp.dma_start(gu_raw[:, :], gu_d[e + 1]).then_inc(gu_loaded, 16)
                        sp.wait_ge(down1_w_split, 3 * e + 3)
                        sp.dma_start(down1_raw[:, :], down1_d[e + 1]).then_inc(down1_loaded, 16)
            for j in range(4):
                sp.wait_ge(y1_added, 4 * (E1 - 1) + j + 1)
                sp.dma_start(out_d[:, 2 * j:2 * j + 2, :], x_sb[:, 2 * j:2 * j + 2, :]).then_inc(stored, 16)
            sp.wait_ge(stored, 64)

        @block.tensor
        def _(pe):
            def product(out, w, x, first, last):
                nc.tensor.matmul(out, w[1], x[0], start=first, stop=False)
                nc.tensor.matmul(out, w[0], x[1], start=False, stop=False)
                return nc.tensor.matmul(out, w[0], x[0], start=False, stop=last)

            def xn_half(kc, half):
                return tuple(xn_t[:, i, kc, half * HALF:(half + 1) * HALF] for i in range(2))

            def xn_tile(kc, t):
                return tuple(xn_t[:, i, kc, t * P:(t + 1) * P] for i in range(2))

            def turn_xn(L):
                if L == 0:
                    pe.wait_ge(const_loaded, 16)
                for half in range(2):
                    pe.wait_ge(xn_ready, TILES * L + 4 * half + 4)
                    for kc in range(KC):
                        for t in range(4):
                            last = nc.tensor.transpose(psum[:, 2 + 2 * half + kc, t * P:(t + 1) * P],
                                                       xn[:, 4 * half + t, kc * P:(kc + 1) * P], ident)
                        last.then_inc(xn_turned, 1)

            def router(L):
                W = 32 if L == 0 else E1
                pe.wait_ge(router_split, L + 1)
                for t in range(TILES):
                    for kc in range(KC):
                        last = product(psum[:, 6, t * W:(t + 1) * W], xn_tile(kc, t),
                                       (router_w[:, 0, kc, 0:W], router_w[:, 1, kc, 0:W]), kc == 0, kc == KC - 1)
                last.then_inc(logits_done, 1)

            def project_qk(L, p, s, before, turning=None):
                head = 2 * p + (L * HEADS + s)
                for j in range(4):
                    half, c = j // 2, j % 2
                    if turning is not None:
                        turn_probs(*turning, j)
                    if j == 0:
                        pe.wait_ge(qk_w_split, head + 1)
                    if j < 2 and before is not None:
                        pe.wait_ge(before[0], before[1] + j)
                    if j >= 2:
                        pe.wait_ge(qk_copied, 4 * head + (j - 1))
                    for kc in range(KC):
                        w = tuple(qk_w[:, s, i, kc, c * P:(c + 1) * P] for i in range(2))
                        last = product(psum[:, proj_bank[j % 2], :], w, xn_half(kc, half), kc == 0, kc == KC - 1)
                    last.then_inc(qk_done, 1)

            def project_v(L, p):
                pair = p + L * PAIRS
                pe.wait_ge(v_w_split, pair + 1)
                for j in range(4):
                    if j < 2:
                        pe.wait_ge(qk_copied, 8 * pair + (j + 3))
                    else:
                        pe.wait_ge(v_copied, 4 * pair + (j - 1))
                    for i in range(2):
                        t = 2 * j + i
                        for kc in range(KC):
                            w = tuple(v_w[:, k, kc, :] for k in range(2))
                            last = product(psum[:, proj_bank[j % 2], i * D:(i + 1) * D], xn_tile(kc, t), w,
                                           kc == 0, kc == KC - 1)
                    last.then_inc(v_done, 1)

            def project_out(L, p, before):
                pair = p + L * PAIRS
                pe.wait_ge(o_w_split, pair + 1)
                pe.wait_ge(z_split, 4 * pair + 4)
                for j in range(4):
                    if j < 2:
                        pe.wait_ge(before[0], before[1] + j)
                    else:
                        pe.wait_ge(o_added, 4 * pair + (j - 1))
                    for i in range(2):
                        t = 2 * j + i
                        for s in range(2):
                            z = tuple(z_p[:, s, k, t * P:(t + 1) * P] for k in range(2))
                            w = tuple(o_w[:, k, s, :] for k in range(2))
                            last = product(psum[:, proj_bank[j % 2], i * D:(i + 1) * D], z, w, s == 0, s == 1)
                    last.then_inc(o_done, 1)

            def scores(head, s, b, first):
                if b % 2 == 0:
                    pe.wait_ge(qk_copied, 4 * head + (b + 2))
                if not (first and b < 2):
                    pe.wait_ge(scores_read, 4 * head + (b - 1))
                bank = psum[:, score_bank[b % 2], :]
                q, k = qk[:, s, 0, :], qk[:, s, 1, :]
                nc.tensor.matmul(bank[:, 0:P], q[:, 2 * b * P:(2 * b + 1) * P], k[:, 2 * b * P:(2 * b + 1) * P],
                                 start=True, stop=True)
                nc.tensor.matmul(bank[:, P:3 * P], q[:, (2 * b + 1) * P:(2 * b + 2) * P],
                                 k[:, 2 * b * P:(2 * b + 2) * P], start=True, stop=True).then_inc(scores_done, 1)

            def turn_probs(head, first, b):
                pe.wait_ge(probs_ready, 4 * head + (b + 1))
                if not (first and b < 2):
                    pe.wait_ge(turned_copied, 4 * head + (b - 1))
                for c in range(3):
                    last = nc.tensor.transpose(psum[:, prt_bank[b % 2], c * P:(c + 1) * P],
                                               pr[:, b, c * P:(c + 1) * P], ident)
                last.then_inc(turned, 1)

            def attend(head, pair, s, b, first):
                if s == 0 and b == 0:
                    pe.wait_ge(v_copied, 4 * pair + 4)
                if b % 2 == 0 and not first:
                    pe.wait_ge(z_split, 2 * head + (b // 2 - 1))
                pe.wait_ge(turned_copied, 4 * head + (b + 1))
                z = psum[:, z_bank[b // 2], (b % 2) * 2 * P:(b % 2 + 1) * 2 * P]
                nc.tensor.matmul(z, v_sb[:, 2 * b, s * P:(s + 1) * P], pr_t[:, b, 0:2 * P], start=True, stop=False)
                last = nc.tensor.matmul(z[:, P:2 * P], v_sb[:, 2 * b + 1, s * P:(s + 1) * P],
                                        pr_t[:, b, 2 * P:3 * P], start=False, stop=True)
                if b % 2 == 1:
                    last.then_inc(z_done, 1)

            def pair_steps(L, p, first=False, last=False):
                pair = p + L * PAIRS
                start = first and L == 0
                for b in (0, 1):
                    scores(2 * pair, 0, b, start)
                if not first:
                    for b in (0, 1):
                        attend(2 * pair - 1, pair - 1, 1, b, False)
                for b in (2, 3):
                    scores(2 * pair, 0, b, start)
                if not first:
                    for b in (2, 3):
                        attend(2 * pair - 1, pair - 1, 1, b, False)
                project_v(L, p)
                project_qk(L, p, 1, (v_copied, 4 * pair + 3), (2 * pair, start))
                for b in (0, 1):
                    scores(2 * pair + 1, 1, b, False)
                if first:
                    pe.wait_ge(logits_copied, L + 1)
                for b in (0, 1):
                    attend(2 * pair, pair, 0, b, start)
                for b in (2, 3):
                    scores(2 * pair + 1, 1, b, False)
                for b in (2, 3):
                    attend(2 * pair, pair, 0, b, start)
                if not first:
                    project_out(L, p - 1, (qk_copied, 8 * pair + 7))
                if not last:
                    project_qk(L, p + 1, 0, (qk_copied, 8 * pair + 7) if first else (o_added, 4 * pair - 1),
                               (2 * pair + 1, False))
                else:
                    for b in range(SEQS):
                        turn_probs(2 * pair + 1, False, b)

            def up(u, s, first):
                pe.wait_ge(up_w_split, u + 1)
                for half in range(2):
                    if not first:
                        pe.wait_ge(relu_done, 2 * u + (half - 3))
                    for kc in range(KC):
                        w = tuple(up_w[:, s, i, kc, :] for i in range(2))
                        last = product(psum[:, up_bank[2 * s + half], :], w, xn_half(kc, half), kc == 0, kc == KC - 1)
                    last.then_inc(up_done, 1)

            def down(u, s, first):
                pe.wait_ge(down_w_split, u + 1)
                for j in range(4):
                    if j % 2 == 0:
                        pe.wait_ge(hid_split, 2 * u + (j // 2 + 1))
                    if not first:
                        pe.wait_ge(y_added, 4 * u + (j - 3))
                    for i in range(2):
                        t = 2 * j + i
                        h = tuple(h0_p[:, s, k, t * P:(t + 1) * P] for k in range(2))
                        last = product(psum[:, down_bank[j], i * D:(i + 1) * D], h,
                                       (down_w[:, s, 0, :], down_w[:, s, 1, :]), True, True)
                    last.then_inc(down_done, 1)

            def gate_up(e, half, first):
                for c in range(CH):
                    if half == 0:
                        pe.wait_ge(gu_w_split, CH * e + (c + 1))
                    if not (first and c < 2):
                        pe.wait_ge(mul_done, 12 * e + (6 * half + c - 1))
                    n = 2 if c < FULL else 1
                    at = c * KC * 2 * P
                    for g in range(n):
                        for kc in range(KC):
                            col = at + kc * n * P + g * P
                            last = product(psum[:, up_bank[2 * (c % 2) + g], :],
                                           (gu_w[:, 0, col:col + P], gu_w[:, 1, col:col + P]),
                                           xn_half(kc, half), kc == 0, kc == KC - 1)
                    last.then_inc(gu_done, 1)

            def down1(e, half, first):
                if half == 0:
                    pe.wait_ge(down1_w_split, 3 * e + 3)
                pe.wait_ge(hid1_split, 12 * e + (6 * half + 6))
                for j in range(2):
                    if not first:
                        pe.wait_ge(y1_added, 4 * e + (2 * half + j - 3))
                    for i in range(2):
                        t = 2 * j + i
                        for c in range(CH):
                            h = tuple(h1_p[:, half, k, c, t * P:(t + 1) * P] for k in range(2))
                            w = tuple(down1_w[:, k, c, :] for k in range(2))
                            last = product(psum[:, down_bank[2 * half + j], i * D:(i + 1) * D], h, w,
                                           c == 0, c == CH - 1)
                    last.then_inc(down1_done, 1)

            for L in range(2):
                turn_xn(L)
                pe.wait_ge(xn_split, 4 * L + 4)
                if L == 0:
                    project_qk(L, 0, 0, None)
                else:
                    project_qk(L, 0, 0, (o_added, 4 * PAIRS - 1))
                router(L)
                pair_steps(L, 0, first=True)
                with pe.Fori(1, PAIRS - 1) as p:
                    pair_steps(L, p)
                pair_steps(L, PAIRS - 1, last=True)
                for b in range(SEQS):
                    attend(L * HEADS + HEADS - 1, L * PAIRS + PAIRS - 1, 1, b, False)
                project_out(L, PAIRS - 1, (o_added, 4 * (L * PAIRS + PAIRS - 1) - 1))
                if L == 0:
                    pe.wait_ge(o_added, 4 * PAIRS)
                    up(0, 0, True)
                    up(1, 1, True)
                    down(0, 0, True)
                    up(2, 0, False)
                    down(1, 1, False)
                    with pe.Fori(1, UNITS // 2 - 1) as i:
                        up(2 * i + 1, 1, False)
                        down(2 * i, 0, False)
                        up(2 * i + 2, 0, False)
                        down(2 * i + 1, 1, False)
                    up(UNITS - 1, 1, False)
                    down(UNITS - 2, 0, False)
                    down(UNITS - 1, 1, False)
                else:
                    pe.wait_ge(o_added, 8 * PAIRS)
                    gate_up(0, 0, True)
                    pe.wait_ge(pad_zero, 1)
                    gate_up(0, 1, False)
                    down1(0, 0, True)
                    gate_up(1, 0, False)
                    down1(0, 1, True)
                    with pe.Fori(1, E1 - 1) as e:
                        gate_up(e, 1, False)
                        down1(e, 0, False)
                        gate_up(e + 1, 0, False)
                        down1(e, 1, False)
                    gate_up(E1 - 1, 1, False)
                    down1(E1 - 1, 0, False)
                    down1(E1 - 1, 1, False)

        @block.scalar
        def _(act):
            def hi_part(dst, src):
                return nc.scalar.activation(dst, src, ACT.Copy)

            def split_router(L):
                W = 32 if L == 0 else E1
                act.wait_ge(router_loaded, 16 * (L + 1))
                if L == 1:
                    act.wait_ge(logits_done, 1)
                hi_part(router_w[:, 0, :, 0:W], router_raw[:, :, 0:W]).then_inc(router_hi, 1)

            def split_qk(L, p, s, old):
                head = 2 * p + (L * HEADS + s)
                act.wait_ge(qk_loaded[s], 16 * p + 16 * (L * PAIRS + 1))
                if old:
                    act.wait_ge(qk_done, 4 * head - 4)
                hi_part(qk_w[:, s, 0, :, :].rearrange("p a b -> p (a b)"), qk_raw[:, s, :]).then_inc(qk_w_hi, 1)

            def split_v(L, p, old):
                pair = p + L * PAIRS
                act.wait_ge(v_loaded, 16 * pair + 16)
                if old:
                    act.wait_ge(v_done, 4 * pair)
                hi_part(v_w[:, 0, :, :].rearrange("p a b -> p (a b)"), v_raw[:, :]).then_inc(v_w_hi, 1)

            def split_o(L, p, old):
                pair = p + L * PAIRS
                act.wait_ge(o_loaded, 16 * pair + 16)
                if old:
                    act.wait_ge(o_done, 4 * pair)
                hi_part(o_w[:, 0, :, :].rearrange("p a b -> p (a b)"), o_raw[:, :]).then_inc(o_w_hi, 1)

            def split_up(u, s, old):
                act.wait_ge(up_loaded[s], 8 * u + (16 - 8 * s))
                if old:
                    act.wait_ge(up_done, 2 * u - 2)
                hi_part(up_w[:, s, 0, :, :].rearrange("p a b -> p (a b)"), up_raw[:, s, :]).then_inc(up_w_hi, 1)

            def split_down(u, s, old):
                act.wait_ge(down_loaded[s], 8 * u + (16 - 8 * s))
                if old:
                    act.wait_ge(down_done, 4 * u - 4)
                hi_part(down_w[:, s, 0, :], down_raw[:, s, :]).then_inc(down_w_hi, 1)

            def split_gu(e, c, old):
                at, n = c * KC * 2 * P, KC * 2 * P if c < FULL else KC * P
                if c == 0:
                    act.wait_ge(gu_loaded, 16 * e + 16)
                if old:
                    act.wait_ge(gu_done, 12 * e + (c - 5))
                hi_part(gu_w[:, 0, at:at + n], gu_raw[:, at:at + n]).then_inc(gu_w_hi, 1)

            def split_down1(e, k, old):
                if k == 0:
                    act.wait_ge(down1_loaded, 16 * e + 16)
                    if old:
                        act.wait_ge(down1_done, 4 * e)
                hi_part(down1_w[:, 0, 2 * k:2 * k + 2, :].rearrange("p a b -> p (a b)"),
                        down1_raw[:, 2 * k * D:(2 * k + 2) * D]).then_inc(down1_w_hi, 1)

            def copy_turned(head, b):
                act.wait_ge(turned, 4 * head + (b + 1))
                nc.scalar.activation(pr_t[:, b, :], psum[:, prt_bank[b % 2], 0:3 * P],
                                     ACT.Copy).then_inc(turned_copied, 1)

            def softcap(head):
                for b in range(SEQS):
                    act.wait_ge(scores_done, 4 * head + (b + 1))
                    nc.scalar.activation(sc[:, b, :], psum[:, score_bank[b % 2], 0:3 * P], ACT.Tanh,
                                         scale=SCALE / CAP).then_inc(scores_read, 1)

            def exponentials(L, head, b):
                if L == 0:
                    act.wait_ge(masked, 4 * head + (b + 1))
                else:
                    act.wait_ge(negmax_ready, 4 * (head - HEADS) + (b + 1))
                for c, (lo, hi) in enumerate(((0, P), (P, 3 * P))):
                    if L == 0:
                        nc.scalar.activation(pr[:, b, lo:hi], sc[:, b, lo:hi], ACT.Exp, scale=CAP,
                                             accum_out=row_sum[:, b, c:c + 1]).then_inc(exp_done, 1)
                    else:
                        nc.scalar.activation(pr[:, b, lo:hi], sc[:, b, lo:hi], ACT.Exp,
                                             bias=neg_max[:, b, c:c + 1],
                                             accum_out=row_sum[:, b, c:c + 1]).then_inc(exp_done, 1)

            def take_z(head, pair, s, old):
                for j in range(2):
                    act.wait_ge(z_done, 2 * head + (j + 1))
                    if old and s == 0 and j == 0:
                        act.wait_ge(o_done, 4 * pair)
                    hi_part(z_p[:, s, 0, j * HALF:(j + 1) * HALF], psum[:, z_bank[j], :]).then_inc(z_hi, 1)

            def copy_v(pair, j):
                act.wait_ge(v_done, 4 * pair + (j + 1))
                nc.scalar.activation(v_sb[:, 2 * j:2 * j + 2, :].rearrange("p a b -> p (a b)"),
                                     psum[:, proj_bank[j % 2], :], ACT.Copy).then_inc(v_copied, 1)

            def copy_qk(head, s, turning=None):
                for j in range(4):
                    if turning is not None:
                        copy_turned(turning, j)
                    act.wait_ge(qk_done, 4 * head + (j + 1))
                    nc.scalar.activation(qk[:, s, j % 2, (j // 2) * HALF:(j // 2 + 1) * HALF],
                                         psum[:, proj_bank[j % 2], :], ACT.Copy).then_inc(qk_copied, 1)

            def pair_steps(L, p, first=False, last=False):
                pair = p + L * PAIRS
                if L == 0:
                    softcap(2 * pair)
                if not last:
                    split_qk(L, p + 1, 0, True)
                if not first:
                    split_o(L, p - 1, not (isinstance(p, int) and p == 1))
                exponentials(L, 2 * pair, 0)
                exponentials(L, 2 * pair, 1)
                copy_v(pair, 0)
                exponentials(L, 2 * pair, 2)
                copy_v(pair, 1)
                copy_v(pair, 2)
                exponentials(L, 2 * pair, 3)
                copy_v(pair, 3)
                if not first:
                    take_z(2 * pair - 1, pair - 1, 1, False)
                copy_qk(2 * pair + 1, 1, turning=2 * pair)
                if L == 0:
                    softcap(2 * pair + 1)
                if not last:
                    split_qk(L, p + 1, 1, True)
                    split_v(L, p + 1, True)
                for b in range(SEQS):
                    exponentials(L, 2 * pair + 1, b)
                take_z(2 * pair, pair, 0, not first)
                if not last:
                    copy_qk(2 * pair + 2, 0, turning=2 * pair + 1)
                else:
                    for b in range(SEQS):
                        copy_turned(2 * pair + 1, b)

            def hidden(u, s):
                for half in range(2):
                    act.wait_ge(up_done, 2 * u + (half + 1))
                    nc.scalar.activation(hid[:, half, :], psum[:, up_bank[2 * s + half], :],
                                         ACT.Relu).then_inc(relu_done, 1)
                for half in range(2):
                    act.wait_ge(relu_done, 2 * u + (half + 1))
                    nc.scalar.activation(hid[:, half, :], hid[:, half, :], ACT.Square).then_inc(square_done, 1)
                for half in range(2):
                    act.wait_ge(square_done, 2 * u + (half + 1))
                    hi_part(h0_p[:, s, 0, half * HALF:(half + 1) * HALF], hid[:, half, :]).then_inc(hid_hi, 1)

            def unit(u, s, up_old, down_old, more=True):
                if more:
                    split_up(u + 1, 1 - s, up_old)
                act.wait_ge(hid_split, 2 * u)
                hidden(u, s)
                split_down(u, s, down_old)

            def expert_half(e, half, split_next, first):
                def take_hi(c):
                    act.wait_ge(mul_done, 12 * e + (6 * half + c + 1))
                    r = P if c < FULL else TAIL
                    hi_part(h1_p[0:r, half, 0, c, :], hid[0:r, c % 2, :]).then_inc(hid1_hi, 1)

                for c in range(CH):
                    act.wait_ge(gu_done, 12 * e + (6 * half + c + 1))
                    if not (first and c < 2):
                        act.wait_ge(mul_done, 12 * e + (6 * half + c - 1))
                    r = P if c < FULL else TAIL
                    nc.scalar.activation(gate_act[0:r, c % 2, :], psum[0:r, up_bank[2 * (c % 2)], :],
                                         ACT.Silu).then_inc(silu_done, 1)
                    if c > 0:
                        take_hi(c - 1)
                    if split_next:
                        split_gu(e + 1, c, True)
                take_hi(CH - 1)

            for L in range(2):
                split_router(L)
                split_qk(L, 0, 0, False)
                split_qk(L, 0, 1, False)
                split_v(L, 0, False)
                act.wait_ge(var_ready, L + 1)
                nc.scalar.activation(std[:, :], var_eps[:, :], ACT.Sqrt).then_inc(std_ready, 1)
                for half in range(2):
                    for kc in range(KC):
                        act.wait_ge(xn_turned, 4 * L + 2 * half + kc + 1)
                        hi_part(xn_t[:, 0, kc, half * HALF:(half + 1) * HALF],
                                psum[:, 2 + 2 * half + kc, :]).then_inc(xn_hi, 1)
                copy_qk(L * HEADS, 0)
                act.wait_ge(logits_copied, L + 1)
                if L == 0:
                    nc.scalar.activation(sig[:, :, :], logits[:, :, :], ACT.Exp, scale=-1.0).then_inc(logits_exp, 1)
                else:
                    nc.scalar.activation(sig[:, :, 0:E1], logits[:, :, 0:E1], ACT.Exp).then_inc(logits_exp, 1)
                pair_steps(L, 0, first=True)
                with act.Fori(1, PAIRS - 1) as p:
                    pair_steps(L, p)
                pair_steps(L, PAIRS - 1, last=True)
                split_o(L, PAIRS - 1, True)
                end = L * HEADS + HEADS - 1
                if L == 0:
                    split_up(0, 0, False)
                    split_up(1, 1, False)
                    take_z(end, PAIRS - 1, 1, False)
                    hidden(0, 0)
                    split_down(0, 0, False)
                    unit(1, 1, True, False)
                    with act.Fori(1, UNITS // 2 - 1) as i:
                        unit(2 * i, 0, True, True)
                        unit(2 * i + 1, 1, True, True)
                    unit(UNITS - 2, 0, True, True)
                    unit(UNITS - 1, 1, True, True, more=False)
                else:
                    take_z(end, 2 * PAIRS - 1, 1, False)
                    for c in range(CH):
                        split_gu(0, c, False)
                    for k in range(3):
                        split_down1(0, k, False)
                    expert_half(0, 0, False, True)
                    with act.Fori(0, E1 - 1) as e:
                        expert_half(e, 1, True, False)
                        expert_half(e + 1, 0, False, False)
                        for k in range(3):
                            split_down1(e + 1, k, True)
                    expert_half(E1 - 1, 1, False, False)

        @block.gpsimd
        def _(pool):
            def mask(head, b):
                pool.wait_ge(scores_read, 4 * head + (b + 1))
                blocks = sc[:, b, :].rearrange("p (c k) -> p c k", c=3)[:, 0:3:2, :]
                nc.gpsimd.tensor_tensor(blocks, blocks, future.unsqueeze(1).to_broadcast([P, 2, P]),
                                        ALU.add).then_inc(masked, 1)

            pool.wait_ge(const_loaded, 16)

            with pool.Fori(0, HEADS) as head:
                for b in range(SEQS):
                    mask(head, b)
            pool.wait_ge(up_done, 2 * UNITS)
            pool.wait_ge(o_done, 8 * PAIRS)
            for half in range(2):
                last = nc.gpsimd.memset(h1_p[TAIL:P, half, :, FULL, :].bitcast(F32), 0.0)
            last.then_inc(pad_zero, 1)

        @block.vector
        def _(dve):
            links = [0]

            def link(ins):
                links[0] += 1
                ins.then_inc(dve_chain, 1)
                dve.wait_ge(dve_chain, links[0])

            def lo_part(dst, src, hi):
                return nc.vector.tensor_tensor(dst, src, hi.bitcast(F32), ALU.subtract)

            def split_router(L):
                W = 32 if L == 0 else E1
                dve.wait_ge(router_hi, L + 1)
                lo_part(router_w[:, 1, :, 0:W], router_raw[:, :, 0:W], router_w[:, 0, :, 0:W]).then_inc(router_split, 1)

            def split_qk(L, p, s):
                head = 2 * p + (L * HEADS + s)
                dve.wait_ge(qk_w_hi, head + 1)
                lo_part(qk_w[:, s, 1, :, :].rearrange("p a b -> p (a b)"), qk_raw[:, s, :],
                        qk_w[:, s, 0, :, :].rearrange("p a b -> p (a b)")).then_inc(qk_w_split, 1)

            def split_v(L, p):
                dve.wait_ge(v_w_hi, p + (L * PAIRS + 1))
                lo_part(v_w[:, 1, :, :].rearrange("p a b -> p (a b)"), v_raw[:, :],
                        v_w[:, 0, :, :].rearrange("p a b -> p (a b)")).then_inc(v_w_split, 1)

            def split_o(L, p):
                dve.wait_ge(o_w_hi, p + (L * PAIRS + 1))
                lo_part(o_w[:, 1, :, :].rearrange("p a b -> p (a b)"), o_raw[:, :],
                        o_w[:, 0, :, :].rearrange("p a b -> p (a b)")).then_inc(o_w_split, 1)

            def split_up(u, s):
                dve.wait_ge(up_w_hi, u + 1)
                lo_part(up_w[:, s, 1, :, :].rearrange("p a b -> p (a b)"), up_raw[:, s, :],
                        up_w[:, s, 0, :, :].rearrange("p a b -> p (a b)")).then_inc(up_w_split, 1)

            def split_down(u, s):
                dve.wait_ge(down_w_hi, u + 1)
                lo_part(down_w[:, s, 1, :], down_raw[:, s, :], down_w[:, s, 0, :]).then_inc(down_w_split, 1)

            def split_gu(e, c):
                at, n = c * KC * 2 * P, KC * 2 * P if c < FULL else KC * P
                dve.wait_ge(gu_w_hi, CH * e + (c + 1))
                lo_part(gu_w[:, 1, at:at + n], gu_raw[:, at:at + n], gu_w[:, 0, at:at + n]).then_inc(gu_w_split, 1)

            def split_down1(e, k):
                dve.wait_ge(down1_w_hi, 3 * e + (k + 1))
                lo_part(down1_w[:, 1, 2 * k:2 * k + 2, :].rearrange("p a b -> p (a b)"),
                        down1_raw[:, 2 * k * D:(2 * k + 2) * D],
                        down1_w[:, 0, 2 * k:2 * k + 2, :].rearrange("p a b -> p (a b)")).then_inc(down1_w_split, 1)

            def layernorm(L):
                for t in range(TILES):
                    if L == 1 and t % 2 == 0:
                        dve.wait_ge(y_added, 4 * (UNITS - 1) + t // 2 + 1)
                    last = nc.vector.bn_stats(stats[:, t, :], x_sb[:, t, :])
                link(last)
                for t in range(TILES):
                    last = nc.vector.bn_aggr(mean_var[:, t, :], stats[:, t, :])
                link(last)
                link(nc.vector.tensor_scalar(var_eps[:, :], mean_var[:, :, 1], EPS, None, ALU.add))
                nc.vector.tensor_scalar(newton[:, :], var_eps[:, :], 1.0, None, ALU.mult).then_inc(var_ready, 1)
                dve.wait_ge(std_ready, L + 1)
                link(nc.vector.reciprocal(rstd[:, :], std[:, :]))
                link(nc.vector.tensor_tensor(newton[:, :], rstd[:, :], rstd[:, :], ALU.mult))
                link(nc.vector.tensor_tensor(newton[:, :], newton[:, :], var_eps[:, :], ALU.mult))
                link(nc.vector.tensor_scalar(newton[:, :], newton[:, :], -0.5, 1.5, ALU.mult, ALU.add))
                link(nc.vector.tensor_tensor(rstd[:, :], rstd[:, :], newton[:, :], ALU.mult))
                for t in range(TILES):
                    nc.vector.tensor_scalar(xn[:, t, :], x_sb[:, t, :], mean_var[:, t, 0:1], rstd[:, t:t + 1],
                                            ALU.subtract, ALU.mult).then_inc(xn_ready, 1)

            def rank_of(values, n, tiles, ahead, tie, tri, out):
                shape = [P, tiles, n, n]
                a = ahead[:, 0:tiles * n * n].rearrange("p (t i j) -> p t i j", t=tiles, i=n)
                b = tie[:, 0:tiles * n * n].rearrange("p (t i j) -> p t i j", t=tiles, i=n)
                other = values.unsqueeze(2).to_broadcast(shape)
                own = values.unsqueeze(3).to_broadcast(shape)
                nc.vector.tensor_tensor(a, other, own, ALU.is_gt)
                link(nc.vector.tensor_tensor(b, other, own, ALU.is_equal))
                link(nc.vector.tensor_tensor(b, b, tri.unsqueeze(1).to_broadcast(shape), ALU.mult))
                link(nc.vector.tensor_tensor(a, a, b, ALU.add))
                link(nc.vector.tensor_reduce(out, a, X_AXIS, ALU.add))

            def router_scores(L):
                W = 32 if L == 0 else E1
                dve.wait_ge(logits_done, L + 1)
                link(nc.vector.tensor_copy(logits[:, :, 0:W],
                                           psum[:, 6, 0:TILES * W].rearrange("p (t w) -> p t w", t=TILES)))
                if L == 0:
                    nc.vector.memset(coef[:, :, E0:UNITS], 1.0).then_inc(logits_copied, 1)
                    dve.wait_ge(logits_exp, 1)
                    link(nc.vector.tensor_scalar(sig[:, :, :], sig[:, :, :], 1.0, None, ALU.add))
                    link(nc.vector.reciprocal(sig[:, :, :], sig[:, :, :]))
                else:
                    link(nc.vector.tensor_reduce(per_tile[:, 0, :], logits[:, :, 0:E1], X_AXIS, ALU.max))
                    nc.vector.tensor_tensor(logits[:, :, 0:E1], logits[:, :, 0:E1],
                                            per_tile[:, 0, :].unsqueeze(2).to_broadcast([P, TILES, E1]),
                                            ALU.subtract).then_inc(logits_copied, 1)
                    dve.wait_ge(logits_exp, 2)
                    link(nc.vector.tensor_reduce(per_tile[:, 0, :], sig[:, :, 0:E1], X_AXIS, ALU.add))
                    link(nc.vector.reciprocal(per_tile[:, 1, :], per_tile[:, 0, :]))
                    link(nc.vector.tensor_tensor(sig[:, :, 0:E1], sig[:, :, 0:E1],
                                                 per_tile[:, 1, :].unsqueeze(2).to_broadcast([P, TILES, E1]), ALU.mult))

            def choose0():
                prob = sig[:, :, 0:E0]
                link(nc.vector.tensor_tensor(choice[:, :, :], prob,
                                             e_bias.unsqueeze(1).to_broadcast([P, TILES, E0]), ALU.add))
                four = choice[:, :, :].rearrange("p t (g e) -> p (t g) e", e=4)
                a, b, c, d = (four[:, :, i] for i in range(4))
                s = [small[:, i, :] for i in range(8)]
                nc.vector.tensor_tensor(s[0], a, b, ALU.max)
                nc.vector.tensor_tensor(s[1], a, b, ALU.min)
                nc.vector.tensor_tensor(s[2], c, d, ALU.max)
                link(nc.vector.tensor_tensor(s[3], c, d, ALU.min))
                nc.vector.tensor_tensor(s[4], s[0], s[2], ALU.max)
                nc.vector.tensor_tensor(s[5], s[0], s[2], ALU.min)
                link(nc.vector.tensor_tensor(s[6], s[1], s[3], ALU.max))
                link(nc.vector.tensor_tensor(s[7], s[5], s[6], ALU.max))
                link(nc.vector.tensor_tensor(groups[:, :, :], s[4].rearrange("p (t g) -> p t g", g=4),
                                             s[7].rearrange("p (t g) -> p t g", g=4), ALU.add))
                rank_of(groups[:, :, :], 4, TILES, beats, ties, tri4, rank[:, :, 0:4])
                link(nc.vector.tensor_scalar(groups[:, :, :], rank[:, :, 0:4], 2.0, None, ALU.is_lt))
                by_group = choice[:, :, :].rearrange("p t (g e) -> p t g e", e=4)
                link(nc.vector.tensor_tensor(by_group, by_group,
                                             groups[:, :, :].unsqueeze(3).to_broadcast([P, TILES, 4, 4]), ALU.mult))
                for t in range(0, TILES, 4):
                    rank_of(choice[:, t:t + 4, :], E0, 4, beats, ties, tri16, rank[:, t:t + 4, :])
                link(nc.vector.tensor_scalar(rank[:, :, :], rank[:, :, :], 2.0, None, ALU.is_lt))
                link(nc.vector.tensor_tensor(rank[:, :, :], rank[:, :, :], prob, ALU.mult))
                link(nc.vector.tensor_reduce(per_tile[:, 0, :], rank[:, :, :], X_AXIS, ALU.add))
                link(nc.vector.tensor_scalar(per_tile[:, 0, :], per_tile[:, 0, :], 1e-20, None, ALU.add))
                link(nc.vector.reciprocal(per_tile[:, 1, :], per_tile[:, 0, :]))
                link(nc.vector.tensor_tensor(coef[:, :, 0:E0], rank[:, :, :],
                                             per_tile[:, 1, :].unsqueeze(2).to_broadcast([P, TILES, E0]), ALU.mult))

            def choose1():
                rank_of(sig[:, :, 0:E1], E1, TILES, beats1, ties1, tri8, rank[:, :, 0:E1])
                link(nc.vector.tensor_scalar(rank[:, :, 0:E1], rank[:, :, 0:E1], 2.0, None, ALU.is_lt))
                link(nc.vector.tensor_tensor(coef[:, :, 0:E1], rank[:, :, 0:E1], sig[:, :, 0:E1], ALU.mult))

            def clip_scores(head):
                for b in range(SEQS):
                    dve.wait_ge(scores_done, 4 * head + (b + 1))
                    nc.vector.tensor_scalar(sc[:, b, :], psum[:, score_bank[b % 2], 0:3 * P], -CLIP / SCALE,
                                            CLIP / SCALE, ALU.max, ALU.min).then_inc(scores_read, 1)

            def bias_and_max(head, b, s):
                own = head - HEADS
                for c, (lo, hi) in enumerate(((0, P), (P, 3 * P))):
                    nc.vector.tensor_tensor_reduce(out=sc[:, b, lo:hi], in0=sc[:, b, lo:hi], in1=alibi[:, s, lo:hi],
                                                   scale=SCALE, scalar=NEG, op0=ALU.add, op1=ALU.max,
                                                   accum_out=row_max[:, b, c:c + 1]).then_inc(max_ready, 1)
                dve.wait_ge(max_ready, 8 * own + (2 * b + 2))
                nc.vector.tensor_scalar(neg_max[:, b, :], row_max[:, b, :], -1.0, None,
                                        ALU.mult).then_inc(negmax_ready, 1)

            def normalise(L, head, b, gate_at):
                dve.wait_ge(exp_done, 8 * head + (2 * b + 2))
                nc.vector.reciprocal(row_scale[:, b, :], row_sum[:, b, :]).then_inc(recip_done, 1)
                dve.wait_ge(recip_done, 4 * head + (b + 1))
                if L == 0:
                    nc.vector.tensor_tensor(row_scale[:, b, :], row_scale[:, b, :], gate_at(b),
                                            ALU.mult).then_inc(row_scaled, 1)
                    dve.wait_ge(row_scaled, 4 * head + (b + 1))
                nc.vector.tensor_scalar(pr[:, b, 0:P], pr[:, b, 0:P], row_scale[:, b, 0:1], None, ALU.mult)
                nc.vector.tensor_scalar(pr[:, b, P:3 * P], pr[:, b, P:3 * P], row_scale[:, b, 1:2], None,
                                        ALU.mult).then_inc(probs_ready, 1)

            def softmax(L, p, s, adding=None):
                head = 2 * p + (L * HEADS + s)

                def gate_at(b):
                    return sig[:, 2 * b:2 * b + 2, bass.ds(2 * p + (E0 + s), 1)].rearrange("p a b -> p (a b)")

                def add(j):
                    if adding is not None:
                        add_out(adding, j)

                if L == 1:
                    bias_and_max(head, 0, s)
                    bias_and_max(head, 1, s)
                normalise(L, head, 0, gate_at)
                if L == 1:
                    bias_and_max(head, 2, s)
                    add(0)
                normalise(L, head, 1, gate_at)
                if L == 1:
                    bias_and_max(head, 3, s)
                else:
                    add(0)
                add(1)
                normalise(L, head, 2, gate_at)
                add(2)
                normalise(L, head, 3, gate_at)
                add(3)

            def take_z(head, s):
                for j in range(2):
                    dve.wait_ge(z_hi, 2 * head + (j + 1))
                    cols = slice(j * HALF, (j + 1) * HALF)
                    lo_part(z_p[:, s, 1, cols], psum[:, z_bank[j], :], z_p[:, s, 0, cols]).then_inc(z_split, 1)

            def add_out(pair, j):
                dve.wait_ge(o_done, 4 * pair + (j + 1))
                x2 = x_sb[:, 2 * j:2 * j + 2, :].rearrange("p a b -> p (a b)")
                nc.vector.tensor_tensor(x2, psum[:, proj_bank[j % 2], :], x2, ALU.add).then_inc(o_added, 1)

            def pair_steps(L, p, first=False, last=False):
                pair = p + L * PAIRS
                if L == 1:
                    clip_scores(2 * pair)
                    dve.wait_ge(alibi_loaded[0], 16 * p + 16)
                    dve.wait_ge(scores_read, 8 * pair + 4)
                if not last:
                    split_qk(L, p + 1, 0)
                softmax(L, p, 0)
                if not first:
                    split_o(L, p - 1)
                    take_z(2 * pair - 1, 1)
                if L == 1:
                    clip_scores(2 * pair + 1)
                    dve.wait_ge(alibi_loaded[1], 16 * p + 16)
                    dve.wait_ge(scores_read, 8 * pair + 8)
                if not last:
                    split_qk(L, p + 1, 1)
                softmax(L, p, 1, adding=None if first else pair - 1)
                if not last:
                    split_v(L, p + 1)
                take_z(2 * pair, 0)

            def hidden_lo(u, s):
                for half in range(2):
                    dve.wait_ge(hid_hi, 2 * u + (half + 1))
                    cols = slice(half * HALF, (half + 1) * HALF)
                    lo_part(h0_p[:, s, 1, cols], hid[:, half, :], h0_p[:, s, 0, cols]).then_inc(hid_split, 1)

            def add_unit(u):
                for j in range(4):
                    dve.wait_ge(down_done, 4 * u + (j + 1))
                    if not (isinstance(u, int) and u == 0):
                        dve.wait_ge(y_added, 4 * u + (j - 3))
                    for i in range(2):
                        t = 2 * j + i
                        last = nc.vector.scalar_tensor_tensor(
                            out=x_sb[:, t, :], in0=psum[:, down_bank[j], i * D:(i + 1) * D],
                            scalar=coef[:, t, bass.ds(u, 1)], in1=x_sb[:, t, :], op0=ALU.mult, op1=ALU.add)
                    last.then_inc(y_added, 1)

            def unit(u, s, more=True):
                if more:
                    split_up(u + 1, 1 - s)
                hidden_lo(u, s)
                split_down(u, s)
                add_unit(u - 1)

            def expert_half(e, half, split_next, first=False):
                def take_lo(c):
                    dve.wait_ge(hid1_hi, 12 * e + (6 * half + c + 1))
                    r = P if c < FULL else TAIL
                    lo_part(h1_p[0:r, half, 1, c, :], hid[0:r, c % 2, :], h1_p[0:r, half, 0, c, :]).then_inc(hid1_split, 1)

                for c in range(CH):
                    dve.wait_ge(silu_done, 12 * e + (6 * half + c + 1))
                    if not (first and c < 2):
                        dve.wait_ge(hid1_split, 12 * e + (6 * half + c - 1))
                    b = up_bank[2 * (c % 2)]
                    if c < FULL:
                        r, up_part = P, psum[:, b + 1, :]
                    else:
                        r, up_part = TAIL, psum[TAIL:2 * TAIL, b, :]
                    nc.vector.tensor_tensor(hid[0:r, c % 2, :], gate_act[0:r, c % 2, :], up_part,
                                            ALU.mult).then_inc(mul_done, 1)
                    if c > 0:
                        take_lo(c - 1)
                    if split_next:
                        split_gu(e + 1, c)
                take_lo(CH - 1)

            def add_expert(e, half):
                for j in range(2):
                    dve.wait_ge(down1_done, 4 * e + (2 * half + j + 1))
                    for i in range(2):
                        t = 4 * half + 2 * j + i
                        last = nc.vector.scalar_tensor_tensor(
                            out=x_sb[:, t, :], in0=psum[:, down_bank[2 * half + j], i * D:(i + 1) * D],
                            scalar=coef[:, t, bass.ds(e, 1)], in1=x_sb[:, t, :], op0=ALU.mult, op1=ALU.add)
                    last.then_inc(y1_added, 1)

            dve.wait_ge(x_loaded, 16)
            for L in range(2):
                if L == 0:
                    split_router(L)
                    split_qk(L, 0, 0)
                    split_qk(L, 0, 1)
                    split_v(L, 0)
                layernorm(L)
                if L == 1:
                    split_router(L)
                    split_qk(L, 0, 0)
                    split_qk(L, 0, 1)
                    split_v(L, 0)
                for half in range(2):
                    for kc in range(KC):
                        dve.wait_ge(xn_hi, 4 * L + 2 * half + kc + 1)
                        cols = slice(half * HALF, (half + 1) * HALF)
                        lo_part(xn_t[:, 1, kc, cols], psum[:, 2 + 2 * half + kc, :],
                                xn_t[:, 0, kc, cols]).then_inc(xn_split, 1)
                router_scores(L)
                pair_steps(L, 0, first=True)
                with dve.Fori(1, PAIRS - 1) as p:
                    pair_steps(L, p)
                pair_steps(L, PAIRS - 1, last=True)
                split_o(L, PAIRS - 1)
                end = L * HEADS + HEADS - 1
                if L == 0:
                    split_up(0, 0)
                    split_up(1, 1)
                    take_z(end, 1)
                    choose0()
                    for j in range(4):
                        add_out(PAIRS - 1, j)
                    hidden_lo(0, 0)
                    split_down(0, 0)
                    unit(1, 1)
                    with dve.Fori(1, UNITS // 2 - 1) as i:
                        unit(2 * i, 0)
                        unit(2 * i + 1, 1)
                    unit(UNITS - 2, 0)
                    unit(UNITS - 1, 1, more=False)
                    add_unit(UNITS - 1)
                else:
                    take_z(end, 1)
                    for c in range(CH):
                        split_gu(0, c)
                    choose1()
                    for j in range(4):
                        add_out(2 * PAIRS - 1, j)
                    for k in range(3):
                        split_down1(0, k)
                    expert_half(0, 0, False, first=True)
                    with dve.Fori(0, E1 - 1) as e:
                        expert_half(e, 1, True)
                        add_expert(e, 0)
                        expert_half(e + 1, 0, False)
                        add_expert(e, 1)
                        for k in range(3):
                            split_down1(e + 1, k)
                    expert_half(E1 - 1, 1, False)
                    add_expert(E1 - 1, 0)
                    add_expert(E1 - 1, 1)


def kernel(L0_attn_x, L0_attn_w_qkv, L0_attn_w_gates, L0_attn_w_out, L0_ffn_router_weight, L0_ffn_e_bias,
           L0_ffn_w_up, L0_ffn_w_down, L0_ffn_shared_up, L0_ffn_shared_down, L1_attn_Wq, L1_attn_Wk, L1_attn_Wv,
           L1_attn_Wo, L1_ffn_router_w, L1_ffn_gate_w, L1_ffn_up_w, L1_ffn_down_w):
    import numpy as np
    import concourse.bacc as bacc
    from concourse.bass_utils import run_bass_kernel_spmd

    def a(v):
        return np.asarray(v)

    def chunks(w):
        return w.reshape(KC, P, -1).transpose(1, 0, 2)

    def attention_weights(wq, wk, wv, wo):
        q, k = (chunks(w).reshape(P, KC, HEADS, P).transpose(2, 0, 1, 3) for w in (wq, wk))
        qk = np.concatenate([q, k], axis=3).reshape(HEADS, P, KC * 2 * P)
        v = chunks(wv).reshape(P, KC, PAIRS, 2 * P).transpose(2, 0, 1, 3).reshape(PAIRS, P, KC * 2 * P)
        o = wo.reshape(PAIRS, 2, P, D).transpose(0, 2, 1, 3).reshape(PAIRS, P, 2 * D)
        return qk, v, o

    HD = HEADS * P
    qkv = a(L0_attn_w_qkv)
    layer0 = attention_weights(qkv[:, 0:HD], qkv[:, HD:2 * HD], qkv[:, 2 * HD:3 * HD], a(L0_attn_w_out))
    layer1 = attention_weights(a(L1_attn_Wq).T, a(L1_attn_Wk).T, a(L1_attn_Wv).T, a(L1_attn_Wo).T)
    router0 = chunks(np.concatenate([a(L0_ffn_router_weight).T, a(L0_attn_w_gates)], axis=1))
    router1 = chunks(a(L1_ffn_router_w).T)
    ups = np.concatenate([a(L0_ffn_w_up), a(L0_ffn_shared_up).reshape(D, SHARED, P).transpose(1, 0, 2)])
    ups = ups.reshape(UNITS, KC, P, P).transpose(0, 2, 1, 3).reshape(UNITS, P, KC * P)
    downs = np.concatenate([a(L0_ffn_w_down), a(L0_ffn_shared_down).reshape(SHARED, P, D)])
    wide = FULL * P

    def inner(w):
        w = w.transpose(0, 2, 1).reshape(E1, KC, P, -1).transpose(0, 2, 1, 3)
        return w[..., 0:wide].reshape(E1, P, KC, FULL, P).transpose(0, 1, 3, 2, 4), w[..., wide:]

    (g, g_tail), (u, u_tail) = inner(a(L1_ffn_gate_w)), inner(a(L1_ffn_up_w))
    gu = np.concatenate([np.concatenate([g, u], axis=4).reshape(E1, P, -1),
                         np.concatenate([g_tail, u_tail], axis=3).reshape(E1, P, -1)], axis=2)
    d1 = np.zeros((E1, CH * P, D), np.float32)
    d1[:, 0:wide + TAIL, :] = a(L1_ffn_down_w).transpose(0, 2, 1)
    d1 = d1.reshape(E1, CH, P, D).transpose(0, 2, 1, 3).reshape(E1, P, CH * D)

    def before(n):
        return np.broadcast_to(np.tril(np.ones((n, n), np.float32), -1).reshape(1, n * n), (P, n * n))

    const = np.concatenate([np.eye(P, dtype=np.float32), np.broadcast_to(a(L0_ffn_e_bias)[None, :], (P, E0)),
                            before(16), before(4), before(8),
                            np.where(np.arange(P)[None, :] > np.arange(P)[:, None], NEG, 0.0).astype(np.float32)],
                           axis=1)
    start = 2.0 ** (-8.0 / HEADS)
    slopes = np.array([start * start ** i for i in range(HEADS)], np.float32).astype(np.float64)
    query, key = np.arange(P)[:, None], np.arange(2 * P)[None, :]
    line = slopes[:, None, None] * key[None] * (P ** 0.5)
    alibi = np.concatenate([np.where(key[None, :, 0:P] > query[None], NEG, line[:, :, 0:P]),
                            np.where(key[None] > query[None] + P, NEG, line)], axis=2).astype(np.float32)

    arrays, args = {}, []
    nc = bacc.Bacc("TRN2", target_bir_lowering=False, num_devices=1)

    def give(name, array):
        arrays[name] = np.ascontiguousarray(array)
        return nc.dram_tensor(name, arrays[name].shape, F32, kind="ExternalInput").ap()

    x_d = give("x", a(L0_attn_x).reshape(TILES, P, D).transpose(1, 0, 2))
    const_d = give("const_in", const)
    alibi_d = give("alibi_in", alibi)
    qk_d, v_d, o_d = ([give(f"{n}{i}", w[k]) for i, w in enumerate((layer0, layer1))]
                      for k, n in enumerate(("w_qk", "w_v", "w_o")))
    router_d = [give("router0", router0), give("router1", router1)]
    up_d, down_d = give("w_up0", ups), give("w_down0", downs)
    gu_d, down1_d = give("w_gate_up1", gu), give("w_down1", d1)
    out_d = nc.dram_tensor("out", (P, TILES, D), F32, kind="ExternalOutput").ap()
    bass_two_layers(nc, x_d, const_d, alibi_d, qk_d, v_d, o_d, router_d, up_d, down_d, gu_d, down1_d, out_d)
    r = run_bass_kernel_spmd(nc, [arrays], core_ids=[0])
    return r.results[0]["out"].transpose(1, 0, 2).reshape(SEQS, 2 * P, D)
```

```python
from contextlib import ExitStack

import concourse.bass as bass
from concourse import mybir

F32 = mybir.dt.float32
F32R = mybir.dt.float32r
ALU = mybir.AluOpType
ACT = mybir.ActivationFunctionType
X_AXIS = mybir.AxisListType.X

P = 128
D = 256
KC = D // P
SEQS = 4
TILES = 8
TOK = TILES * P
HALF = TOK // 2
HEADS = 16
PAIRS = HEADS // 2
E0, SHARED, E1 = 16, 4, 8
UNITS = E0 + SHARED
FULL, TAIL = 5, 64
CH = FULL + 1
GU = FULL * KC * 2 * P + KC * P
CAP = 50.0
SCALE = float(P) ** -0.5
CLIP = 1024.0
NEG = -1e30
EPS = 1e-5


def bass_two_layers(nc, x_d, const_d, alibi_d, qk_d, v_d, o_d, router_d, up_d, down_d, gu_d, down1_d, out_d):
    with ExitStack() as ctx:
        def sb(name, shape, dt=F32):
            return ctx.enter_context(nc.sbuf_tensor(name, shape, dt))

        def sem(name):
            return ctx.enter_context(nc.semaphore(name))

        H1 = 2 * 2 * CH * HALF
        parts = sb("parts", [P, H1 + 2 * GU + 2 * CH * D], F32R)

        def region(at, *dims):
            n = 1
            for d in dims:
                n *= d
            names = " ".join(f"a{i}" for i in range(len(dims)))
            sizes = {f"a{i}": d for i, d in enumerate(dims)}
            return parts[:, at:at + n].rearrange(f"p ({names}) -> p {names}", **sizes)

        qk_w = region(0, 2, 2, KC, 2 * P)
        v_w = region(2048, 2, KC, 2 * P)
        h0_p = region(3072, 2, 2, TOK)
        z_p = region(7168, 2, 2, TOK)
        o_w = region(11264, 2, 2, D)
        h1_p = region(0, 2, 2, CH, HALF)
        gu_w = region(H1, 2, GU)
        down1_w = region(H1 + 2 * GU, 2, CH, D)
        up_w = region(H1, 2, 2, KC, P)
        down_w = region(H1 + 1024, 2, 2, D)
        xn_t = sb("xn_t", [P, 2, KC, TOK], F32R)
        router_w = sb("router_w", [P, 2, KC, 32], F32R)

        x_sb = sb("x_sb", [P, TILES, D])
        qk = sb("qk", [P, 2, 2, TOK])
        xn = qk[:, 1, :, :].rearrange("p b t -> p (b t)").rearrange("p (t d) -> p t d", t=TILES)
        v_sb = sb("v_sb", [P, TILES, 2 * P])
        sc = sb("sc", [P, SEQS, 3 * P])
        pr = sb("pr", [P, SEQS, 3 * P])
        pr_t = sb("pr_t", [P, SEQS, 3 * P])
        qk_raw = sb("qk_raw", [P, 2, KC * 2 * P])
        v_raw = sb("v_raw", [P, KC * 2 * P])
        o_raw = sb("o_raw", [P, 2 * D])
        alibi = sb("alibi", [P, 2, 3 * P])
        up_raw = sb("up_raw", [P, 2, KC * P])
        down_raw = sb("down_raw", [P, 2, D])
        gu_raw = sb("gu_raw", [P, GU])
        down1_raw = sb("down1_raw", [P, CH * D])
        router_raw = sb("router_raw", [P, KC, 32])
        const = sb("const", [P, 608])
        ident = const[:, 0:128]
        future = const[:, 480:608]
        e_bias = const[:, 128:144]
        tri16 = const[:, 144:400].rearrange("p (a b) -> p a b", a=16)
        tri4 = const[:, 400:416].rearrange("p (a b) -> p a b", a=4)
        tri8 = const[:, 416:480].rearrange("p (a b) -> p a b", a=8)
        gate_act = sc[:, :, :].rearrange("p b c -> p (b c)")[:, 0:2 * HALF].rearrange("p (s t) -> p s t", s=2)
        hid = pr[:, :, :].rearrange("p b c -> p (b c)")[:, 0:2 * HALF].rearrange("p (s t) -> p s t", s=2)
        row_sum = sb("row_sum", [P, SEQS, 2])
        row_max = sb("row_max", [P, SEQS, 2])
        neg_max = sb("neg_max", [P, SEQS, 2])
        row_scale = sb("row_scale", [P, SEQS, 2])
        stats = sb("stats", [P, TILES, 6])
        mean_var = sb("mean_var", [P, TILES, 2])
        var_eps = sb("var_eps", [P, TILES])
        std = sb("std", [P, TILES])
        rstd = sb("rstd", [P, TILES])
        newton = sb("newton", [P, TILES])
        logits = sb("logits", [P, TILES, 32])
        sig = sb("sig", [P, TILES, 32])
        coef = sb("coef", [P, TILES, UNITS])
        small = sb("small", [P, 8, 32])
        groups = sb("groups", [P, TILES, 4])
        choice = sb("choice", [P, TILES, 16])
        rank = sb("rank", [P, TILES, 16])
        per_tile = sb("per_tile", [P, 2, TILES])
        beats = gu_raw[:, 0:1024]
        ties = gu_raw[:, 1024:2048]
        beats1 = up_raw[:, :, :].rearrange("p a b -> p (a b)")
        ties1 = down_raw[:, :, :].rearrange("p a b -> p (a b)")

        psum = ctx.enter_context(nc.psum_tensor("psum", [P, 8, 512], F32))
        proj_bank, score_bank, prt_bank, z_bank = (0, 1), (2, 3), (4, 5), (6, 7)
        up_bank, down_bank = (0, 1, 2, 3), (4, 5, 6, 7)

        x_loaded, const_loaded = [sem(f"x_loaded{i}") for i in range(2)], sem("const_loaded")
        router_loaded = sem("router_loaded")
        qk_loaded = [sem(f"qk_loaded{s}") for s in range(2)]
        alibi_loaded = [sem(f"alibi_loaded{s}") for s in range(2)]
        v_loaded, o_loaded = sem("v_loaded"), sem("o_loaded")
        up_loaded = [sem(f"up_loaded{s}") for s in range(2)]
        down_loaded = [sem(f"down_loaded{s}") for s in range(2)]
        gu_loaded, down1_loaded = sem("gu_loaded"), sem("down1_loaded")
        qk_w_hi, qk_w_split = sem("qk_w_hi"), sem("qk_w_split")
        v_w_hi, v_w_split = sem("v_w_hi"), sem("v_w_split")
        o_w_hi, o_w_split = sem("o_w_hi"), sem("o_w_split")
        up_w_hi, up_w_split = sem("up_w_hi"), sem("up_w_split")
        down_w_hi, down_w_split = sem("down_w_hi"), sem("down_w_split")
        gu_w_hi, gu_w_split = sem("gu_w_hi"), sem("gu_w_split")
        down1_w_hi, down1_w_split = sem("down1_w_hi"), sem("down1_w_split")
        router_hi, router_split = sem("router_hi"), sem("router_split")
        dve_chain = sem("dve_chain")
        var_ready, std_ready = sem("var_ready"), sem("std_ready")
        xn_ready, xn_turned, xn_hi, xn_split = sem("xn_ready"), sem("xn_turned"), sem("xn_hi"), sem("xn_split")
        logits_done, logits_copied, logits_exp = sem("logits_done"), sem("logits_copied"), sem("logits_exp")
        qk_done, qk_copied = sem("qk_done"), sem("qk_copied")
        v_done, v_copied = sem("v_done"), sem("v_copied")
        o_done, o_added = sem("o_done"), sem("o_added")
        scores_done, scores_read = sem("scores_done"), sem("scores_read")
        masked, max_ready, negmax_ready = sem("masked"), sem("max_ready"), sem("negmax_ready")
        exp_done, recip_done, row_scaled, probs_ready = (sem("exp_done"), sem("recip_done"), sem("row_scaled"),
                                                         sem("probs_ready"))
        turned, turned_copied = sem("turned"), sem("turned_copied")
        z_done, z_hi, z_split = sem("z_done"), sem("z_hi"), sem("z_split")
        up_done, relu_done, square_done, hid_hi, hid_split = (sem("up_done"), sem("relu_done"), sem("square_done"),
                                                              sem("hid_hi"), sem("hid_split"))
        down_done, y_added = sem("down_done"), sem("y_added")
        gu_done, silu_done, mul_done, hid1_hi, hid1_split = (sem("gu_done"), sem("silu_done"), sem("mul_done"),
                                                             sem("hid1_hi"), sem("hid1_split"))
        down1_done, y1_added = sem("down1_done"), sem("y1_added")
        pad_zero = sem("pad_zero")
        stored = sem("stored")

        last_jobs = [(u, 2 * half + i) for half in range(2) for u in (UNITS - 2, UNITS - 1) for i in range(2)]

        block = ctx.enter_context(nc.Block())

        @block.sync
        def _(sp):
            for half in range(2):
                sp.dma_start(x_sb[:, 4 * half:4 * half + 4, :],
                             x_d[:, 4 * half:4 * half + 4, :]).then_inc(x_loaded[half], 16)
            sp.dma_start(const[:, :], const_d).then_inc(const_loaded, 16)
            for L in range(2):
                W = 32 if L == 0 else E1

                def load_qk(h, s):
                    sp.dma_start(qk_raw[:, s, :], qk_d[L][h]).then_inc(qk_loaded[s], 16)

                def load_v(p):
                    sp.dma_start(v_raw[:, :], v_d[L][p]).then_inc(v_loaded, 16)

                def load_o(p):
                    sp.dma_start(o_raw[:, :], o_d[L][p]).then_inc(o_loaded, 16)

                def load_alibi(h, s):
                    sp.dma_start(alibi[:, s, :], alibi_d[h]).then_inc(alibi_loaded[s], 16)

                if L == 1:
                    sp.wait_ge(qk_w_split, HEADS)
                    sp.wait_ge(v_w_split, PAIRS)
                load_qk(0, 0)
                sp.dma_start(router_raw[:, :, 0:W], router_d[L]).then_inc(router_loaded, 16)
                load_v(0)
                load_qk(1, 1)
                if L == 1:
                    sp.wait_ge(o_w_split, PAIRS)
                    load_alibi(0, 0)
                    load_alibi(1, 1)
                load_o(0)
                if L == 0:
                    for u in range(2):
                        sp.dma_start(up_raw[:, u, :], up_d[u]).then_inc(up_loaded[u], 16)
                        sp.dma_start(down_raw[:, u, :], down_d[u]).then_inc(down_loaded[u], 16)
                else:
                    sp.dma_start(gu_raw[:, :], gu_d[0]).then_inc(gu_loaded, 16)
                    sp.dma_start(down1_raw[:, :], down1_d[0]).then_inc(down1_loaded, 16)

                def next_pair(p, first=False):
                    sp.wait_ge(qk_w_split, 2 * p + (L * HEADS + 1))
                    load_qk(2 * p + 2, 0)
                    sp.wait_ge(v_w_split, p + (L * PAIRS + 1))
                    load_v(p + 1)
                    sp.wait_ge(qk_w_split, 2 * p + (L * HEADS + 2))
                    load_qk(2 * p + 3, 1)
                    if not first:
                        sp.wait_ge(o_w_split, p + L * PAIRS)
                        load_o(p)
                    if L == 1:
                        sp.wait_ge(max_ready, 16 * p + 8)
                        load_alibi(2 * p + 2, 0)
                        sp.wait_ge(max_ready, 16 * p + 16)
                        load_alibi(2 * p + 3, 1)

                next_pair(0, first=True)
                with sp.Fori(1, PAIRS - 1) as p:
                    next_pair(p)
                sp.wait_ge(o_w_split, L * PAIRS + PAIRS - 1)
                load_o(PAIRS - 1)
                if L == 0:
                    with sp.Fori(0, UNITS // 2 - 1) as i:
                        for s in range(2):
                            sp.wait_ge(up_w_split, 2 * i + (s + 1))
                            sp.dma_start(up_raw[:, s, :], up_d[2 * i + (2 + s)]).then_inc(up_loaded[s], 16)
                            sp.wait_ge(down_w_split, 2 * i + (s + 1))
                            sp.dma_start(down_raw[:, s, :], down_d[2 * i + (2 + s)]).then_inc(down_loaded[s], 16)
                else:
                    with sp.Fori(0, E1 - 1) as e:
                        sp.wait_ge(gu_w_split, CH * e + CH)
                        sp.dma_start(gu_raw[:, :], gu_d[e + 1]).then_inc(gu_loaded, 16)
                        sp.wait_ge(down1_w_split, 3 * e + 3)
                        sp.dma_start(down1_raw[:, :], down1_d[e + 1]).then_inc(down1_loaded, 16)
            for j in range(4):
                sp.wait_ge(y1_added, 4 * (E1 - 1) + j + 1)
                sp.dma_start(out_d[:, 2 * j:2 * j + 2, :], x_sb[:, 2 * j:2 * j + 2, :]).then_inc(stored, 16)
            sp.wait_ge(stored, 64)

        @block.tensor
        def _(pe):
            def product(out, w, x, first, last):
                nc.tensor.matmul(out, w[1], x[0], start=first, stop=False)
                nc.tensor.matmul(out, w[0], x[1], start=False, stop=False)
                return nc.tensor.matmul(out, w[0], x[0], start=False, stop=last)

            def xn_half(kc, half):
                return tuple(xn_t[:, i, kc, half * HALF:(half + 1) * HALF] for i in range(2))

            def xn_tile(kc, t):
                return tuple(xn_t[:, i, kc, t * P:(t + 1) * P] for i in range(2))

            def turn_xn(L, half):
                if L == 0 and half == 0:
                    pe.wait_ge(const_loaded, 16)
                pe.wait_ge(xn_ready, TILES * L + 4 * half + 4)
                for kc in range(KC):
                    for t in range(4):
                        last = nc.tensor.transpose(psum[:, 2 + 2 * half + kc, t * P:(t + 1) * P],
                                                   xn[:, 4 * half + t, kc * P:(kc + 1) * P], ident)
                    last.then_inc(xn_turned, 1)

            def router(L, half):
                W = 32 if L == 0 else E1
                if half == 0:
                    pe.wait_ge(router_split, L + 1)
                for t in range(4 * half, 4 * half + 4):
                    for kc in range(KC):
                        last = product(psum[:, 6, t * W:(t + 1) * W], xn_tile(kc, t),
                                       (router_w[:, 0, kc, 0:W], router_w[:, 1, kc, 0:W]), kc == 0, kc == KC - 1)
                if half == 1:
                    last.then_inc(logits_done, 1)

            def project_qk(L, p, s, before, turning=None, jobs=range(4)):
                head = 2 * p + (L * HEADS + s)
                for j in jobs:
                    half, c = j // 2, j % 2
                    if turning is not None:
                        turn_probs(*turning, j)
                    if j == 0:
                        pe.wait_ge(qk_w_split, head + 1)
                    if j < 2 and before is not None:
                        pe.wait_ge(before[0], before[1] + j)
                    if j >= 2:
                        pe.wait_ge(qk_copied, 4 * head + (j - 1))
                    for kc in range(KC):
                        w = tuple(qk_w[:, s, i, kc, c * P:(c + 1) * P] for i in range(2))
                        last = product(psum[:, proj_bank[j % 2], :], w, xn_half(kc, half), kc == 0, kc == KC - 1)
                    last.then_inc(qk_done, 1)

            def project_v(L, p):
                pair = p + L * PAIRS
                pe.wait_ge(v_w_split, pair + 1)
                for j in range(4):
                    if j < 2:
                        pe.wait_ge(qk_copied, 8 * pair + (j + 3))
                    else:
                        pe.wait_ge(v_copied, 4 * pair + (j - 1))
                    for i in range(2):
                        t = 2 * j + i
                        for kc in range(KC):
                            w = tuple(v_w[:, k, kc, :] for k in range(2))
                            last = product(psum[:, proj_bank[j % 2], i * D:(i + 1) * D], xn_tile(kc, t), w,
                                           kc == 0, kc == KC - 1)
                    last.then_inc(v_done, 1)

            def project_out(L, p, before):
                pair = p + L * PAIRS
                pe.wait_ge(o_w_split, pair + 1)
                pe.wait_ge(z_split, 4 * pair + 4)
                for j in range(4):
                    if j < 2:
                        pe.wait_ge(before[0], before[1] + j)
                    else:
                        pe.wait_ge(o_added, 4 * pair + (j - 1))
                    for i in range(2):
                        t = 2 * j + i
                        for s in range(2):
                            z = tuple(z_p[:, s, k, t * P:(t + 1) * P] for k in range(2))
                            w = tuple(o_w[:, k, s, :] for k in range(2))
                            last = product(psum[:, proj_bank[j % 2], i * D:(i + 1) * D], z, w, s == 0, s == 1)
                    last.then_inc(o_done, 1)

            def scores(head, s, b, first):
                if b % 2 == 0:
                    pe.wait_ge(qk_copied, 4 * head + (b + 2))
                if not (first and b < 2):
                    pe.wait_ge(scores_read, 4 * head + (b - 1))
                bank = psum[:, score_bank[b % 2], :]
                q, k = qk[:, s, 0, :], qk[:, s, 1, :]
                nc.tensor.matmul(bank[:, 0:P], q[:, 2 * b * P:(2 * b + 1) * P], k[:, 2 * b * P:(2 * b + 1) * P],
                                 start=True, stop=True)
                nc.tensor.matmul(bank[:, P:3 * P], q[:, (2 * b + 1) * P:(2 * b + 2) * P],
                                 k[:, 2 * b * P:(2 * b + 2) * P], start=True, stop=True).then_inc(scores_done, 1)

            def turn_probs(head, first, b):
                pe.wait_ge(probs_ready, 4 * head + (b + 1))
                if not (first and b < 2):
                    pe.wait_ge(turned_copied, 4 * head + (b - 1))
                for c in range(3):
                    last = nc.tensor.transpose(psum[:, prt_bank[b % 2], c * P:(c + 1) * P],
                                               pr[:, b, c * P:(c + 1) * P], ident)
                last.then_inc(turned, 1)

            def attend(head, pair, s, b, first):
                if s == 0 and b == 0:
                    pe.wait_ge(v_copied, 4 * pair + 4)
                if b % 2 == 0 and not first:
                    pe.wait_ge(z_split, 2 * head + (b // 2 - 1))
                pe.wait_ge(turned_copied, 4 * head + (b + 1))
                z = psum[:, z_bank[b // 2], (b % 2) * 2 * P:(b % 2 + 1) * 2 * P]
                nc.tensor.matmul(z, v_sb[:, 2 * b, s * P:(s + 1) * P], pr_t[:, b, 0:2 * P], start=True, stop=False)
                last = nc.tensor.matmul(z[:, P:2 * P], v_sb[:, 2 * b + 1, s * P:(s + 1) * P],
                                        pr_t[:, b, 2 * P:3 * P], start=False, stop=True)
                if b % 2 == 1:
                    last.then_inc(z_done, 1)

            def pair_steps(L, p, first=False, last=False):
                pair = p + L * PAIRS
                start = first and L == 0
                for b in (0, 1):
                    scores(2 * pair, 0, b, start)
                if not first:
                    for b in (0, 1):
                        attend(2 * pair - 1, pair - 1, 1, b, False)
                for b in (2, 3):
                    scores(2 * pair, 0, b, start)
                if not first:
                    for b in (2, 3):
                        attend(2 * pair - 1, pair - 1, 1, b, False)
                project_v(L, p)
                project_qk(L, p, 1, (v_copied, 4 * pair + 3), (2 * pair, start))
                for b in (0, 1):
                    scores(2 * pair + 1, 1, b, False)
                if first:
                    pe.wait_ge(logits_copied, L + 1)
                for b in (0, 1):
                    attend(2 * pair, pair, 0, b, start)
                for b in (2, 3):
                    scores(2 * pair + 1, 1, b, False)
                for b in (2, 3):
                    attend(2 * pair, pair, 0, b, start)
                if not first:
                    project_out(L, p - 1, (qk_copied, 8 * pair + 7))
                if not last:
                    project_qk(L, p + 1, 0, (qk_copied, 8 * pair + 7) if first else (o_added, 4 * pair - 1),
                               (2 * pair + 1, False))
                else:
                    for b in range(SEQS):
                        turn_probs(2 * pair + 1, False, b)

            def attend_last(L):
                for b in range(SEQS):
                    attend(L * HEADS + HEADS - 1, L * PAIRS + PAIRS - 1, 1, b, False)

            def up(u, s, first):
                pe.wait_ge(up_w_split, u + 1)
                for half in range(2):
                    if not first:
                        pe.wait_ge(relu_done, 2 * u + (half - 3))
                    for kc in range(KC):
                        w = tuple(up_w[:, s, i, kc, :] for i in range(2))
                        last = product(psum[:, up_bank[2 * s + half], :], w, xn_half(kc, half), kc == 0, kc == KC - 1)
                    last.then_inc(up_done, 1)

            def down_two(u, s, j, n, first):
                pe.wait_ge(hid_split, 2 * u + (j // 2 + 1))
                if not first:
                    pe.wait_ge(y_added, n - 3)
                for i in range(2):
                    t = 2 * j + i
                    h = tuple(h0_p[:, s, k, t * P:(t + 1) * P] for k in range(2))
                    last = product(psum[:, down_bank[n % 4 if isinstance(n, int) else j], i * D:(i + 1) * D],
                                   h, (down_w[:, s, 0, :], down_w[:, s, 1, :]), True, True)
                last.then_inc(down_done, 1)

            def down(u, s, first):
                pe.wait_ge(down_w_split, u + 1)
                for j in range(4):
                    down_two(u, s, j, 4 * u + j, first)

            def gate_up(e, half, first, chunks=range(CH)):
                for c in chunks:
                    if half == 0:
                        pe.wait_ge(gu_w_split, CH * e + (c + 1))
                    if not (first and c < 2):
                        pe.wait_ge(mul_done, 12 * e + (6 * half + c - 1))
                    n = 2 if c < FULL else 1
                    at = c * KC * 2 * P
                    for g in range(n):
                        for kc in range(KC):
                            col = at + kc * n * P + g * P
                            last = product(psum[:, up_bank[2 * (c % 2) + g], :],
                                           (gu_w[:, 0, col:col + P], gu_w[:, 1, col:col + P]),
                                           xn_half(kc, half), kc == 0, kc == KC - 1)
                    last.then_inc(gu_done, 1)

            def down1(e, half, first):
                if half == 0:
                    pe.wait_ge(down1_w_split, 3 * e + 3)
                pe.wait_ge(hid1_split, 12 * e + (6 * half + 6))
                for j in range(2):
                    if not first:
                        pe.wait_ge(y1_added, 4 * e + (2 * half + j - 3))
                    for i in range(2):
                        t = 2 * j + i
                        for c in range(CH):
                            h = tuple(h1_p[:, half, k, c, t * P:(t + 1) * P] for k in range(2))
                            w = tuple(down1_w[:, k, c, :] for k in range(2))
                            last = product(psum[:, down_bank[2 * half + j], i * D:(i + 1) * D], h, w,
                                           c == 0, c == CH - 1)
                    last.then_inc(down1_done, 1)

            for L in range(2):
                before = None if L == 0 else (o_added, 4 * PAIRS - 1)
                for half in range(2):
                    turn_xn(L, half)
                    pe.wait_ge(xn_split, 4 * L + 2 * half + 2)
                    project_qk(L, 0, 0, before, jobs=(2 * half, 2 * half + 1))
                    router(L, half)
                pair_steps(L, 0, first=True)
                with pe.Fori(1, PAIRS - 1) as p:
                    pair_steps(L, p)
                pair_steps(L, PAIRS - 1, last=True)
                pe.wait_ge(o_added, 4 * (L * PAIRS + PAIRS - 1))
                if L == 0:
                    up(0, 0, True)
                    attend_last(L)
                    pe.wait_ge(scores_read, 4 * HEADS)
                    up(1, 1, True)
                    project_out(L, PAIRS - 1, (relu_done, 1))
                    down(0, 0, True)
                    pe.wait_ge(o_added, 4 * PAIRS)
                    up(2, 0, False)
                    down(1, 1, False)
                    with pe.Fori(1, UNITS // 2 - 1) as i:
                        up(2 * i + 1, 1, False)
                        down(2 * i, 0, False)
                        up(2 * i + 2, 0, False)
                        down(2 * i + 1, 1, False)
                    up(UNITS - 1, 1, False)
                    pe.wait_ge(down_w_split, UNITS)
                    for n, (u, j) in enumerate(last_jobs):
                        down_two(u, u % 2, j, 4 * (UNITS - 2) + n, False)
                else:
                    gate_up(0, 0, True, chunks=(0,))
                    attend_last(L)
                    pe.wait_ge(scores_read, 8 * HEADS)
                    gate_up(0, 0, True, chunks=(1,))
                    project_out(L, PAIRS - 1, (mul_done, 1))
                    pe.wait_ge(o_added, 8 * PAIRS)
                    gate_up(0, 0, True, chunks=range(2, CH))
                    gate_up(0, 1, False)
                    pe.wait_ge(pad_zero, 2)
                    down1(0, 0, True)
                    gate_up(1, 0, False)
                    down1(0, 1, True)
                    with pe.Fori(1, E1 - 1) as e:
                        gate_up(e, 1, False)
                        down1(e, 0, False)
                        gate_up(e + 1, 0, False)
                        down1(e, 1, False)
                    gate_up(E1 - 1, 1, False)
                    down1(E1 - 1, 0, False)
                    down1(E1 - 1, 1, False)

        @block.scalar
        def _(act):
            def hi_part(dst, src):
                return nc.scalar.activation(dst, src, ACT.Copy)

            def split_router(L):
                W = 32 if L == 0 else E1
                act.wait_ge(router_loaded, 16 * (L + 1))
                if L == 1:
                    act.wait_ge(logits_done, 1)
                hi_part(router_w[:, 0, :, 0:W], router_raw[:, :, 0:W]).then_inc(router_hi, 1)

            def split_qk(L, p, s, old):
                head = 2 * p + (L * HEADS + s)
                act.wait_ge(qk_loaded[s], 16 * p + 16 * (L * PAIRS + 1))
                if old:
                    act.wait_ge(qk_done, 4 * head - 4)
                hi_part(qk_w[:, s, 0, :, :].rearrange("p a b -> p (a b)"), qk_raw[:, s, :]).then_inc(qk_w_hi, 1)

            def split_v(L, p, old):
                pair = p + L * PAIRS
                act.wait_ge(v_loaded, 16 * pair + 16)
                if old:
                    act.wait_ge(v_done, 4 * pair)
                hi_part(v_w[:, 0, :, :].rearrange("p a b -> p (a b)"), v_raw[:, :]).then_inc(v_w_hi, 1)

            def split_o(L, p, old):
                pair = p + L * PAIRS
                act.wait_ge(o_loaded, 16 * pair + 16)
                if old:
                    act.wait_ge(o_done, 4 * pair)
                hi_part(o_w[:, 0, :, :].rearrange("p a b -> p (a b)"), o_raw[:, :]).then_inc(o_w_hi, 1)

            def split_up(u, s, old):
                act.wait_ge(up_loaded[s], 8 * u + (16 - 8 * s))
                if old:
                    act.wait_ge(up_done, 2 * u - 2)
                hi_part(up_w[:, s, 0, :, :].rearrange("p a b -> p (a b)"), up_raw[:, s, :]).then_inc(up_w_hi, 1)

            def split_down(u, s, old):
                act.wait_ge(down_loaded[s], 8 * u + (16 - 8 * s))
                if old:
                    act.wait_ge(down_done, 4 * u - 4)
                hi_part(down_w[:, s, 0, :], down_raw[:, s, :]).then_inc(down_w_hi, 1)

            def split_gu(e, c, old):
                at, n = c * KC * 2 * P, KC * 2 * P if c < FULL else KC * P
                if c == 0:
                    act.wait_ge(gu_loaded, 16 * e + 16)
                if old:
                    act.wait_ge(gu_done, 12 * e + (c - 5))
                hi_part(gu_w[:, 0, at:at + n], gu_raw[:, at:at + n]).then_inc(gu_w_hi, 1)

            def split_down1(e, k, old):
                if k == 0:
                    act.wait_ge(down1_loaded, 16 * e + 16)
                    if old:
                        act.wait_ge(down1_done, 4 * e)
                hi_part(down1_w[:, 0, 2 * k:2 * k + 2, :].rearrange("p a b -> p (a b)"),
                        down1_raw[:, 2 * k * D:(2 * k + 2) * D]).then_inc(down1_w_hi, 1)

            def copy_turned(head, b):
                act.wait_ge(turned, 4 * head + (b + 1))
                nc.scalar.activation(pr_t[:, b, :], psum[:, prt_bank[b % 2], 0:3 * P],
                                     ACT.Copy).then_inc(turned_copied, 1)

            def softcap(head):
                for b in range(SEQS):
                    act.wait_ge(scores_done, 4 * head + (b + 1))
                    nc.scalar.activation(sc[:, b, :], psum[:, score_bank[b % 2], 0:3 * P], ACT.Tanh,
                                         scale=SCALE / CAP).then_inc(scores_read, 1)

            def exponentials(L, head, b):
                if L == 0:
                    act.wait_ge(masked, 4 * head + (b + 1))
                else:
                    act.wait_ge(negmax_ready, 4 * (head - HEADS) + (b + 1))
                for c, (lo, hi) in enumerate(((0, P), (P, 3 * P))):
                    if L == 0:
                        nc.scalar.activation(pr[:, b, lo:hi], sc[:, b, lo:hi], ACT.Exp, scale=CAP,
                                             accum_out=row_sum[:, b, c:c + 1]).then_inc(exp_done, 1)
                    else:
                        nc.scalar.activation(pr[:, b, lo:hi], sc[:, b, lo:hi], ACT.Exp,
                                             bias=neg_max[:, b, c:c + 1],
                                             accum_out=row_sum[:, b, c:c + 1]).then_inc(exp_done, 1)

            def take_z(head, pair, s, old):
                for j in range(2):
                    act.wait_ge(z_done, 2 * head + (j + 1))
                    if old and s == 0 and j == 0:
                        act.wait_ge(o_done, 4 * pair)
                    hi_part(z_p[:, s, 0, j * HALF:(j + 1) * HALF], psum[:, z_bank[j], :]).then_inc(z_hi, 1)

            def copy_v(pair, j):
                act.wait_ge(v_done, 4 * pair + (j + 1))
                nc.scalar.activation(v_sb[:, 2 * j:2 * j + 2, :].rearrange("p a b -> p (a b)"),
                                     psum[:, proj_bank[j % 2], :], ACT.Copy).then_inc(v_copied, 1)

            def copy_qk(head, s, turning=None, jobs=range(4)):
                for j in jobs:
                    if turning is not None:
                        copy_turned(turning, j)
                    act.wait_ge(qk_done, 4 * head + (j + 1))
                    nc.scalar.activation(qk[:, s, j % 2, (j // 2) * HALF:(j // 2 + 1) * HALF],
                                         psum[:, proj_bank[j % 2], :], ACT.Copy).then_inc(qk_copied, 1)

            def pair_steps(L, p, first=False, last=False):
                pair = p + L * PAIRS

                def weights0():
                    if not last:
                        split_qk(L, p + 1, 0, True)
                    if not first:
                        split_o(L, p - 1, not (isinstance(p, int) and p == 1))

                def weights1():
                    if not last:
                        split_qk(L, p + 1, 1, True)
                        split_v(L, p + 1, True)

                if L == 0:
                    softcap(2 * pair)
                if L == 1:
                    weights0()
                exponentials(L, 2 * pair, 0)
                exponentials(L, 2 * pair, 1)
                copy_v(pair, 0)
                exponentials(L, 2 * pair, 2)
                copy_v(pair, 1)
                copy_v(pair, 2)
                exponentials(L, 2 * pair, 3)
                copy_v(pair, 3)
                if L == 0:
                    weights0()
                if L == 1 and last:
                    for c in range(3):
                        split_gu(0, c, False)
                if not first:
                    take_z(2 * pair - 1, pair - 1, 1, False)
                copy_qk(2 * pair + 1, 1, turning=2 * pair)
                if L == 0:
                    softcap(2 * pair + 1)
                if L == 1:
                    weights1()
                for b in range(SEQS):
                    exponentials(L, 2 * pair + 1, b)
                if L == 0:
                    weights1()
                if L == 0 and last:
                    split_up(0, 0, False)
                    split_up(1, 1, False)
                if L == 1 and last:
                    for c in range(3, CH):
                        split_gu(0, c, False)
                take_z(2 * pair, pair, 0, not first)
                if last:
                    split_o(L, p, True)
                if not last:
                    copy_qk(2 * pair + 2, 0, turning=2 * pair + 1)
                else:
                    for b in range(SEQS):
                        copy_turned(2 * pair + 1, b)

            def hidden(u, s):
                for half in range(2):
                    act.wait_ge(up_done, 2 * u + (half + 1))
                    nc.scalar.activation(hid[:, half, :], psum[:, up_bank[2 * s + half], :],
                                         ACT.Relu).then_inc(relu_done, 1)
                for half in range(2):
                    act.wait_ge(relu_done, 2 * u + (half + 1))
                    nc.scalar.activation(hid[:, half, :], hid[:, half, :], ACT.Square).then_inc(square_done, 1)
                for half in range(2):
                    act.wait_ge(square_done, 2 * u + (half + 1))
                    hi_part(h0_p[:, s, 0, half * HALF:(half + 1) * HALF], hid[:, half, :]).then_inc(hid_hi, 1)

            def unit(u, s, up_old, down_old, more=True):
                if more:
                    split_up(u + 1, 1 - s, up_old)
                act.wait_ge(hid_split, 2 * u)
                hidden(u, s)
                split_down(u, s, down_old)

            def expert_half(e, half, split_next, first, after_first=None):
                def take_hi(c):
                    act.wait_ge(mul_done, 12 * e + (6 * half + c + 1))
                    r = P if c < FULL else TAIL
                    hi_part(h1_p[0:r, half, 0, c, :], hid[0:r, c % 2, :]).then_inc(hid1_hi, 1)

                for c in range(CH):
                    act.wait_ge(gu_done, 12 * e + (6 * half + c + 1))
                    if not (first and c < 2):
                        act.wait_ge(mul_done, 12 * e + (6 * half + c - 1))
                    r = P if c < FULL else TAIL
                    nc.scalar.activation(gate_act[0:r, c % 2, :], psum[0:r, up_bank[2 * (c % 2)], :],
                                         ACT.Silu).then_inc(silu_done, 1)
                    if c > 0:
                        take_hi(c - 1)
                    elif after_first is not None:
                        after_first()
                    if split_next:
                        split_gu(e + 1, c, True)
                take_hi(CH - 1)

            for L in range(2):
                end = L * HEADS + HEADS - 1
                for half in range(2):
                    act.wait_ge(var_ready, 2 * L + half + 1)
                    tiles = slice(4 * half, 4 * half + 4)
                    nc.scalar.activation(std[:, tiles], var_eps[:, tiles], ACT.Sqrt).then_inc(std_ready, 1)
                    if half == 0:
                        split_qk(L, 0, 0, False)
                    else:
                        split_router(L)
                        copy_qk(L * HEADS, 0, jobs=(0, 1))
                    for kc in range(KC):
                        act.wait_ge(xn_turned, 4 * L + 2 * half + kc + 1)
                        hi_part(xn_t[:, 0, kc, half * HALF:(half + 1) * HALF],
                                psum[:, 2 + 2 * half + kc, :]).then_inc(xn_hi, 1)
                split_v(L, 0, False)
                split_qk(L, 0, 1, False)
                copy_qk(L * HEADS, 0, jobs=(2, 3))
                act.wait_ge(logits_copied, L + 1)
                if L == 0:
                    nc.scalar.activation(sig[:, :, :], logits[:, :, :], ACT.Exp, scale=-1.0).then_inc(logits_exp, 1)
                else:
                    nc.scalar.activation(sig[:, :, 0:E1], logits[:, :, 0:E1], ACT.Exp).then_inc(logits_exp, 1)
                pair_steps(L, 0, first=True)
                with act.Fori(1, PAIRS - 1) as p:
                    pair_steps(L, p)
                pair_steps(L, PAIRS - 1, last=True)
                if L == 0:
                    hidden(0, 0)
                    take_z(end, PAIRS - 1, 1, False)
                    split_down(0, 0, False)
                    unit(1, 1, True, False)
                    with act.Fori(1, UNITS // 2 - 1) as i:
                        unit(2 * i, 0, True, True)
                        unit(2 * i + 1, 1, True, True)
                    unit(UNITS - 2, 0, True, True)
                    unit(UNITS - 1, 1, True, True, more=False)
                else:
                    expert_half(0, 0, False, True, after_first=lambda: take_z(end, 2 * PAIRS - 1, 1, False))
                    for k in range(3):
                        split_down1(0, k, False)
                    with act.Fori(0, E1 - 1) as e:
                        expert_half(e, 1, True, False)
                        expert_half(e + 1, 0, False, False)
                        for k in range(3):
                            split_down1(e + 1, k, True)
                    expert_half(E1 - 1, 1, False, False)

        @block.gpsimd
        def _(pool):
            def mask(head, b):
                pool.wait_ge(scores_read, 4 * head + (b + 1))
                blocks = sc[:, b, :].rearrange("p (c k) -> p c k", c=3)[:, 0:3:2, :]
                nc.gpsimd.tensor_tensor(blocks, blocks, future.unsqueeze(1).to_broadcast([P, 2, P]),
                                        ALU.add).then_inc(masked, 1)

            pool.wait_ge(const_loaded, 16)

            with pool.Fori(0, HEADS) as head:
                for b in range(SEQS):
                    mask(head, b)
            for half, left in enumerate((v_done, o_done)):
                pool.wait_ge(left, 8 * PAIRS)
                nc.gpsimd.memset(h1_p[TAIL:P, half, :, FULL, :].bitcast(F32), 0.0).then_inc(pad_zero, 1)

        @block.vector
        def _(dve):
            links = [0]

            def link(ins):
                links[0] += 1
                ins.then_inc(dve_chain, 1)
                dve.wait_ge(dve_chain, links[0])

            def lo_part(dst, src, hi):
                return nc.vector.tensor_tensor(dst, src, hi.bitcast(F32), ALU.subtract)

            def split_router(L):
                W = 32 if L == 0 else E1
                dve.wait_ge(router_hi, L + 1)
                lo_part(router_w[:, 1, :, 0:W], router_raw[:, :, 0:W], router_w[:, 0, :, 0:W]).then_inc(router_split, 1)

            def split_qk(L, p, s):
                head = 2 * p + (L * HEADS + s)
                dve.wait_ge(qk_w_hi, head + 1)
                lo_part(qk_w[:, s, 1, :, :].rearrange("p a b -> p (a b)"), qk_raw[:, s, :],
                        qk_w[:, s, 0, :, :].rearrange("p a b -> p (a b)")).then_inc(qk_w_split, 1)

            def split_v(L, p):
                dve.wait_ge(v_w_hi, p + (L * PAIRS + 1))
                lo_part(v_w[:, 1, :, :].rearrange("p a b -> p (a b)"), v_raw[:, :],
                        v_w[:, 0, :, :].rearrange("p a b -> p (a b)")).then_inc(v_w_split, 1)

            def split_o(L, p):
                dve.wait_ge(o_w_hi, p + (L * PAIRS + 1))
                lo_part(o_w[:, 1, :, :].rearrange("p a b -> p (a b)"), o_raw[:, :],
                        o_w[:, 0, :, :].rearrange("p a b -> p (a b)")).then_inc(o_w_split, 1)

            def split_up(u, s):
                dve.wait_ge(up_w_hi, u + 1)
                lo_part(up_w[:, s, 1, :, :].rearrange("p a b -> p (a b)"), up_raw[:, s, :],
                        up_w[:, s, 0, :, :].rearrange("p a b -> p (a b)")).then_inc(up_w_split, 1)

            def split_down(u, s):
                dve.wait_ge(down_w_hi, u + 1)
                lo_part(down_w[:, s, 1, :], down_raw[:, s, :], down_w[:, s, 0, :]).then_inc(down_w_split, 1)

            def split_gu(e, c):
                at, n = c * KC * 2 * P, KC * 2 * P if c < FULL else KC * P
                dve.wait_ge(gu_w_hi, CH * e + (c + 1))
                lo_part(gu_w[:, 1, at:at + n], gu_raw[:, at:at + n], gu_w[:, 0, at:at + n]).then_inc(gu_w_split, 1)

            def split_down1(e, k):
                dve.wait_ge(down1_w_hi, 3 * e + (k + 1))
                lo_part(down1_w[:, 1, 2 * k:2 * k + 2, :].rearrange("p a b -> p (a b)"),
                        down1_raw[:, 2 * k * D:(2 * k + 2) * D],
                        down1_w[:, 0, 2 * k:2 * k + 2, :].rearrange("p a b -> p (a b)")).then_inc(down1_w_split, 1)

            def variances(L, half):
                tiles = range(4 * half, 4 * half + 4)
                if L == 0:
                    dve.wait_ge(x_loaded[half], 16)
                for t in tiles:
                    if L == 1 and t % 2 == 0:
                        dve.wait_ge(y_added, 4 * (UNITS - 2) + last_jobs.index((UNITS - 1, t // 2)) + 1)
                    last = nc.vector.bn_stats(stats[:, t, :], x_sb[:, t, :])
                link(last)
                for t in tiles:
                    last = nc.vector.bn_aggr(mean_var[:, t, :], stats[:, t, :])
                link(last)
                four = slice(4 * half, 4 * half + 4)
                nc.vector.tensor_scalar(var_eps[:, four], mean_var[:, four, 1], EPS, None,
                                        ALU.add).then_inc(var_ready, 1)

            def normalise_x(L, half):
                four = slice(4 * half, 4 * half + 4)
                r, v, n = rstd[:, four], var_eps[:, four], newton[:, four]
                dve.wait_ge(std_ready, 2 * L + half + 1)
                link(nc.vector.reciprocal(r, std[:, four]))
                link(nc.vector.tensor_tensor(n, r, r, ALU.mult))
                link(nc.vector.tensor_tensor(n, n, v, ALU.mult))
                link(nc.vector.tensor_scalar(n, n, -0.5, 1.5, ALU.mult, ALU.add))
                link(nc.vector.tensor_tensor(r, r, n, ALU.mult))
                for t in range(4 * half, 4 * half + 4):
                    nc.vector.tensor_scalar(xn[:, t, :], x_sb[:, t, :], mean_var[:, t, 0:1], rstd[:, t:t + 1],
                                            ALU.subtract, ALU.mult).then_inc(xn_ready, 1)

            def split_xn(L, half):
                for kc in range(KC):
                    dve.wait_ge(xn_hi, 4 * L + 2 * half + kc + 1)
                    cols = slice(half * HALF, (half + 1) * HALF)
                    lo_part(xn_t[:, 1, kc, cols], psum[:, 2 + 2 * half + kc, :],
                            xn_t[:, 0, kc, cols]).then_inc(xn_split, 1)

            def rank_of(values, n, tiles, ahead, tie, tri, out):
                shape = [P, tiles, n, n]
                a = ahead[:, 0:tiles * n * n].rearrange("p (t i j) -> p t i j", t=tiles, i=n)
                b = tie[:, 0:tiles * n * n].rearrange("p (t i j) -> p t i j", t=tiles, i=n)
                other = values.unsqueeze(2).to_broadcast(shape)
                own = values.unsqueeze(3).to_broadcast(shape)
                nc.vector.tensor_tensor(a, other, own, ALU.is_gt)
                link(nc.vector.tensor_tensor(b, other, own, ALU.is_equal))
                link(nc.vector.tensor_tensor(b, b, tri.unsqueeze(1).to_broadcast(shape), ALU.mult))
                link(nc.vector.tensor_tensor(a, a, b, ALU.add))
                link(nc.vector.tensor_reduce(out, a, X_AXIS, ALU.add))

            def router_scores(L):
                W = 32 if L == 0 else E1
                dve.wait_ge(logits_done, L + 1)
                link(nc.vector.tensor_copy(logits[:, :, 0:W],
                                           psum[:, 6, 0:TILES * W].rearrange("p (t w) -> p t w", t=TILES)))
                if L == 0:
                    nc.vector.memset(coef[:, :, E0:UNITS], 1.0).then_inc(logits_copied, 1)
                    dve.wait_ge(logits_exp, 1)
                    link(nc.vector.tensor_scalar(sig[:, :, :], sig[:, :, :], 1.0, None, ALU.add))
                    link(nc.vector.reciprocal(sig[:, :, :], sig[:, :, :]))
                else:
                    link(nc.vector.tensor_reduce(per_tile[:, 0, :], logits[:, :, 0:E1], X_AXIS, ALU.max))
                    nc.vector.tensor_tensor(logits[:, :, 0:E1], logits[:, :, 0:E1],
                                            per_tile[:, 0, :].unsqueeze(2).to_broadcast([P, TILES, E1]),
                                            ALU.subtract).then_inc(logits_copied, 1)
                    dve.wait_ge(logits_exp, 2)
                    link(nc.vector.tensor_reduce(per_tile[:, 0, :], sig[:, :, 0:E1], X_AXIS, ALU.add))
                    link(nc.vector.reciprocal(per_tile[:, 1, :], per_tile[:, 0, :]))
                    link(nc.vector.tensor_tensor(sig[:, :, 0:E1], sig[:, :, 0:E1],
                                                 per_tile[:, 1, :].unsqueeze(2).to_broadcast([P, TILES, E1]), ALU.mult))

            def choose0_groups():
                prob = sig[:, :, 0:E0]
                link(nc.vector.tensor_tensor(choice[:, :, :], prob,
                                             e_bias.unsqueeze(1).to_broadcast([P, TILES, E0]), ALU.add))
                four = choice[:, :, :].rearrange("p t (g e) -> p (t g) e", e=4)
                a, b, c, d = (four[:, :, i] for i in range(4))
                s = [small[:, i, :] for i in range(8)]
                nc.vector.tensor_tensor(s[0], a, b, ALU.max)
                nc.vector.tensor_tensor(s[1], a, b, ALU.min)
                nc.vector.tensor_tensor(s[2], c, d, ALU.max)
                link(nc.vector.tensor_tensor(s[3], c, d, ALU.min))
                nc.vector.tensor_tensor(s[4], s[0], s[2], ALU.max)
                nc.vector.tensor_tensor(s[5], s[0], s[2], ALU.min)
                link(nc.vector.tensor_tensor(s[6], s[1], s[3], ALU.max))
                link(nc.vector.tensor_tensor(s[7], s[5], s[6], ALU.max))
                link(nc.vector.tensor_tensor(groups[:, :, :], s[4].rearrange("p (t g) -> p t g", g=4),
                                             s[7].rearrange("p (t g) -> p t g", g=4), ALU.add))
                rank_of(groups[:, :, :], 4, TILES, beats, ties, tri4, rank[:, :, 0:4])
                link(nc.vector.tensor_scalar(groups[:, :, :], rank[:, :, 0:4], 2.0, None, ALU.is_lt))
                by_group = choice[:, :, :].rearrange("p t (g e) -> p t g e", e=4)
                link(nc.vector.tensor_tensor(by_group, by_group,
                                             groups[:, :, :].unsqueeze(3).to_broadcast([P, TILES, 4, 4]), ALU.mult))

            def choose0_rank(t):
                rank_of(choice[:, t:t + 4, :], E0, 4, beats, ties, tri16, rank[:, t:t + 4, :])

            def choose0_weights():
                prob = sig[:, :, 0:E0]
                link(nc.vector.tensor_scalar(rank[:, :, :], rank[:, :, :], 2.0, None, ALU.is_lt))
                link(nc.vector.tensor_tensor(rank[:, :, :], rank[:, :, :], prob, ALU.mult))
                link(nc.vector.tensor_reduce(per_tile[:, 0, :], rank[:, :, :], X_AXIS, ALU.add))
                link(nc.vector.tensor_scalar(per_tile[:, 0, :], per_tile[:, 0, :], 1e-20, None, ALU.add))
                link(nc.vector.reciprocal(per_tile[:, 1, :], per_tile[:, 0, :]))
                link(nc.vector.tensor_tensor(coef[:, :, 0:E0], rank[:, :, :],
                                             per_tile[:, 1, :].unsqueeze(2).to_broadcast([P, TILES, E0]), ALU.mult))

            def choose1():
                rank_of(sig[:, :, 0:E1], E1, TILES, beats1, ties1, tri8, rank[:, :, 0:E1])
                link(nc.vector.tensor_scalar(rank[:, :, 0:E1], rank[:, :, 0:E1], 2.0, None, ALU.is_lt))
                link(nc.vector.tensor_tensor(coef[:, :, 0:E1], rank[:, :, 0:E1], sig[:, :, 0:E1], ALU.mult))

            def clip_scores(head):
                for b in range(SEQS):
                    dve.wait_ge(scores_done, 4 * head + (b + 1))
                    nc.vector.tensor_scalar(sc[:, b, :], psum[:, score_bank[b % 2], 0:3 * P], -CLIP / SCALE,
                                            CLIP / SCALE, ALU.max, ALU.min).then_inc(scores_read, 1)

            def bias_and_max(head, b, s):
                own = head - HEADS
                for c, (lo, hi) in enumerate(((0, P), (P, 3 * P))):
                    nc.vector.tensor_tensor_reduce(out=sc[:, b, lo:hi], in0=sc[:, b, lo:hi], in1=alibi[:, s, lo:hi],
                                                   scale=SCALE, scalar=NEG, op0=ALU.add, op1=ALU.max,
                                                   accum_out=row_max[:, b, c:c + 1]).then_inc(max_ready, 1)
                dve.wait_ge(max_ready, 8 * own + (2 * b + 2))
                nc.vector.tensor_scalar(neg_max[:, b, :], row_max[:, b, :], -1.0, None,
                                        ALU.mult).then_inc(negmax_ready, 1)

            def normalise(L, head, b, gate_at):
                dve.wait_ge(exp_done, 8 * head + (2 * b + 2))
                nc.vector.reciprocal(row_scale[:, b, :], row_sum[:, b, :]).then_inc(recip_done, 1)
                dve.wait_ge(recip_done, 4 * head + (b + 1))
                if L == 0:
                    nc.vector.tensor_tensor(row_scale[:, b, :], row_scale[:, b, :], gate_at(b),
                                            ALU.mult).then_inc(row_scaled, 1)
                    dve.wait_ge(row_scaled, 4 * head + (b + 1))
                nc.vector.tensor_scalar(pr[:, b, 0:P], pr[:, b, 0:P], row_scale[:, b, 0:1], None, ALU.mult)
                nc.vector.tensor_scalar(pr[:, b, P:3 * P], pr[:, b, P:3 * P], row_scale[:, b, 1:2], None,
                                        ALU.mult).then_inc(probs_ready, 1)

            def softmax(L, p, s, adding=None):
                head = 2 * p + (L * HEADS + s)

                def gate_at(b):
                    return sig[:, 2 * b:2 * b + 2, bass.ds(2 * p + (E0 + s), 1)].rearrange("p a b -> p (a b)")

                def add(j):
                    if adding is not None:
                        add_out(adding, j)

                if L == 1:
                    bias_and_max(head, 0, s)
                    bias_and_max(head, 1, s)
                normalise(L, head, 0, gate_at)
                if L == 1:
                    bias_and_max(head, 2, s)
                add(0)
                normalise(L, head, 1, gate_at)
                if L == 1:
                    bias_and_max(head, 3, s)
                add(1)
                normalise(L, head, 2, gate_at)
                add(2)
                normalise(L, head, 3, gate_at)
                add(3)

            def take_z(head, s):
                for j in range(2):
                    dve.wait_ge(z_hi, 2 * head + (j + 1))
                    cols = slice(j * HALF, (j + 1) * HALF)
                    lo_part(z_p[:, s, 1, cols], psum[:, z_bank[j], :], z_p[:, s, 0, cols]).then_inc(z_split, 1)

            def add_out(pair, j):
                dve.wait_ge(o_done, 4 * pair + (j + 1))
                x2 = x_sb[:, 2 * j:2 * j + 2, :].rearrange("p a b -> p (a b)")
                nc.vector.tensor_tensor(x2, psum[:, proj_bank[j % 2], :], x2, ALU.add).then_inc(o_added, 1)

            def pair_steps(L, p, first=False, last=False):
                pair = p + L * PAIRS
                if L == 1:
                    clip_scores(2 * pair)
                    dve.wait_ge(alibi_loaded[0], 16 * p + 16)
                    dve.wait_ge(scores_read, 8 * pair + 4)
                    if not last:
                        split_qk(L, p + 1, 0)
                softmax(L, p, 0)
                if L == 0 and not last:
                    split_qk(L, p + 1, 0)
                if not first:
                    split_o(L, p - 1)
                if L == 0 and first:
                    choose0_groups()
                if L == 0 and last:
                    choose0_rank(4)
                if L == 1 and last:
                    for c in range(3):
                        split_gu(0, c)
                if not first:
                    take_z(2 * pair - 1, 1)
                if L == 1:
                    clip_scores(2 * pair + 1)
                    dve.wait_ge(alibi_loaded[1], 16 * p + 16)
                    dve.wait_ge(scores_read, 8 * pair + 8)
                    if not last:
                        split_qk(L, p + 1, 1)
                softmax(L, p, 1, adding=None if first else pair - 1)
                if not last:
                    if L == 0:
                        split_qk(L, p + 1, 1)
                    split_v(L, p + 1)
                if L == 0 and first:
                    choose0_rank(0)
                if L == 1 and first:
                    choose1()
                if L == 0 and last:
                    split_up(0, 0)
                    split_up(1, 1)
                if L == 1 and last:
                    for c in range(3, CH):
                        split_gu(0, c)
                take_z(2 * pair, 0)
                if last:
                    split_o(L, p)
                if L == 0 and last:
                    choose0_weights()

            def hidden_lo(u, s):
                for half in range(2):
                    dve.wait_ge(hid_hi, 2 * u + (half + 1))
                    cols = slice(half * HALF, (half + 1) * HALF)
                    lo_part(h0_p[:, s, 1, cols], hid[:, half, :], h0_p[:, s, 0, cols]).then_inc(hid_split, 1)

            def add_two(u, j, n):
                dve.wait_ge(down_done, n + 1)
                if isinstance(n, int) and n < 4:
                    dve.wait_ge(o_added, 4 * (PAIRS - 1) + j + 1)
                elif isinstance(n, int) and n >= 4 * (UNITS - 2):
                    dve.wait_ge(y_added, n - 1)
                else:
                    dve.wait_ge(y_added, n - 3)
                for i in range(2):
                    t = 2 * j + i
                    last = nc.vector.scalar_tensor_tensor(
                        out=x_sb[:, t, :], in0=psum[:, down_bank[n % 4 if isinstance(n, int) else j], i * D:(i + 1) * D],
                        scalar=coef[:, t, bass.ds(u, 1)], in1=x_sb[:, t, :], op0=ALU.mult, op1=ALU.add)
                last.then_inc(y_added, 1)

            def add_unit(u):
                for j in range(4):
                    add_two(u, j, 4 * u + j)

            def unit(u, s, more=True):
                if more:
                    split_up(u + 1, 1 - s)
                hidden_lo(u, s)
                split_down(u, s)
                add_unit(u - 1)

            def expert_half(e, half, split_next, first=False, after=(None, None)):
                def take_lo(c):
                    dve.wait_ge(hid1_hi, 12 * e + (6 * half + c + 1))
                    r = P if c < FULL else TAIL
                    lo_part(h1_p[0:r, half, 1, c, :], hid[0:r, c % 2, :], h1_p[0:r, half, 0, c, :]).then_inc(hid1_split, 1)

                for c in range(CH):
                    dve.wait_ge(silu_done, 12 * e + (6 * half + c + 1))
                    if not (first and c < 2):
                        dve.wait_ge(hid1_split, 12 * e + (6 * half + c - 1))
                    b = up_bank[2 * (c % 2)]
                    if c < FULL:
                        r, up_part = P, psum[:, b + 1, :]
                    else:
                        r, up_part = TAIL, psum[TAIL:2 * TAIL, b, :]
                    nc.vector.tensor_tensor(hid[0:r, c % 2, :], gate_act[0:r, c % 2, :], up_part,
                                            ALU.mult).then_inc(mul_done, 1)
                    if c > 0:
                        take_lo(c - 1)
                    if c < 2 and after[c] is not None:
                        after[c]()
                    if split_next:
                        split_gu(e + 1, c)
                take_lo(CH - 1)

            def add_expert(e, half):
                for j in range(2):
                    dve.wait_ge(down1_done, 4 * e + (2 * half + j + 1))
                    for i in range(2):
                        t = 4 * half + 2 * j + i
                        last = nc.vector.scalar_tensor_tensor(
                            out=x_sb[:, t, :], in0=psum[:, down_bank[2 * half + j], i * D:(i + 1) * D],
                            scalar=coef[:, t, bass.ds(e, 1)], in1=x_sb[:, t, :], op0=ALU.mult, op1=ALU.add)
                    last.then_inc(y1_added, 1)

            for L in range(2):
                variances(L, 0)
                normalise_x(L, 0)
                if L == 1:
                    for n in range(4, 8):
                        add_two(*last_jobs[n], 4 * (UNITS - 2) + n)
                variances(L, 1)
                split_qk(L, 0, 0)
                split_xn(L, 0)
                normalise_x(L, 1)
                split_router(L)
                split_xn(L, 1)
                split_v(L, 0)
                split_qk(L, 0, 1)
                router_scores(L)
                pair_steps(L, 0, first=True)
                with dve.Fori(1, PAIRS - 1) as p:
                    pair_steps(L, p)
                pair_steps(L, PAIRS - 1, last=True)
                end = L * HEADS + HEADS - 1

                def add_last_out():
                    for j in range(4):
                        add_out(L * PAIRS + PAIRS - 1, j)

                if L == 0:
                    hidden_lo(0, 0)
                    take_z(end, 1)
                    split_down(0, 0)
                    add_last_out()
                    unit(1, 1)
                    with dve.Fori(1, UNITS // 2 - 1) as i:
                        unit(2 * i, 0)
                        unit(2 * i + 1, 1)
                    unit(UNITS - 2, 0)
                    hidden_lo(UNITS - 1, 1)
                    split_down(UNITS - 1, 1)
                    for n in range(4):
                        add_two(*last_jobs[n], 4 * (UNITS - 2) + n)
                else:
                    expert_half(0, 0, False, first=True, after=(lambda: take_z(end, 1), add_last_out))
                    for k in range(3):
                        split_down1(0, k)
                    with dve.Fori(0, E1 - 1) as e:
                        expert_half(e, 1, True)
                        add_expert(e, 0)
                        expert_half(e + 1, 0, False)
                        add_expert(e, 1)
                        for k in range(3):
                            split_down1(e + 1, k)
                    expert_half(E1 - 1, 1, False)
                    add_expert(E1 - 1, 0)
                    add_expert(E1 - 1, 1)


def kernel(L0_attn_x, L0_attn_w_qkv, L0_attn_w_gates, L0_attn_w_out, L0_ffn_router_weight, L0_ffn_e_bias,
           L0_ffn_w_up, L0_ffn_w_down, L0_ffn_shared_up, L0_ffn_shared_down, L1_attn_Wq, L1_attn_Wk, L1_attn_Wv,
           L1_attn_Wo, L1_ffn_router_w, L1_ffn_gate_w, L1_ffn_up_w, L1_ffn_down_w):
    import numpy as np
    import concourse.bacc as bacc
    from concourse.bass_utils import run_bass_kernel_spmd

    def a(v):
        return np.asarray(v)

    def chunks(w):
        return w.reshape(KC, P, -1).transpose(1, 0, 2)

    def attention_weights(wq, wk, wv, wo):
        q, k = (chunks(w).reshape(P, KC, HEADS, P).transpose(2, 0, 1, 3) for w in (wq, wk))
        qk = np.concatenate([q, k], axis=3).reshape(HEADS, P, KC * 2 * P)
        v = chunks(wv).reshape(P, KC, PAIRS, 2 * P).transpose(2, 0, 1, 3).reshape(PAIRS, P, KC * 2 * P)
        o = wo.reshape(PAIRS, 2, P, D).transpose(0, 2, 1, 3).reshape(PAIRS, P, 2 * D)
        return qk, v, o

    HD = HEADS * P
    qkv = a(L0_attn_w_qkv)
    layer0 = attention_weights(qkv[:, 0:HD], qkv[:, HD:2 * HD], qkv[:, 2 * HD:3 * HD], a(L0_attn_w_out))
    layer1 = attention_weights(a(L1_attn_Wq).T, a(L1_attn_Wk).T, a(L1_attn_Wv).T, a(L1_attn_Wo).T)
    router0 = chunks(np.concatenate([a(L0_ffn_router_weight).T, a(L0_attn_w_gates)], axis=1))
    router1 = chunks(a(L1_ffn_router_w).T)
    ups = np.concatenate([a(L0_ffn_w_up), a(L0_ffn_shared_up).reshape(D, SHARED, P).transpose(1, 0, 2)])
    ups = ups.reshape(UNITS, KC, P, P).transpose(0, 2, 1, 3).reshape(UNITS, P, KC * P)
    downs = np.concatenate([a(L0_ffn_w_down), a(L0_ffn_shared_down).reshape(SHARED, P, D)])
    wide = FULL * P

    def inner(w):
        w = w.transpose(0, 2, 1).reshape(E1, KC, P, -1).transpose(0, 2, 1, 3)
        return w[..., 0:wide].reshape(E1, P, KC, FULL, P).transpose(0, 1, 3, 2, 4), w[..., wide:]

    (g, g_tail), (u, u_tail) = inner(a(L1_ffn_gate_w)), inner(a(L1_ffn_up_w))
    gu = np.concatenate([np.concatenate([g, u], axis=4).reshape(E1, P, -1),
                         np.concatenate([g_tail, u_tail], axis=3).reshape(E1, P, -1)], axis=2)
    d1 = np.zeros((E1, CH * P, D), np.float32)
    d1[:, 0:wide + TAIL, :] = a(L1_ffn_down_w).transpose(0, 2, 1)
    d1 = d1.reshape(E1, CH, P, D).transpose(0, 2, 1, 3).reshape(E1, P, CH * D)

    def before(n):
        return np.broadcast_to(np.tril(np.ones((n, n), np.float32), -1).reshape(1, n * n), (P, n * n))

    const = np.concatenate([np.eye(P, dtype=np.float32), np.broadcast_to(a(L0_ffn_e_bias)[None, :], (P, E0)),
                            before(16), before(4), before(8),
                            np.where(np.arange(P)[None, :] > np.arange(P)[:, None], NEG, 0.0).astype(np.float32)],
                           axis=1)
    start = 2.0 ** (-8.0 / HEADS)
    slopes = np.array([start * start ** i for i in range(HEADS)], np.float32).astype(np.float64)
    query, key = np.arange(P)[:, None], np.arange(2 * P)[None, :]
    line = slopes[:, None, None] * key[None] * (P ** 0.5)
    alibi = np.concatenate([np.where(key[None, :, 0:P] > query[None], NEG, line[:, :, 0:P]),
                            np.where(key[None] > query[None] + P, NEG, line)], axis=2).astype(np.float32)

    arrays, args = {}, []
    nc = bacc.Bacc("TRN2", target_bir_lowering=False, num_devices=1)

    def give(name, array):
        arrays[name] = np.ascontiguousarray(array)
        return nc.dram_tensor(name, arrays[name].shape, F32, kind="ExternalInput").ap()

    x_d = give("x", a(L0_attn_x).reshape(TILES, P, D).transpose(1, 0, 2))
    const_d = give("const_in", const)
    alibi_d = give("alibi_in", alibi)
    qk_d, v_d, o_d = ([give(f"{n}{i}", w[k]) for i, w in enumerate((layer0, layer1))]
                      for k, n in enumerate(("w_qk", "w_v", "w_o")))
    router_d = [give("router0", router0), give("router1", router1)]
    up_d, down_d = give("w_up0", ups), give("w_down0", downs)
    gu_d, down1_d = give("w_gate_up1", gu), give("w_down1", d1)
    out_d = nc.dram_tensor("out", (P, TILES, D), F32, kind="ExternalOutput").ap()
    bass_two_layers(nc, x_d, const_d, alibi_d, qk_d, v_d, o_d, router_d, up_d, down_d, gu_d, down1_d, out_d)
    r = run_bass_kernel_spmd(nc, [arrays], core_ids=[0])
    return r.results[0]["out"].transpose(1, 0, 2).reshape(SEQS, 2 * P, D)
```

```python
from contextlib import ExitStack

import concourse.bass as bass
from concourse import mybir

F32 = mybir.dt.float32
F32R = mybir.dt.float32r
U32 = mybir.dt.uint32
ALU = mybir.AluOpType
ACT = mybir.ActivationFunctionType
X_AXIS = mybir.AxisListType.X

P = 128
D = 256
KC = D // P
SEQS = 4
TILES = 8
TOK = TILES * P
HALF = TOK // 2
HEADS = 16
PAIRS = HEADS // 2
E0, SHARED, E1 = 16, 4, 8
UNITS = E0 + SHARED
FULL, TAIL = 5, 64
CH = FULL + 1
ROWS = 2 * P
SLOTS = 2 * TOK // ROWS + E1 - 1
ZERO_BLOCKS = 2 * SLOTS // (PAIRS - 2)
JOBS = CH // 2
JOB_COLS = [2 * KC * 2 * P] * (JOBS - 1) + [KC * 2 * P + KC * P]
JOB_AT = [sum(JOB_COLS[:k]) for k in range(JOBS)]
GU = FULL * KC * 2 * P + KC * P
CAP = 50.0
SCALE = float(P) ** -0.5
CLIP = 1024.0
NEG = -1e30
EPS = 1e-5


def bass_two_layers(nc, x_d, const_d, alibi_d, qk_d, v_d, o_d, router_d, up_d, down_d, gu_d, down1_d,
                    route_d, sorted_d, outputs_d, out_d):
    with ExitStack() as ctx:
        def sb(name, shape, dt=F32):
            return ctx.enter_context(nc.sbuf_tensor(name, shape, dt))

        def sem(name):
            return ctx.enter_context(nc.semaphore(name))

        H1 = 11264 + 2 * 2 * D
        parts = sb("parts", [P, H1 + 2 * GU + 2 * CH * D], F32R)

        def region(at, *dims):
            n = 1
            for d in dims:
                n *= d
            names = " ".join(f"a{i}" for i in range(len(dims)))
            sizes = {f"a{i}": d for i, d in enumerate(dims)}
            return parts[:, at:at + n].rearrange(f"p ({names}) -> p {names}", **sizes)

        qk_w = region(0, 2, 2, KC, 2 * P)
        v_w = region(2048, 2, KC, 2 * P)
        h0_p = region(3072, 2, 2, TOK)
        z_p = region(7168, 2, 2, TOK)
        o_w = region(11264, 2, 2, D)
        h1_p = region(0, 2, 2, CH, ROWS)
        gu_w = region(H1, 2, GU)
        down1_w = region(H1 + 2 * GU, 2, CH, D)
        last_down_w = gu_w[:, :, 0:CH * D].rearrange("p a (c d) -> p a c d", c=CH)
        up_w = region(H1, 2, 2, KC, P)
        down_w = region(H1 + 1024, 2, 2, D)
        xn_t = sb("xn_t", [P, 2, KC, TOK], F32R)
        xs_t = xn_t[:, :, :, :].rearrange("p a b c -> p (a b c)")[:, 0:4 * KC * ROWS].rearrange(
            "p (a b c d) -> p a b c d", a=2, b=2, c=KC)
        router_w = sb("router_w", [P, 2, KC, 32], F32R)

        x_sb = sb("x_sb", [P, TILES, D])
        qk = sb("qk", [P, 2, 2, TOK])
        xs = qk[:, :, :, :].rearrange("p a b t -> p a (b t)")[:, :, 0:2 * D].rearrange(
            "p a (i d) -> p a i d", i=2)
        y_back = qk[:, :, :, :].rearrange("p a b t -> p (a b t)").rearrange(
            "p (t c d) -> p t c d", t=TILES, c=2)
        v_sb = sb("v_sb", [P, TILES, 2 * P])
        y_out = v_sb[:, 0:4, :].rearrange("p (a i) d -> p a i d", a=2)
        sc = sb("sc", [P, SEQS, 3 * P])
        pr = sb("pr", [P, SEQS, 3 * P])
        pr_t = sb("pr_t", [P, SEQS, 3 * P])
        qk_raw = sb("qk_raw", [P, 2, KC * 2 * P])
        v_raw = sb("v_raw", [P, KC * 2 * P])
        o_raw = sb("o_raw", [P, 2 * D])
        alibi = sb("alibi", [P, 2, 3 * P])
        up_raw = sb("up_raw", [P, 2, KC * P])
        down_raw = sb("down_raw", [P, 2, D])
        gu_raw = sb("gu_raw", [P, GU])
        down1_raw = sb("down1_raw", [P, CH * D])
        xn = [qk[:, 1, :, :].rearrange("p b t -> p (b t)").rearrange("p (t d) -> p t d", t=TILES),
              gu_raw[:, 0:TILES * D].rearrange("p (t d) -> p t d", t=TILES)]
        router_raw = sb("router_raw", [P, KC, 32])
        const = sb("const", [P, 608])
        ident = const[:, 0:128]
        future = const[:, 480:608]
        e_bias = const[:, 128:144]
        tri16 = const[:, 144:400].rearrange("p (a b) -> p a b", a=16)
        tri4 = const[:, 400:416].rearrange("p (a b) -> p a b", a=4)
        tri8 = const[:, 416:480].rearrange("p (a b) -> p a b", a=8)
        gate_act = sc[:, :, :].rearrange("p b c -> p (b c)")[:, 0:2 * HALF].rearrange("p (s t) -> p s t", s=2)
        gate1 = gate_act.rearrange("p s (c t) -> p s c t", c=2)
        hid = pr[:, :, :].rearrange("p b c -> p (b c)")[:, 0:2 * HALF].rearrange("p (s t) -> p s t", s=2)
        hid1 = hid.rearrange("p s (c t) -> p s c t", c=2)
        at = TILES * D
        before_row, all_rows = gu_raw[:, at:at + P], gu_raw[:, at + P:at + 2 * P]
        slot_number = gu_raw[:, at + 2 * P:at + 2 * P + SLOTS]
        own_row = gu_raw[:, at + 2 * P + 15:at + 2 * P + 16]
        zeros = gu_raw[:, GU - D:GU]
        at += 2 * P + 16
        row_of, mark, by_expert = (gu_raw[:, at + 64 * i:at + 64 * i + 64] for i in range(3))
        past = gu_raw[:, at + 192:at + 192 + SLOTS * (E1 - 1)]
        at += 192 + SLOTS * (E1 - 1)
        first_mark, both_marks, used, start, end_slot = (gu_raw[:, at + 8 * i:at + 8 * i + 8] for i in range(5))
        expert_of = gu_raw[:, at + 40:at + 40 + SLOTS]
        position = gu_raw[:, at + 56:at + 56 + TILES * E1]
        count = gu_raw[:, at + 120:at + 120 + E1]
        token_row = sb("token_row", [P, 2, TILES], U32)
        weight_row = sb("weight_row", [P, 16], U32)
        row_sum = sb("row_sum", [P, SEQS, 2])
        row_max = sb("row_max", [P, SEQS, 2])
        neg_max = sb("neg_max", [P, SEQS, 2])
        row_scale = sb("row_scale", [P, SEQS, 2])
        stats = sb("stats", [P, TILES, 6])
        mean_var = sb("mean_var", [P, TILES, 2])
        var_eps = sb("var_eps", [P, TILES])
        std = sb("std", [P, TILES])
        rstd = sb("rstd", [P, TILES])
        newton = sb("newton", [P, TILES])
        logits = sb("logits", [P, TILES, 32])
        sig = sb("sig", [P, TILES, 32])
        coef = sb("coef", [P, TILES, UNITS])
        small = sb("small", [P, 8, 32])
        selected = small[:, 0:2, :].rearrange("p a b -> p (a b)")
        weight = small[:, 2, 0:2 * TILES].rearrange("p (c t) -> p c t", c=2)
        groups = sb("groups", [P, TILES, 4])
        choice = sb("choice", [P, TILES, 16])
        rank = sb("rank", [P, TILES, 16])
        per_tile = sb("per_tile", [P, 2, TILES])
        beats = gu_raw[:, 0:1024]
        ties = gu_raw[:, 1024:2048]
        beats1 = up_raw[:, :, :].rearrange("p a b -> p (a b)")
        ties1 = down_raw[:, :, :].rearrange("p a b -> p (a b)")

        psum = ctx.enter_context(nc.psum_tensor("psum", [P, 8, 512], F32))
        proj_bank, score_bank, prt_bank, z_bank = (0, 1), (2, 3), (4, 5), (6, 7)
        up_bank, down_bank = (0, 1, 2, 3), (4, 5, 6, 7)

        x_loaded, const_loaded = [sem(f"x_loaded{i}") for i in range(2)], sem("const_loaded")
        router_loaded = sem("router_loaded")
        qk_loaded = [sem(f"qk_loaded{s}") for s in range(2)]
        alibi_loaded = [sem(f"alibi_loaded{s}") for s in range(2)]
        v_loaded, o_loaded = sem("v_loaded"), sem("o_loaded")
        up_loaded = [sem(f"up_loaded{s}") for s in range(2)]
        down_loaded = [sem(f"down_loaded{s}") for s in range(2)]
        gu_loaded, down1_loaded = [sem(f"gu_loaded{k}") for k in range(JOBS)], sem("down1_loaded")
        route_loaded, zeros_set, zeros_stored = sem("route_loaded"), sem("zeros_set"), sem("zeros_stored")
        selection_ready, placed, placed_read = sem("selection_ready"), sem("placed"), sem("placed_read")
        rows_ready, sorted_rows = sem("rows_ready"), sem("sorted_rows")
        xs_loaded = [sem(f"xs_loaded{s}") for s in range(2)]
        xs_turned, xs_hi, xs_split = sem("xs_turned"), sem("xs_hi"), sem("xs_split")
        y_copied, y_stored = sem("y_copied"), [sem(f"y_stored{s}") for s in range(2)]
        y_loaded = [[sem(f"y_loaded{choice}_{t}") for t in range(TILES)] for choice in range(2)]
        qk_w_hi, qk_w_split = sem("qk_w_hi"), sem("qk_w_split")
        v_w_hi, v_w_split = sem("v_w_hi"), sem("v_w_split")
        o_w_hi, o_w_split = sem("o_w_hi"), sem("o_w_split")
        up_w_hi, up_w_split = sem("up_w_hi"), sem("up_w_split")
        down_w_hi, down_w_split = sem("down_w_hi"), sem("down_w_split")
        gu_w_hi, gu_w_split = sem("gu_w_hi"), sem("gu_w_split")
        down1_w_hi, down1_w_split = sem("down1_w_hi"), sem("down1_w_split")
        router_hi, router_split = sem("router_hi"), sem("router_split")
        dve_chain = sem("dve_chain")
        var_ready, std_ready = sem("var_ready"), sem("std_ready")
        xn_ready, xn_turned, xn_hi, xn_split = sem("xn_ready"), sem("xn_turned"), sem("xn_hi"), sem("xn_split")
        logits_done, logits_copied, logits_exp = sem("logits_done"), sem("logits_copied"), sem("logits_exp")
        qk_done, qk_copied = sem("qk_done"), sem("qk_copied")
        v_done, v_copied = sem("v_done"), sem("v_copied")
        o_done, o_added = sem("o_done"), sem("o_added")
        scores_done, scores_read = sem("scores_done"), sem("scores_read")
        masked, max_ready, negmax_ready = sem("masked"), sem("max_ready"), sem("negmax_ready")
        exp_done, recip_done, row_scaled, probs_ready = (sem("exp_done"), sem("recip_done"), sem("row_scaled"),
                                                         sem("probs_ready"))
        turned, turned_copied = sem("turned"), sem("turned_copied")
        z_done, z_hi, z_split = sem("z_done"), sem("z_hi"), sem("z_split")
        up_done, relu_done, square_done, hid_hi, hid_split = (sem("up_done"), sem("relu_done"), sem("square_done"),
                                                              sem("hid_hi"), sem("hid_split"))
        down_done, y_added = sem("down_done"), sem("y_added")
        gu_done, silu_done, mul_done, hid1_hi, hid1_split = (sem("gu_done"), sem("silu_done"), sem("mul_done"),
                                                             sem("hid1_hi"), sem("hid1_split"))
        down1_done, final = sem("down1_done"), sem("final")
        pad_zero = sem("pad_zero")
        stored = sem("stored")

        last_jobs = [(u, 2 * half + i) for half in range(2) for u in (UNITS - 2, UNITS - 1) for i in range(2)]

        block = ctx.enter_context(nc.Block())

        @block.sync
        def _(sp):
            for half in range(2):
                sp.dma_start(x_sb[:, 4 * half:4 * half + 4, :],
                             x_d[:, 4 * half:4 * half + 4, :]).then_inc(x_loaded[half], 16)
            sp.dma_start(const[:, :], const_d).then_inc(const_loaded, 16)
            for L in range(2):
                W = 32 if L == 0 else E1

                def load_qk(h, s):
                    sp.dma_start(qk_raw[:, s, :], qk_d[L][h]).then_inc(qk_loaded[s], 16)

                def load_v(p):
                    sp.dma_start(v_raw[:, :], v_d[L][p]).then_inc(v_loaded, 16)

                def load_o(p):
                    sp.dma_start(o_raw[:, :], o_d[L][p]).then_inc(o_loaded, 16)

                def load_alibi(h, s):
                    sp.dma_start(alibi[:, s, :], alibi_d[h]).then_inc(alibi_loaded[s], 16)

                if L == 1:
                    sp.wait_ge(qk_w_split, HEADS)
                    sp.wait_ge(v_w_split, PAIRS)
                load_qk(0, 0)
                sp.dma_start(router_raw[:, :, 0:W], router_d[L]).then_inc(router_loaded, 16)
                load_v(0)
                load_qk(1, 1)
                if L == 1:
                    sp.wait_ge(o_w_split, PAIRS)
                    load_alibi(0, 0)
                    load_alibi(1, 1)
                load_o(0)
                if L == 0:
                    for u in range(2):
                        sp.dma_start(up_raw[:, u, :], up_d[u]).then_inc(up_loaded[u], 16)
                        sp.dma_start(down_raw[:, u, :], down_d[u]).then_inc(down_loaded[u], 16)
                    sp.dma_start(gu_raw[:, TILES * D:TILES * D + 2 * P + 16], route_d).then_inc(route_loaded, 16)
                    sp.wait_ge(zeros_set, 1)
                    for i in range(2):
                        at_row = (SLOTS - 1) * ROWS + i * P
                        sp.dma_start(outputs_d[at_row:at_row + P, :], zeros).then_inc(zeros_stored, 16)

                def next_pair(p, first=False):
                    sp.wait_ge(qk_w_split, 2 * p + (L * HEADS + 1))
                    load_qk(2 * p + 2, 0)
                    sp.wait_ge(v_w_split, p + (L * PAIRS + 1))
                    load_v(p + 1)
                    sp.wait_ge(qk_w_split, 2 * p + (L * HEADS + 2))
                    load_qk(2 * p + 3, 1)
                    if not first:
                        sp.wait_ge(o_w_split, p + L * PAIRS)
                        load_o(p)
                    if L == 1:
                        sp.wait_ge(max_ready, 16 * p + 8)
                        load_alibi(2 * p + 2, 0)
                        sp.wait_ge(max_ready, 16 * p + 16)
                        load_alibi(2 * p + 3, 1)

                next_pair(0, first=True)
                with sp.Fori(1, PAIRS - 1) as p:
                    next_pair(p)
                    if L == 0:
                        for i in range(ZERO_BLOCKS):
                            at_row = (p - 1) * (ZERO_BLOCKS * P) + i * P
                            sp.dma_start(sorted_d[bass.ds(at_row, P), :], zeros).then_inc(zeros_stored, 16)
                sp.wait_ge(o_w_split, L * PAIRS + PAIRS - 1)
                load_o(PAIRS - 1)
                if L == 0:
                    with sp.Fori(0, UNITS // 2 - 1) as i:
                        for s in range(2):
                            sp.wait_ge(up_w_split, 2 * i + (s + 1))
                            sp.dma_start(up_raw[:, s, :], up_d[2 * i + (2 + s)]).then_inc(up_loaded[s], 16)
                            sp.wait_ge(down_w_split, 2 * i + (s + 1))
                            sp.dma_start(down_raw[:, s, :], down_d[2 * i + (2 + s)]).then_inc(down_loaded[s], 16)
                else:
                    def load_rows(s, parity):
                        for i in range(2):
                            sp.dma_start(xs[:, parity, i, :],
                                         sorted_d[bass.ds(s * ROWS + i * P, P), :]).then_inc(xs_loaded[parity], 16)

                    def store_outputs(s, parity):
                        sp.wait_ge(y_copied, s + 1)
                        for i in range(2):
                            sp.dma_start(outputs_d[bass.ds(s * ROWS + i * P, P), :],
                                         y_out[:, parity, i, :]).then_inc(y_stored[parity], 16)

                    sp.wait_ge(sorted_rows, 16 * 2 * TILES)
                    for s in range(2):
                        sp.wait_ge(scores_done, 4 * (2 * HEADS - 1 + s))
                        load_rows(s, s)
                    sp.wait_ge(xs_turned, 1)
                    load_rows(2, 0)
                    with sp.Fori(0, (SLOTS - 3) // 2) as i:
                        for r in range(2):
                            sp.wait_ge(xs_turned, 2 * i + (r + 2))
                            load_rows(2 * i + (r + 3), 1 - r)
                            store_outputs(2 * i + r, r)
                    for s in range(SLOTS - 3, SLOTS):
                        store_outputs(s, s % 2)
            for j in range(4):
                sp.wait_ge(final, TILES + 2 * j + 2)
                sp.dma_start(out_d[:, 2 * j:2 * j + 2, :], x_sb[:, 2 * j:2 * j + 2, :]).then_inc(stored, 16)
            sp.wait_ge(stored, 64)

        @block.tensor
        def _(pe):
            def product(out, w, x, first, last):
                nc.tensor.matmul(out, w[1], x[0], start=first, stop=False)
                nc.tensor.matmul(out, w[0], x[1], start=False, stop=False)
                return nc.tensor.matmul(out, w[0], x[0], start=False, stop=last)

            def xn_half(kc, half):
                return tuple(xn_t[:, i, kc, half * HALF:(half + 1) * HALF] for i in range(2))

            def xn_tile(kc, t):
                return tuple(xn_t[:, i, kc, t * P:(t + 1) * P] for i in range(2))

            def turn_xn(L, half):
                if L == 0 and half == 0:
                    pe.wait_ge(const_loaded, 16)
                pe.wait_ge(xn_ready, TILES * L + 4 * half + 4)
                for kc in range(KC):
                    for t in range(4):
                        last = nc.tensor.transpose(psum[:, 2 + 2 * half + kc, t * P:(t + 1) * P],
                                                   xn[L][:, 4 * half + t, kc * P:(kc + 1) * P], ident)
                    last.then_inc(xn_turned, 1)

            def router(L, half):
                W = 32 if L == 0 else E1
                if half == 0:
                    pe.wait_ge(router_split, L + 1)
                for t in range(4 * half, 4 * half + 4):
                    for kc in range(KC):
                        last = product(psum[:, 6, t * W:(t + 1) * W], xn_tile(kc, t),
                                       (router_w[:, 0, kc, 0:W], router_w[:, 1, kc, 0:W]), kc == 0, kc == KC - 1)
                if half == 1:
                    last.then_inc(logits_done, 1)

            def project_qk(L, p, s, before, turning=None, jobs=range(4)):
                head = 2 * p + (L * HEADS + s)
                for j in jobs:
                    half, c = j // 2, j % 2
                    if turning is not None:
                        turn_probs(*turning, j)
                    if j == 0:
                        pe.wait_ge(qk_w_split, head + 1)
                    if j < 2 and before is not None:
                        pe.wait_ge(before[0], before[1] + j)
                    if j >= 2:
                        pe.wait_ge(qk_copied, 4 * head + (j - 1))
                    for kc in range(KC):
                        w = tuple(qk_w[:, s, i, kc, c * P:(c + 1) * P] for i in range(2))
                        last = product(psum[:, proj_bank[j % 2], :], w, xn_half(kc, half), kc == 0, kc == KC - 1)
                    last.then_inc(qk_done, 1)

            def project_v(L, p):
                pair = p + L * PAIRS
                pe.wait_ge(v_w_split, pair + 1)
                for j in range(4):
                    if j < 2:
                        pe.wait_ge(qk_copied, 8 * pair + (j + 3))
                    else:
                        pe.wait_ge(v_copied, 4 * pair + (j - 1))
                    for i in range(2):
                        t = 2 * j + i
                        for kc in range(KC):
                            w = tuple(v_w[:, k, kc, :] for k in range(2))
                            last = product(psum[:, proj_bank[j % 2], i * D:(i + 1) * D], xn_tile(kc, t), w,
                                           kc == 0, kc == KC - 1)
                    last.then_inc(v_done, 1)

            def project_out(L, p, before):
                pair = p + L * PAIRS
                pe.wait_ge(o_w_split, pair + 1)
                pe.wait_ge(z_split, 4 * pair + 4)
                for j in range(4):
                    if j < 2:
                        pe.wait_ge(before[0], before[1] + j)
                    else:
                        pe.wait_ge(o_added, 4 * pair + (j - 1))
                    for i in range(2):
                        t = 2 * j + i
                        for s in range(2):
                            z = tuple(z_p[:, s, k, t * P:(t + 1) * P] for k in range(2))
                            w = tuple(o_w[:, k, s, :] for k in range(2))
                            last = product(psum[:, proj_bank[j % 2], i * D:(i + 1) * D], z, w, s == 0, s == 1)
                    last.then_inc(o_done, 1)

            def scores(head, s, b, first):
                if b % 2 == 0:
                    pe.wait_ge(qk_copied, 4 * head + (b + 2))
                if not (first and b < 2):
                    pe.wait_ge(scores_read, 4 * head + (b - 1))
                bank = psum[:, score_bank[b % 2], :]
                q, k = qk[:, s, 0, :], qk[:, s, 1, :]
                nc.tensor.matmul(bank[:, 0:P], q[:, 2 * b * P:(2 * b + 1) * P], k[:, 2 * b * P:(2 * b + 1) * P],
                                 start=True, stop=True)
                nc.tensor.matmul(bank[:, P:3 * P], q[:, (2 * b + 1) * P:(2 * b + 2) * P],
                                 k[:, 2 * b * P:(2 * b + 2) * P], start=True, stop=True).then_inc(scores_done, 1)

            def turn_probs(head, first, b):
                pe.wait_ge(probs_ready, 4 * head + (b + 1))
                if not (first and b < 2):
                    pe.wait_ge(turned_copied, 4 * head + (b - 1))
                for c in range(3):
                    last = nc.tensor.transpose(psum[:, prt_bank[b % 2], c * P:(c + 1) * P],
                                               pr[:, b, c * P:(c + 1) * P], ident)
                last.then_inc(turned, 1)

            def attend(head, pair, s, b, first):
                if s == 0 and b == 0:
                    pe.wait_ge(v_copied, 4 * pair + 4)
                if b % 2 == 0 and not first:
                    pe.wait_ge(z_split, 2 * head + (b // 2 - 1))
                pe.wait_ge(turned_copied, 4 * head + (b + 1))
                z = psum[:, z_bank[b // 2], (b % 2) * 2 * P:(b % 2 + 1) * 2 * P]
                nc.tensor.matmul(z, v_sb[:, 2 * b, s * P:(s + 1) * P], pr_t[:, b, 0:2 * P], start=True, stop=False)
                last = nc.tensor.matmul(z[:, P:2 * P], v_sb[:, 2 * b + 1, s * P:(s + 1) * P],
                                        pr_t[:, b, 2 * P:3 * P], start=False, stop=True)
                if b % 2 == 1:
                    last.then_inc(z_done, 1)

            def place_tokens(pair):
                pe.wait_ge(selection_ready, 1)
                pe.wait_ge(scores_read, 8 * pair + 4)
                pe.wait_ge(route_loaded, 16)
                out = psum[:, score_bank[1], :]
                n = TILES * E1
                nc.tensor.matmul(out[:, 0:n], before_row, selected, start=True, stop=False)
                for tiles in range(1, TILES):
                    nc.tensor.matmul(out[:, tiles * E1:n], all_rows, selected[:, 0:n - tiles * E1], start=False,
                                     stop=tiles == TILES - 1)
                for t in range(TILES):
                    last = nc.tensor.matmul(out[:, n:n + E1], all_rows, selected[:, t * E1:(t + 1) * E1],
                                            start=t == 0, stop=t == TILES - 1)
                last.then_inc(placed, 1)

            def pair_steps(L, p, first=False, last=False, placing=False):
                pair = p + L * PAIRS
                start = first and L == 0
                for b in (0, 1):
                    scores(2 * pair, 0, b, start)
                if not first:
                    for b in (0, 1):
                        attend(2 * pair - 1, pair - 1, 1, b, False)
                for b in (2, 3):
                    scores(2 * pair, 0, b, start)
                if not first:
                    for b in (2, 3):
                        attend(2 * pair - 1, pair - 1, 1, b, False)
                project_v(L, p)
                project_qk(L, p, 1, (v_copied, 4 * pair + 3), (2 * pair, start))
                if placing:
                    place_tokens(pair)
                scores(2 * pair + 1, 1, 0, False)
                if placing:
                    pe.wait_ge(placed_read, 1)
                scores(2 * pair + 1, 1, 1, False)
                if first:
                    pe.wait_ge(logits_copied, L + 1)
                for b in (0, 1):
                    attend(2 * pair, pair, 0, b, start)
                for b in (2, 3):
                    scores(2 * pair + 1, 1, b, False)
                for b in (2, 3):
                    attend(2 * pair, pair, 0, b, start)
                if L == 1 and last:
                    turn_rows(0, 0, score_bank[0])
                if not first:
                    project_out(L, p - 1, (qk_copied, 8 * pair + 7))
                if not last:
                    project_qk(L, p + 1, 0, (qk_copied, 8 * pair + 7) if first else (o_added, 4 * pair - 1),
                               (2 * pair + 1, False))
                else:
                    if L == 1:
                        pe.wait_ge(o_added, 4 * pair)
                        gate_up(0, 0, 0)
                    for b in range(SEQS):
                        turn_probs(2 * pair + 1, False, b)

            def attend_last(L):
                for b in range(SEQS):
                    attend(L * HEADS + HEADS - 1, L * PAIRS + PAIRS - 1, 1, b, False)

            def up(u, s, first):
                pe.wait_ge(up_w_split, u + 1)
                for half in range(2):
                    if not first:
                        pe.wait_ge(relu_done, 2 * u + (half - 3))
                    for kc in range(KC):
                        w = tuple(up_w[:, s, i, kc, :] for i in range(2))
                        last = product(psum[:, up_bank[2 * s + half], :], w, xn_half(kc, half), kc == 0, kc == KC - 1)
                    last.then_inc(up_done, 1)

            def down_two(u, s, j, n, first):
                pe.wait_ge(hid_split, 2 * u + (j // 2 + 1))
                if not first:
                    pe.wait_ge(y_added, n - 3)
                for i in range(2):
                    t = 2 * j + i
                    h = tuple(h0_p[:, s, k, t * P:(t + 1) * P] for k in range(2))
                    last = product(psum[:, down_bank[n % 4 if isinstance(n, int) else j], i * D:(i + 1) * D],
                                   h, (down_w[:, s, 0, :], down_w[:, s, 1, :]), True, True)
                last.then_inc(down_done, 1)

            def down(u, s, first):
                pe.wait_ge(down_w_split, u + 1)
                for j in range(4):
                    down_two(u, s, j, 4 * u + j, first)

            def turn_rows(s, parity, bank):
                pe.wait_ge(xs_loaded[parity], 16 * s + (32 - 16 * parity))
                if isinstance(s, int) and s == 0:
                    pe.wait_ge(scores_read, 8 * HEADS)
                if not (isinstance(s, int) and s < 3):
                    pe.wait_ge(xs_split, s - 1)
                for kc in range(KC):
                    for i in range(2):
                        last = nc.tensor.transpose(psum[:, bank, kc * ROWS + i * P:kc * ROWS + (i + 1) * P],
                                                   xs[:, parity, i, kc * P:(kc + 1) * P], ident)
                last.then_inc(xs_turned, 1)

            def gate_up(s, parity, k):
                n = JOBS * s + k
                bank = 2 * ((JOBS * parity + k) % 2)
                if k == 0:
                    pe.wait_ge(xs_split, s + 1)
                pe.wait_ge(gu_w_split, n + 1)
                if not (isinstance(s, int) and JOBS * s + k < 2):
                    pe.wait_ge(mul_done, n - 1)
                for c in (2 * k, 2 * k + 1):
                    parts_of = 2 if c < FULL else 1
                    for g in range(parts_of):
                        for kc in range(KC):
                            col = c * KC * 2 * P + kc * parts_of * P + g * P
                            last = product(psum[:, up_bank[bank + c % 2], g * ROWS:(g + 1) * ROWS],
                                           (gu_w[:, 0, col:col + P], gu_w[:, 1, col:col + P]),
                                           (xs_t[:, parity, 0, kc, :], xs_t[:, parity, 1, kc, :]),
                                           kc == 0, kc == KC - 1)
                last.then_inc(gu_done, 1)

            def down1(s, parity, weights=down1_w):
                pe.wait_ge(down1_w_split, s + 1)
                pe.wait_ge(hid1_split, JOBS * s + JOBS)
                if not (isinstance(s, int) and s < 2):
                    pe.wait_ge(y_copied, s - 1)
                for i in range(2):
                    for c in range(CH):
                        h = tuple(h1_p[:, parity, part, c, i * P:(i + 1) * P] for part in range(2))
                        w = tuple(weights[:, part, c, :] for part in range(2))
                        last = product(psum[:, down_bank[parity], i * D:(i + 1) * D], h, w, c == 0, c == CH - 1)
                last.then_inc(down1_done, 1)

            def slot(s, parity):
                gate_up(s, parity, 0)
                turn_rows(s + 1, 1 - parity, 7 - parity)
                gate_up(s, parity, 1)
                down1(s - 1, 1 - parity)
                gate_up(s, parity, 2)

            for L in range(2):
                before = None if L == 0 else (o_added, 4 * PAIRS - 1)
                turn_xn(L, 0)
                pe.wait_ge(xn_split, 4 * L + 2)
                project_qk(L, 0, 0, before, jobs=(0, 1))
                turn_xn(L, 1)
                router(L, 0)
                pe.wait_ge(xn_split, 4 * L + 4)
                project_qk(L, 0, 0, before, jobs=(2, 3))
                router(L, 1)
                pair_steps(L, 0, first=True)
                if L == 1:
                    pair_steps(L, 1, placing=True)
                with pe.Fori(1 + L, PAIRS - 1) as p:
                    pair_steps(L, p)
                pair_steps(L, PAIRS - 1, last=True)
                if L == 0:
                    pe.wait_ge(o_added, 4 * (PAIRS - 1))
                    up(0, 0, True)
                    attend_last(L)
                    pe.wait_ge(scores_read, 4 * HEADS)
                    up(1, 1, True)
                    project_out(L, PAIRS - 1, (relu_done, 1))
                    down(0, 0, True)
                    pe.wait_ge(o_added, 4 * PAIRS)
                    up(2, 0, False)
                    down(1, 1, False)
                    with pe.Fori(1, UNITS // 2 - 1) as i:
                        up(2 * i + 1, 1, False)
                        down(2 * i, 0, False)
                        up(2 * i + 2, 0, False)
                        down(2 * i + 1, 1, False)
                    up(UNITS - 1, 1, False)
                    for n, (u, j) in enumerate(last_jobs):
                        if n in (0, 2):
                            pe.wait_ge(down_w_split, u + 1)
                        down_two(u, u % 2, j, 4 * (UNITS - 2) + n, False)
                else:
                    attend_last(L)
                    gate_up(0, 0, 1)
                    project_out(L, PAIRS - 1, (mul_done, 1))
                    turn_rows(1, 1, 7)
                    pe.wait_ge(o_added, 8 * PAIRS)
                    gate_up(0, 0, 2)
                    pe.wait_ge(pad_zero, 2)
                    slot(1, 1)
                    with pe.Fori(1, (SLOTS - 1) // 2) as i:
                        slot(2 * i, 0)
                        slot(2 * i + 1, 1)
                    for k in range(JOBS):
                        gate_up(SLOTS - 1, 0, k)
                    down1(SLOTS - 2, 1)
                    down1(SLOTS - 1, 0, last_down_w)

        @block.scalar
        def _(act):
            def hi_part(dst, src):
                return nc.scalar.activation(dst, src, ACT.Copy)

            def split_router(L):
                W = 32 if L == 0 else E1
                act.wait_ge(router_loaded, 16 * (L + 1))
                if L == 1:
                    act.wait_ge(logits_done, 1)
                hi_part(router_w[:, 0, :, 0:W], router_raw[:, :, 0:W]).then_inc(router_hi, 1)

            def split_qk(L, p, s, old):
                head = 2 * p + (L * HEADS + s)
                act.wait_ge(qk_loaded[s], 16 * p + 16 * (L * PAIRS + 1))
                if old:
                    act.wait_ge(qk_done, 4 * head - 4)
                hi_part(qk_w[:, s, 0, :, :].rearrange("p a b -> p (a b)"), qk_raw[:, s, :]).then_inc(qk_w_hi, 1)

            def split_v(L, p, old):
                pair = p + L * PAIRS
                act.wait_ge(v_loaded, 16 * pair + 16)
                if old:
                    act.wait_ge(v_done, 4 * pair)
                hi_part(v_w[:, 0, :, :].rearrange("p a b -> p (a b)"), v_raw[:, :]).then_inc(v_w_hi, 1)

            def split_o(L, p, old):
                pair = p + L * PAIRS
                act.wait_ge(o_loaded, 16 * pair + 16)
                if old:
                    act.wait_ge(o_done, 4 * pair)
                hi_part(o_w[:, 0, :, :].rearrange("p a b -> p (a b)"), o_raw[:, :]).then_inc(o_w_hi, 1)

            def split_up(u, s, old):
                act.wait_ge(up_loaded[s], 8 * u + (16 - 8 * s))
                if old:
                    act.wait_ge(up_done, 2 * u - 2)
                hi_part(up_w[:, s, 0, :, :].rearrange("p a b -> p (a b)"), up_raw[:, s, :]).then_inc(up_w_hi, 1)

            def split_down(u, s, old):
                act.wait_ge(down_loaded[s], 8 * u + (16 - 8 * s))
                if old:
                    act.wait_ge(down_done, 4 * u - 4)
                hi_part(down_w[:, s, 0, :], down_raw[:, s, :]).then_inc(down_w_hi, 1)

            def split_gu(s, k):
                act.wait_ge(gu_loaded[k], 16 * s + 16)
                if not (isinstance(s, int) and s == 0):
                    act.wait_ge(gu_done, JOBS * s + (k - JOBS + 1))
                cols = slice(JOB_AT[k], JOB_AT[k] + JOB_COLS[k])
                hi_part(gu_w[:, 0, cols], gu_raw[:, cols]).then_inc(gu_w_hi, 1)

            def split_down1(s, weights=down1_w):
                act.wait_ge(down1_loaded, 16 * s + 16)
                if isinstance(s, int) and s == SLOTS - 1:
                    act.wait_ge(gu_done, JOBS * s + 2)
                elif not (isinstance(s, int) and s == 0):
                    act.wait_ge(down1_done, s)
                hi_part(weights[:, 0, :, :].rearrange("p a b -> p (a b)"), down1_raw[:, :]).then_inc(down1_w_hi, 1)

            def take_rows(s, parity, bank):
                act.wait_ge(xs_turned, s + 1)
                hi_part(xs_t[:, parity, 0, :, :].rearrange("p c r -> p (c r)"), psum[:, bank, :]).then_inc(xs_hi, 1)

            def copy_turned(head, b):
                act.wait_ge(turned, 4 * head + (b + 1))
                nc.scalar.activation(pr_t[:, b, :], psum[:, prt_bank[b % 2], 0:3 * P],
                                     ACT.Copy).then_inc(turned_copied, 1)

            def softcap(head):
                for b in range(SEQS):
                    act.wait_ge(scores_done, 4 * head + (b + 1))
                    nc.scalar.activation(sc[:, b, :], psum[:, score_bank[b % 2], 0:3 * P], ACT.Tanh,
                                         scale=SCALE / CAP).then_inc(scores_read, 1)

            def exponentials(L, head, b):
                if L == 0:
                    act.wait_ge(masked, 4 * head + (b + 1))
                else:
                    act.wait_ge(negmax_ready, 4 * (head - HEADS) + (b + 1))
                for c, (lo, hi) in enumerate(((0, P), (P, 3 * P))):
                    if L == 0:
                        nc.scalar.activation(pr[:, b, lo:hi], sc[:, b, lo:hi], ACT.Exp, scale=CAP,
                                             accum_out=row_sum[:, b, c:c + 1]).then_inc(exp_done, 1)
                    else:
                        nc.scalar.activation(pr[:, b, lo:hi], sc[:, b, lo:hi], ACT.Exp,
                                             bias=neg_max[:, b, c:c + 1],
                                             accum_out=row_sum[:, b, c:c + 1]).then_inc(exp_done, 1)

            def take_z(head, pair, s, old):
                for j in range(2):
                    act.wait_ge(z_done, 2 * head + (j + 1))
                    if old and s == 0 and j == 0:
                        act.wait_ge(o_done, 4 * pair)
                    hi_part(z_p[:, s, 0, j * HALF:(j + 1) * HALF], psum[:, z_bank[j], :]).then_inc(z_hi, 1)

            def copy_v(pair, j):
                act.wait_ge(v_done, 4 * pair + (j + 1))
                nc.scalar.activation(v_sb[:, 2 * j:2 * j + 2, :].rearrange("p a b -> p (a b)"),
                                     psum[:, proj_bank[j % 2], :], ACT.Copy).then_inc(v_copied, 1)

            def copy_qk(head, s, turning=None, jobs=range(4)):
                for j in jobs:
                    if turning is not None:
                        copy_turned(turning, j)
                    act.wait_ge(qk_done, 4 * head + (j + 1))
                    nc.scalar.activation(qk[:, s, j % 2, (j // 2) * HALF:(j // 2 + 1) * HALF],
                                         psum[:, proj_bank[j % 2], :], ACT.Copy).then_inc(qk_copied, 1)

            def pair_steps(L, p, first=False, last=False):
                pair = p + L * PAIRS

                def weights0():
                    if not last:
                        split_qk(L, p + 1, 0, True)
                    if not first:
                        split_o(L, p - 1, not (isinstance(p, int) and p == 1))

                def weights1():
                    if not last:
                        split_qk(L, p + 1, 1, True)
                        split_v(L, p + 1, True)

                if L == 0:
                    softcap(2 * pair)
                if L == 1:
                    weights0()
                exponentials(L, 2 * pair, 0)
                exponentials(L, 2 * pair, 1)
                copy_v(pair, 0)
                exponentials(L, 2 * pair, 2)
                copy_v(pair, 1)
                copy_v(pair, 2)
                exponentials(L, 2 * pair, 3)
                copy_v(pair, 3)
                if L == 0:
                    weights0()
                if L == 1 and last:
                    split_gu(0, 0)
                    split_gu(0, 1)
                if not first:
                    take_z(2 * pair - 1, pair - 1, 1, False)
                copy_qk(2 * pair + 1, 1, turning=2 * pair)
                if L == 0:
                    softcap(2 * pair + 1)
                if L == 1:
                    weights1()
                for b in range(SEQS):
                    exponentials(L, 2 * pair + 1, b)
                if L == 0:
                    weights1()
                if L == 0 and last:
                    split_up(0, 0, False)
                    split_up(1, 1, False)
                if L == 1 and last:
                    take_rows(0, 0, score_bank[0])
                take_z(2 * pair, pair, 0, not first)
                if last:
                    split_o(L, p, True)
                if L == 1 and last:
                    split_gu(0, 2)
                if not last:
                    copy_qk(2 * pair + 2, 0, turning=2 * pair + 1)
                else:
                    for b in range(SEQS):
                        copy_turned(2 * pair + 1, b)

            def hidden_by_half(u, s):
                for half in range(2):
                    n = 2 * u + (half + 1)
                    act.wait_ge(up_done, n)
                    nc.scalar.activation(hid[:, half, :], psum[:, up_bank[2 * s + half], :],
                                         ACT.Relu).then_inc(relu_done, 1)
                    act.wait_ge(relu_done, n)
                    nc.scalar.activation(hid[:, half, :], hid[:, half, :], ACT.Square).then_inc(square_done, 1)
                    act.wait_ge(square_done, n)
                    hi_part(h0_p[:, s, 0, half * HALF:(half + 1) * HALF], hid[:, half, :]).then_inc(hid_hi, 1)

            def hidden(u, s):
                for half in range(2):
                    act.wait_ge(up_done, 2 * u + (half + 1))
                    nc.scalar.activation(hid[:, half, :], psum[:, up_bank[2 * s + half], :],
                                         ACT.Relu).then_inc(relu_done, 1)
                for half in range(2):
                    act.wait_ge(relu_done, 2 * u + (half + 1))
                    nc.scalar.activation(hid[:, half, :], hid[:, half, :], ACT.Square).then_inc(square_done, 1)
                for half in range(2):
                    act.wait_ge(square_done, 2 * u + (half + 1))
                    hi_part(h0_p[:, s, 0, half * HALF:(half + 1) * HALF], hid[:, half, :]).then_inc(hid_hi, 1)

            def unit(u, s, up_old, down_old):
                split_up(u + 1, 1 - s, up_old)
                act.wait_ge(hid_split, 2 * u)
                hidden(u, s)
                split_down(u, s, down_old)

            def silu(s, parity, k):
                n, at = JOBS * s + k, (JOBS * parity + k) % 2
                act.wait_ge(gu_done, n + 1)
                if not (isinstance(s, int) and JOBS * s + k < 2):
                    act.wait_ge(mul_done, n - 1)
                nc.scalar.activation(gate1[:, at, :, :], psum[:, 2 * at:2 * at + 2, 0:ROWS],
                                     ACT.Silu).then_inc(silu_done, 1)

            def take_hidden(s, parity, k):
                act.wait_ge(mul_done, JOBS * s + (k + 1))
                at = (JOBS * parity + k) % 2
                if k < JOBS - 1:
                    last = hi_part(h1_p[:, parity, 0, 2 * k:2 * k + 2, :], hid1[:, at, :, :])
                else:
                    hi_part(h1_p[:, parity, 0, 2 * k, :], hid1[:, at, 0, :])
                    last = hi_part(h1_p[0:TAIL, parity, 0, FULL, :], hid1[0:TAIL, at, 1, :])
                last.then_inc(hid1_hi, 1)

            def copy_outputs(s, parity):
                act.wait_ge(down1_done, s + 1)
                if not (isinstance(s, int) and s < 2):
                    act.wait_ge(y_stored[parity], 16 * s - 16 * parity)
                nc.scalar.activation(y_out[:, parity, :, :].rearrange("p i d -> p (i d)"),
                                     psum[:, down_bank[parity], :], ACT.Copy).then_inc(y_copied, 1)

            def slot(s, parity):
                silu(s, parity, 0)
                take_hidden(s - 1, 1 - parity, 2)
                split_gu(s + 1, 0)
                take_rows(s + 1, 1 - parity, 7 - parity)
                silu(s, parity, 1)
                take_hidden(s, parity, 0)
                split_gu(s + 1, 1)
                take_hidden(s, parity, 1)
                copy_outputs(s - 1, 1 - parity)
                split_down1(s)
                silu(s, parity, 2)
                split_gu(s + 1, 2)

            def last_slot(s):
                silu(s, 0, 0)
                take_hidden(s - 1, 1, 2)
                silu(s, 0, 1)
                take_hidden(s, 0, 0)
                split_down1(s, last_down_w)
                silu(s, 0, 2)
                take_hidden(s, 0, 1)
                take_hidden(s, 0, 2)
                copy_outputs(s - 1, 1)
                copy_outputs(s, 0)

            for L in range(2):
                end = L * HEADS + HEADS - 1
                for half in range(2):
                    act.wait_ge(var_ready, 2 * L + half + 1)
                    tiles = slice(4 * half, 4 * half + 4)
                    nc.scalar.activation(std[:, tiles], var_eps[:, tiles], ACT.Sqrt).then_inc(std_ready, 1)
                    if half == 0:
                        split_qk(L, 0, 0, False)
                    else:
                        split_router(L)
                        copy_qk(L * HEADS, 0, jobs=(0, 1))
                    for kc in range(KC):
                        act.wait_ge(xn_turned, 4 * L + 2 * half + kc + 1)
                        hi_part(xn_t[:, 0, kc, half * HALF:(half + 1) * HALF],
                                psum[:, 2 + 2 * half + kc, :]).then_inc(xn_hi, 1)
                split_v(L, 0, False)
                split_qk(L, 0, 1, False)
                copy_qk(L * HEADS, 0, jobs=(2, 3))
                act.wait_ge(logits_copied, L + 1)
                if L == 0:
                    nc.scalar.activation(sig[:, :, :], logits[:, :, :], ACT.Exp, scale=-1.0).then_inc(logits_exp, 1)
                else:
                    nc.scalar.activation(sig[:, :, 0:E1], logits[:, :, 0:E1], ACT.Exp).then_inc(logits_exp, 1)
                pair_steps(L, 0, first=True)
                with act.Fori(1, PAIRS - 1) as p:
                    pair_steps(L, p)
                pair_steps(L, PAIRS - 1, last=True)
                if L == 0:
                    hidden(0, 0)
                    take_z(end, PAIRS - 1, 1, False)
                    split_down(0, 0, False)
                    unit(1, 1, True, False)
                    with act.Fori(1, UNITS // 2 - 1) as i:
                        unit(2 * i, 0, True, True)
                        unit(2 * i + 1, 1, True, True)
                    unit(UNITS - 2, 0, True, True)
                    split_down(UNITS - 1, 1, True)
                    act.wait_ge(hid_split, 2 * (UNITS - 1))
                    hidden_by_half(UNITS - 1, 1)
                else:
                    silu(0, 0, 0)
                    take_z(end, 2 * PAIRS - 1, 1, False)
                    split_gu(1, 0)
                    silu(0, 0, 1)
                    take_hidden(0, 0, 0)
                    split_gu(1, 1)
                    take_rows(1, 1, 7)
                    silu(0, 0, 2)
                    take_hidden(0, 0, 1)
                    split_down1(0)
                    split_gu(1, 2)
                    slot(1, 1)
                    with act.Fori(1, (SLOTS - 1) // 2) as i:
                        slot(2 * i, 0)
                        slot(2 * i + 1, 1)
                    last_slot(SLOTS - 1)

        @block.gpsimd
        def _(pool):
            def mask(head, b):
                pool.wait_ge(scores_read, 4 * head + (b + 1))
                blocks = sc[:, b, :].rearrange("p (c k) -> p c k", c=3)[:, 0:3:2, :]
                nc.gpsimd.tensor_tensor(blocks, blocks, future.unsqueeze(1).to_broadcast([P, 2, P]),
                                        ALU.add).then_inc(masked, 1)

            nc.gpsimd.memset(zeros, 0.0).then_inc(zeros_set, 1)
            pool.wait_ge(const_loaded, 16)

            with pool.Fori(0, HEADS) as head:
                for b in range(SEQS):
                    mask(head, b)
            def lo_part(dst, src, hi):
                return nc.gpsimd.tensor_tensor(dst, src, hi.bitcast(F32), ALU.subtract)

            def split_up(u, s):
                pool.wait_ge(up_w_hi, u + 1)
                lo_part(up_w[:, s, 1, :, :].rearrange("p a b -> p (a b)"), up_raw[:, s, :],
                        up_w[:, s, 0, :, :].rearrange("p a b -> p (a b)")).then_inc(up_w_split, 1)

            def split_down(u, s):
                pool.wait_ge(down_w_hi, u + 1)
                lo_part(down_w[:, s, 1, :], down_raw[:, s, :], down_w[:, s, 0, :]).then_inc(down_w_split, 1)

            split_up(0, 0)
            split_up(1, 1)
            with pool.Fori(0, UNITS // 2 - 1) as i:
                split_down(2 * i, 0)
                split_up(2 * i + 2, 0)
                split_down(2 * i + 1, 1)
                split_up(2 * i + 3, 1)
            split_down(UNITS - 2, 0)
            split_down(UNITS - 1, 1)

            pool.wait_ge(rows_ready, 1)
            pool.wait_ge(zeros_stored, 16 * 2 * (SLOTS + 1))
            pool.wait_ge(xn_ready, 2 * TILES)
            for t in range(TILES):
                for choice_no in range(2):
                    rows = bass.IndirectOffsetOnAxis(token_row[:, choice_no, t:t + 1], 0)
                    nc.gpsimd.indirect_dma_start(sorted_d, rows, xn[1][:, t, :], None).then_inc(sorted_rows, 16)
                    pool.wait_ge(sorted_rows, 32 * t + (16 * choice_no + 16))

            def gather_gu(s):
                for k in range(JOBS):
                    if s > 0:
                        pool.wait_ge(gu_w_split, JOBS * (s - 1) + k + 1)
                    nc.gpsimd.indirect_dma_start(gu_raw[:, JOB_AT[k]:JOB_AT[k] + JOB_COLS[k]], None, gu_d[k],
                                                 bass.IndirectOffsetOnAxis(weight_row[:, s:s + 1], 0)
                                                 ).then_inc(gu_loaded[k], 16)

            def gather_down(s):
                if s > 0:
                    pool.wait_ge(down1_w_split, s)
                nc.gpsimd.indirect_dma_start(down1_raw[:, :], None, down1_d,
                                             bass.IndirectOffsetOnAxis(weight_row[:, s:s + 1], 0)
                                             ).then_inc(down1_loaded, 16)

            gather_gu(0)
            gather_down(0)
            pool.wait_ge(qk_done, 8 * HEADS)
            for parity in range(2):
                nc.gpsimd.memset(h1_p[TAIL:P, parity, :, FULL, :].bitcast(F32), 0.0).then_inc(pad_zero, 1)
            gather_gu(1)
            for s in range(2, SLOTS):
                gather_gu(s)
                gather_down(s - 1)
            gather_down(SLOTS - 1)
            for choice_no in (1, 0):
                for parity in range(2):
                    before = SLOTS - choice_no
                    pool.wait_ge(y_stored[parity], 32 * ((before + 1 - parity) // 2))
                for t in range(TILES):
                    nc.gpsimd.indirect_dma_start(y_back[:, t, choice_no, :], None, outputs_d,
                                                 bass.IndirectOffsetOnAxis(token_row[:, choice_no, t:t + 1], 0)
                                                 ).then_inc(y_loaded[choice_no][t], 16)

        @block.vector
        def _(dve):
            links = [0]

            def link(ins):
                links[0] += 1
                ins.then_inc(dve_chain, 1)
                dve.wait_ge(dve_chain, links[0])

            def lo_part(dst, src, hi):
                return nc.vector.tensor_tensor(dst, src, hi.bitcast(F32), ALU.subtract)

            def split_router(L):
                W = 32 if L == 0 else E1
                dve.wait_ge(router_hi, L + 1)
                lo_part(router_w[:, 1, :, 0:W], router_raw[:, :, 0:W], router_w[:, 0, :, 0:W]).then_inc(router_split, 1)

            def split_qk(L, p, s):
                head = 2 * p + (L * HEADS + s)
                dve.wait_ge(qk_w_hi, head + 1)
                lo_part(qk_w[:, s, 1, :, :].rearrange("p a b -> p (a b)"), qk_raw[:, s, :],
                        qk_w[:, s, 0, :, :].rearrange("p a b -> p (a b)")).then_inc(qk_w_split, 1)

            def split_v(L, p):
                dve.wait_ge(v_w_hi, p + (L * PAIRS + 1))
                lo_part(v_w[:, 1, :, :].rearrange("p a b -> p (a b)"), v_raw[:, :],
                        v_w[:, 0, :, :].rearrange("p a b -> p (a b)")).then_inc(v_w_split, 1)

            def split_o(L, p):
                dve.wait_ge(o_w_hi, p + (L * PAIRS + 1))
                lo_part(o_w[:, 1, :, :].rearrange("p a b -> p (a b)"), o_raw[:, :],
                        o_w[:, 0, :, :].rearrange("p a b -> p (a b)")).then_inc(o_w_split, 1)

            def split_gu(s, k):
                dve.wait_ge(gu_w_hi, JOBS * s + (k + 1))
                cols = slice(JOB_AT[k], JOB_AT[k] + JOB_COLS[k])
                lo_part(gu_w[:, 1, cols], gu_raw[:, cols], gu_w[:, 0, cols]).then_inc(gu_w_split, 1)

            def split_down1(s, weights=down1_w):
                dve.wait_ge(down1_w_hi, s + 1)
                lo_part(weights[:, 1, :, :].rearrange("p a b -> p (a b)"), down1_raw[:, :],
                        weights[:, 0, :, :].rearrange("p a b -> p (a b)")).then_inc(down1_w_split, 1)

            def take_rows(s, parity, bank):
                dve.wait_ge(xs_hi, s + 1)
                lo_part(xs_t[:, parity, 1, :, :].rearrange("p c r -> p (c r)"), psum[:, bank, :],
                        xs_t[:, parity, 0, :, :].rearrange("p c r -> p (c r)")).then_inc(xs_split, 1)

            def variances(L, half):
                tiles = range(4 * half, 4 * half + 4)
                if L == 0:
                    dve.wait_ge(x_loaded[half], 16)
                for t in tiles:
                    if L == 1 and t % 2 == 0:
                        dve.wait_ge(y_added, 4 * (UNITS - 2) + last_jobs.index((UNITS - 1, t // 2)) + 1)
                    last = nc.vector.bn_stats(stats[:, t, :], x_sb[:, t, :])
                link(last)
                for t in tiles:
                    last = nc.vector.bn_aggr(mean_var[:, t, :], stats[:, t, :])
                link(last)
                four = slice(4 * half, 4 * half + 4)
                nc.vector.tensor_scalar(var_eps[:, four], mean_var[:, four, 1], EPS, None,
                                        ALU.add).then_inc(var_ready, 1)

            def normalise_x(L, half):
                four = slice(4 * half, 4 * half + 4)
                r, v, n = rstd[:, four], var_eps[:, four], newton[:, four]
                dve.wait_ge(std_ready, 2 * L + half + 1)
                link(nc.vector.reciprocal(r, std[:, four]))
                link(nc.vector.tensor_tensor(n, r, r, ALU.mult))
                link(nc.vector.tensor_tensor(n, n, v, ALU.mult))
                link(nc.vector.tensor_scalar(n, n, -0.5, 1.5, ALU.mult, ALU.add))
                link(nc.vector.tensor_tensor(r, r, n, ALU.mult))
                for t in range(4 * half, 4 * half + 4):
                    nc.vector.tensor_scalar(xn[L][:, t, :], x_sb[:, t, :], mean_var[:, t, 0:1], rstd[:, t:t + 1],
                                            ALU.subtract, ALU.mult).then_inc(xn_ready, 1)

            def split_xn(L, half):
                for kc in range(KC):
                    dve.wait_ge(xn_hi, 4 * L + 2 * half + kc + 1)
                    cols = slice(half * HALF, (half + 1) * HALF)
                    lo_part(xn_t[:, 1, kc, cols], psum[:, 2 + 2 * half + kc, :],
                            xn_t[:, 0, kc, cols]).then_inc(xn_split, 1)

            def rank_of(values, n, tiles, ahead, tie, tri, out):
                shape = [P, tiles, n, n]
                a = ahead[:, 0:tiles * n * n].rearrange("p (t i j) -> p t i j", t=tiles, i=n)
                b = tie[:, 0:tiles * n * n].rearrange("p (t i j) -> p t i j", t=tiles, i=n)
                other = values.unsqueeze(2).to_broadcast(shape)
                own = values.unsqueeze(3).to_broadcast(shape)
                nc.vector.tensor_tensor(a, other, own, ALU.is_gt)
                link(nc.vector.tensor_tensor(b, other, own, ALU.is_equal))
                link(nc.vector.tensor_tensor(b, b, tri.unsqueeze(1).to_broadcast(shape), ALU.mult))
                link(nc.vector.tensor_tensor(a, a, b, ALU.add))
                link(nc.vector.tensor_reduce(out, a, X_AXIS, ALU.add))

            def router_scores(L):
                W = 32 if L == 0 else E1
                dve.wait_ge(logits_done, L + 1)
                link(nc.vector.tensor_copy(logits[:, :, 0:W],
                                           psum[:, 6, 0:TILES * W].rearrange("p (t w) -> p t w", t=TILES)))
                if L == 0:
                    nc.vector.memset(coef[:, :, E0:UNITS], 1.0).then_inc(logits_copied, 1)
                    dve.wait_ge(logits_exp, 1)
                    link(nc.vector.tensor_scalar(sig[:, :, :], sig[:, :, :], 1.0, None, ALU.add))
                    link(nc.vector.reciprocal(sig[:, :, :], sig[:, :, :]))
                else:
                    link(nc.vector.tensor_reduce(per_tile[:, 0, :], logits[:, :, 0:E1], X_AXIS, ALU.max))
                    nc.vector.tensor_tensor(logits[:, :, 0:E1], logits[:, :, 0:E1],
                                            per_tile[:, 0, :].unsqueeze(2).to_broadcast([P, TILES, E1]),
                                            ALU.subtract).then_inc(logits_copied, 1)
                    dve.wait_ge(logits_exp, 2)
                    link(nc.vector.tensor_reduce(per_tile[:, 0, :], sig[:, :, 0:E1], X_AXIS, ALU.add))
                    link(nc.vector.reciprocal(per_tile[:, 1, :], per_tile[:, 0, :]))
                    link(nc.vector.tensor_tensor(sig[:, :, 0:E1], sig[:, :, 0:E1],
                                                 per_tile[:, 1, :].unsqueeze(2).to_broadcast([P, TILES, E1]), ALU.mult))

            def choose0_groups():
                prob = sig[:, :, 0:E0]
                link(nc.vector.tensor_tensor(choice[:, :, :], prob,
                                             e_bias.unsqueeze(1).to_broadcast([P, TILES, E0]), ALU.add))
                four = choice[:, :, :].rearrange("p t (g e) -> p (t g) e", e=4)
                a, b, c, d = (four[:, :, i] for i in range(4))
                s = [small[:, i, :] for i in range(8)]
                nc.vector.tensor_tensor(s[0], a, b, ALU.max)
                nc.vector.tensor_tensor(s[1], a, b, ALU.min)
                nc.vector.tensor_tensor(s[2], c, d, ALU.max)
                link(nc.vector.tensor_tensor(s[3], c, d, ALU.min))
                nc.vector.tensor_tensor(s[4], s[0], s[2], ALU.max)
                nc.vector.tensor_tensor(s[5], s[0], s[2], ALU.min)
                link(nc.vector.tensor_tensor(s[6], s[1], s[3], ALU.max))
                link(nc.vector.tensor_tensor(s[7], s[5], s[6], ALU.max))
                link(nc.vector.tensor_tensor(groups[:, :, :], s[4].rearrange("p (t g) -> p t g", g=4),
                                             s[7].rearrange("p (t g) -> p t g", g=4), ALU.add))
                rank_of(groups[:, :, :], 4, TILES, beats, ties, tri4, rank[:, :, 0:4])
                link(nc.vector.tensor_scalar(groups[:, :, :], rank[:, :, 0:4], 2.0, None, ALU.is_lt))
                by_group = choice[:, :, :].rearrange("p t (g e) -> p t g e", e=4)
                link(nc.vector.tensor_tensor(by_group, by_group,
                                             groups[:, :, :].unsqueeze(3).to_broadcast([P, TILES, 4, 4]), ALU.mult))

            def choose0_rank(t):
                rank_of(choice[:, t:t + 4, :], E0, 4, beats, ties, tri16, rank[:, t:t + 4, :])

            def choose0_weights():
                prob = sig[:, :, 0:E0]
                link(nc.vector.tensor_scalar(rank[:, :, :], rank[:, :, :], 2.0, None, ALU.is_lt))
                link(nc.vector.tensor_tensor(rank[:, :, :], rank[:, :, :], prob, ALU.mult))
                link(nc.vector.tensor_reduce(per_tile[:, 0, :], rank[:, :, :], X_AXIS, ALU.add))
                link(nc.vector.tensor_scalar(per_tile[:, 0, :], per_tile[:, 0, :], 1e-20, None, ALU.add))
                link(nc.vector.reciprocal(per_tile[:, 1, :], per_tile[:, 0, :]))
                link(nc.vector.tensor_tensor(coef[:, :, 0:E0], rank[:, :, :],
                                             per_tile[:, 1, :].unsqueeze(2).to_broadcast([P, TILES, E0]), ALU.mult))

            def choose1():
                rank_of(sig[:, :, 0:E1], E1, TILES, beats1, ties1, tri8, rank[:, :, 0:E1])
                chosen = selected.rearrange("p (t e) -> p t e", e=E1)
                nc.vector.tensor_scalar(chosen, rank[:, :, 0:E1], 2.0, None, ALU.is_lt).then_inc(selection_ready, 1)
                dve.wait_ge(selection_ready, 1)
                link(nc.vector.tensor_tensor(coef[:, :, 0:E1], chosen, sig[:, :, 0:E1], ALU.mult))

            def read_places():
                dve.wait_ge(placed, 1)
                n = TILES * E1
                dve.wait_ge(zeros_stored, 16 * 2 * (SLOTS + 1))
                nc.vector.tensor_copy(position, psum[:, score_bank[1], 0:n])
                nc.vector.tensor_copy(count, psum[:, score_bank[1], n:n + E1]).then_inc(placed_read, 1)
                dve.wait_ge(placed_read, 1)

            def choose_rows():
                link(nc.vector.tensor_scalar(used, count, 0.5, None, ALU.is_gt))
                for k in range(1, TOK // ROWS):
                    link(nc.vector.scalar_tensor_tensor(out=used, in0=count, scalar=float(k * ROWS) + 0.5, in1=used,
                                                        op0=ALU.is_gt, op1=ALU.add))
                square = by_expert.rearrange("p (i j) -> p i j", i=E1)
                link(nc.vector.tensor_tensor(square, tri8, used.unsqueeze(1).to_broadcast([P, E1, E1]), ALU.mult))
                link(nc.vector.tensor_reduce(start, square, X_AXIS, ALU.add))
                nc.vector.tensor_tensor(end_slot, start, used, ALU.add)
                by_tile = row_of.rearrange("p (t e) -> p t e", e=E1)
                before = position.rearrange("p (t e) -> p t e", e=E1)
                link(nc.vector.scalar_tensor_tensor(out=by_tile, in0=start.unsqueeze(1).to_broadcast([P, TILES, E1]),
                                                    scalar=float(ROWS), in1=before, op0=ALU.mult, op1=ALU.add))
                link(nc.vector.scalar_tensor_tensor(out=mark, in0=row_of, scalar=1.0, in1=selected,
                                                    op0=ALU.add, op1=ALU.mult))
                marks = mark.rearrange("p (t e) -> p t e", e=E1)
                nc.vector.tensor_reduce(first_mark, marks, X_AXIS, ALU.max)
                link(nc.vector.tensor_reduce(both_marks, marks, X_AXIS, ALU.add))
                nc.vector.tensor_scalar(token_row[:, 0, :], first_mark, -1.0, 0.0, ALU.add, ALU.max)
                link(nc.vector.tensor_tensor(both_marks, both_marks, first_mark, ALU.subtract))
                nc.vector.tensor_scalar(token_row[:, 1, :], both_marks, -1.0, 0.0, ALU.add, ALU.max)
                for choice_no, compare in enumerate((ALU.is_equal, ALU.is_lt)):
                    link(nc.vector.tensor_tensor(by_tile, marks, first_mark.unsqueeze(2).to_broadcast([P, TILES, E1]),
                                                 compare))
                    link(nc.vector.tensor_tensor(by_tile, by_tile, coef[:, :, 0:E1], ALU.mult))
                    link(nc.vector.tensor_reduce(weight[:, choice_no, :], by_tile, X_AXIS, ALU.add))
                ends = past.rearrange("p (s e) -> p s e", e=E1 - 1)
                link(nc.vector.tensor_tensor(ends, slot_number.unsqueeze(2).to_broadcast([P, SLOTS, E1 - 1]),
                                             end_slot[:, 0:E1 - 1].unsqueeze(1).to_broadcast([P, SLOTS, E1 - 1]),
                                             ALU.is_ge))
                link(nc.vector.tensor_reduce(expert_of, ends, X_AXIS, ALU.add))
                nc.vector.scalar_tensor_tensor(out=weight_row[:, 0:SLOTS], in0=expert_of, scalar=float(P),
                                               in1=own_row.to_broadcast([P, SLOTS]), op0=ALU.mult,
                                               op1=ALU.add).then_inc(rows_ready, 1)

            def clip_scores(head, two):
                for b in two:
                    dve.wait_ge(scores_done, 4 * head + (b + 1))
                    nc.vector.tensor_scalar(sc[:, b, :], psum[:, score_bank[b % 2], 0:3 * P], -CLIP / SCALE,
                                            CLIP / SCALE, ALU.max, ALU.min).then_inc(scores_read, 1)

            def bias_and_max(head, b, s):
                own = head - HEADS
                for c, (lo, hi) in enumerate(((0, P), (P, 3 * P))):
                    nc.vector.tensor_tensor_reduce(out=sc[:, b, lo:hi], in0=sc[:, b, lo:hi], in1=alibi[:, s, lo:hi],
                                                   scale=SCALE, scalar=NEG, op0=ALU.add, op1=ALU.max,
                                                   accum_out=row_max[:, b, c:c + 1]).then_inc(max_ready, 1)
                dve.wait_ge(max_ready, 8 * own + (2 * b + 2))
                nc.vector.tensor_scalar(neg_max[:, b, :], row_max[:, b, :], -1.0, None,
                                        ALU.mult).then_inc(negmax_ready, 1)

            def normalise(L, head, b, gate_at):
                dve.wait_ge(exp_done, 8 * head + (2 * b + 2))
                nc.vector.reciprocal(row_scale[:, b, :], row_sum[:, b, :]).then_inc(recip_done, 1)
                dve.wait_ge(recip_done, 4 * head + (b + 1))
                if L == 0:
                    nc.vector.tensor_tensor(row_scale[:, b, :], row_scale[:, b, :], gate_at(b),
                                            ALU.mult).then_inc(row_scaled, 1)
                    dve.wait_ge(row_scaled, 4 * head + (b + 1))
                nc.vector.tensor_scalar(pr[:, b, 0:P], pr[:, b, 0:P], row_scale[:, b, 0:1], None, ALU.mult)
                nc.vector.tensor_scalar(pr[:, b, P:3 * P], pr[:, b, P:3 * P], row_scale[:, b, 1:2], None,
                                        ALU.mult).then_inc(probs_ready, 1)

            def softmax(L, p, s, adding=None):
                head = 2 * p + (L * HEADS + s)

                def gate_at(b):
                    return sig[:, 2 * b:2 * b + 2, bass.ds(2 * p + (E0 + s), 1)].rearrange("p a b -> p (a b)")

                def add(j):
                    if adding is not None:
                        add_out(adding, j)

                if L == 1:
                    bias_and_max(head, 0, s)
                    bias_and_max(head, 1, s)
                    clip_scores(head, (2, 3))
                    dve.wait_ge(scores_read, 4 * head + 4)
                normalise(L, head, 0, gate_at)
                if L == 1:
                    bias_and_max(head, 2, s)
                add(0)
                normalise(L, head, 1, gate_at)
                if L == 1:
                    bias_and_max(head, 3, s)
                add(1)
                normalise(L, head, 2, gate_at)
                add(2)
                normalise(L, head, 3, gate_at)
                add(3)

            def take_z(head, s):
                for j in range(2):
                    dve.wait_ge(z_hi, 2 * head + (j + 1))
                    cols = slice(j * HALF, (j + 1) * HALF)
                    lo_part(z_p[:, s, 1, cols], psum[:, z_bank[j], :], z_p[:, s, 0, cols]).then_inc(z_split, 1)

            def add_out(pair, j):
                dve.wait_ge(o_done, 4 * pair + (j + 1))
                x2 = x_sb[:, 2 * j:2 * j + 2, :].rearrange("p a b -> p (a b)")
                nc.vector.tensor_tensor(x2, psum[:, proj_bank[j % 2], :], x2, ALU.add).then_inc(o_added, 1)

            def pair_steps(L, p, first=False, last=False, placing=False):
                pair = p + L * PAIRS
                if L == 1:
                    clip_scores(2 * pair, (0, 1))
                    dve.wait_ge(alibi_loaded[0], 16 * p + 16)
                    dve.wait_ge(scores_read, 8 * pair + 2)
                    if not last:
                        split_qk(L, p + 1, 0)
                softmax(L, p, 0)
                if L == 0 and not last:
                    split_qk(L, p + 1, 0)
                if not first:
                    split_o(L, p - 1)
                if L == 0 and first:
                    choose0_groups()
                if L == 0 and last:
                    choose0_rank(4)
                if L == 1 and last:
                    split_gu(0, 0)
                    split_gu(0, 1)
                if not first:
                    take_z(2 * pair - 1, 1)
                if placing:
                    read_places()
                if L == 1:
                    clip_scores(2 * pair + 1, (0, 1))
                    dve.wait_ge(alibi_loaded[1], 16 * p + 16)
                    dve.wait_ge(scores_read, 8 * pair + 6)
                    if not last:
                        split_qk(L, p + 1, 1)
                softmax(L, p, 1, adding=None if first else pair - 1)
                if not last:
                    if L == 0:
                        split_qk(L, p + 1, 1)
                    split_v(L, p + 1)
                if L == 0 and first:
                    choose0_rank(0)
                if L == 1 and first:
                    choose1()
                if L == 1 and last:
                    take_rows(0, 0, score_bank[0])
                take_z(2 * pair, 0)
                if placing:
                    choose_rows()
                if last:
                    split_o(L, p)
                if L == 1 and last:
                    split_gu(0, 2)
                if L == 0 and last:
                    choose0_weights()

            def hidden_lo(u, s, halves=(0, 1)):
                for half in halves:
                    dve.wait_ge(hid_hi, 2 * u + (half + 1))
                    cols = slice(half * HALF, (half + 1) * HALF)
                    lo_part(h0_p[:, s, 1, cols], hid[:, half, :], h0_p[:, s, 0, cols]).then_inc(hid_split, 1)

            def add_two(u, j, n):
                dve.wait_ge(down_done, n + 1)
                if isinstance(n, int) and n < 4:
                    dve.wait_ge(o_added, 4 * (PAIRS - 1) + j + 1)
                elif isinstance(n, int) and n >= 4 * (UNITS - 2):
                    dve.wait_ge(y_added, n - 1)
                else:
                    dve.wait_ge(y_added, n - 3)
                bank = down_bank[n % 4 if isinstance(n, int) else j]
                for i in range(2):
                    t = 2 * j + i
                    last = nc.vector.scalar_tensor_tensor(
                        out=x_sb[:, t, :], in0=psum[:, bank, i * D:(i + 1) * D],
                        scalar=coef[:, t, bass.ds(u, 1)], in1=x_sb[:, t, :], op0=ALU.mult, op1=ALU.add)
                last.then_inc(y_added, 1)

            def add_unit(u):
                for j in range(4):
                    add_two(u, j, 4 * u + j)

            def unit(u, s):
                hidden_lo(u, s)
                add_unit(u - 1)

            def multiply(s, parity, k):
                n, at = JOBS * s + k, (JOBS * parity + k) % 2
                dve.wait_ge(silu_done, n + 1)
                if not (isinstance(s, int) and JOBS * s + k < 2):
                    dve.wait_ge(hid1_split, n - 1)
                if k < JOBS - 1:
                    last = nc.vector.tensor_tensor(hid1[:, at, :, :], gate1[:, at, :, :],
                                                   psum[:, 2 * at:2 * at + 2, ROWS:2 * ROWS], ALU.mult)
                else:
                    nc.vector.tensor_tensor(hid1[:, at, 0, :], gate1[:, at, 0, :], psum[:, 2 * at, ROWS:2 * ROWS],
                                            ALU.mult)
                    last = nc.vector.tensor_tensor(hid1[0:TAIL, at, 1, :], gate1[0:TAIL, at, 1, :],
                                                   psum[TAIL:2 * TAIL, 2 * at + 1, 0:ROWS], ALU.mult)
                last.then_inc(mul_done, 1)

            def take_hidden(s, parity, k):
                dve.wait_ge(hid1_hi, JOBS * s + (k + 1))
                at = (JOBS * parity + k) % 2
                if k < JOBS - 1:
                    last = lo_part(h1_p[:, parity, 1, 2 * k:2 * k + 2, :], hid1[:, at, :, :],
                                   h1_p[:, parity, 0, 2 * k:2 * k + 2, :])
                else:
                    lo_part(h1_p[:, parity, 1, 2 * k, :], hid1[:, at, 0, :], h1_p[:, parity, 0, 2 * k, :])
                    last = lo_part(h1_p[0:TAIL, parity, 1, FULL, :], hid1[0:TAIL, at, 1, :],
                                   h1_p[0:TAIL, parity, 0, FULL, :])
                last.then_inc(hid1_split, 1)

            def slot(s, parity):
                multiply(s, parity, 0)
                take_hidden(s - 1, 1 - parity, 2)
                split_gu(s + 1, 0)
                take_rows(s + 1, 1 - parity, 7 - parity)
                multiply(s, parity, 1)
                take_hidden(s, parity, 0)
                split_gu(s + 1, 1)
                take_hidden(s, parity, 1)
                split_down1(s)
                multiply(s, parity, 2)
                split_gu(s + 1, 2)

            def last_slot(s):
                multiply(s, 0, 0)
                take_hidden(s - 1, 1, 2)
                multiply(s, 0, 1)
                take_hidden(s, 0, 0)
                split_down1(s, last_down_w)
                take_hidden(s, 0, 1)
                multiply(s, 0, 2)
                take_hidden(s, 0, 2)

            def add_choice(choice_no, t):
                dve.wait_ge(y_loaded[choice_no][t], 16)
                if choice_no == 0:
                    dve.wait_ge(final, t + 1)
                nc.vector.scalar_tensor_tensor(out=x_sb[:, t, :], in0=y_back[:, t, choice_no, :],
                                               scalar=weight[:, choice_no, t:t + 1], in1=x_sb[:, t, :],
                                               op0=ALU.mult, op1=ALU.add).then_inc(final, 1)

            for L in range(2):
                variances(L, 0)
                normalise_x(L, 0)
                if L == 1:
                    for n in range(4, 6):
                        add_two(*last_jobs[n], 4 * (UNITS - 2) + n)
                    split_qk(L, 0, 0)
                    split_xn(L, 0)
                    for n in range(6, 8):
                        add_two(*last_jobs[n], 4 * (UNITS - 2) + n)
                    variances(L, 1)
                else:
                    variances(L, 1)
                    split_qk(L, 0, 0)
                    split_xn(L, 0)
                normalise_x(L, 1)
                split_router(L)
                split_xn(L, 1)
                split_v(L, 0)
                split_qk(L, 0, 1)
                router_scores(L)
                pair_steps(L, 0, first=True)
                if L == 1:
                    pair_steps(L, 1, placing=True)
                with dve.Fori(1 + L, PAIRS - 1) as p:
                    pair_steps(L, p)
                pair_steps(L, PAIRS - 1, last=True)
                end = L * HEADS + HEADS - 1

                def add_last_out():
                    for j in range(4):
                        add_out(L * PAIRS + PAIRS - 1, j)

                if L == 0:
                    hidden_lo(0, 0)
                    take_z(end, 1)
                    add_last_out()
                    unit(1, 1)
                    with dve.Fori(1, UNITS // 2 - 1) as i:
                        unit(2 * i, 0)
                        unit(2 * i + 1, 1)
                    unit(UNITS - 2, 0)
                    for n in range(4):
                        if n < 2:
                            hidden_lo(UNITS - 1, 1, halves=(n,))
                        add_two(*last_jobs[n], 4 * (UNITS - 2) + n)
                else:
                    multiply(0, 0, 0)
                    take_z(end, 1)
                    split_gu(1, 0)
                    multiply(0, 0, 1)
                    take_hidden(0, 0, 0)
                    add_last_out()
                    split_gu(1, 1)
                    take_rows(1, 1, 7)
                    multiply(0, 0, 2)
                    take_hidden(0, 0, 1)
                    split_down1(0)
                    split_gu(1, 2)
                    slot(1, 1)
                    with dve.Fori(1, (SLOTS - 1) // 2) as i:
                        slot(2 * i, 0)
                        slot(2 * i + 1, 1)
                    last_slot(SLOTS - 1)
                    dve.wait_ge(o_added, 8 * PAIRS)
                    for choice_no in (1, 0):
                        for t in range(TILES):
                            add_choice(choice_no, t)


def kernel(L0_attn_x, L0_attn_w_qkv, L0_attn_w_gates, L0_attn_w_out, L0_ffn_router_weight, L0_ffn_e_bias,
           L0_ffn_w_up, L0_ffn_w_down, L0_ffn_shared_up, L0_ffn_shared_down, L1_attn_Wq, L1_attn_Wk, L1_attn_Wv,
           L1_attn_Wo, L1_ffn_router_w, L1_ffn_gate_w, L1_ffn_up_w, L1_ffn_down_w):
    import numpy as np
    import concourse.bacc as bacc
    from concourse.bass_utils import run_bass_kernel_spmd

    def a(v):
        return np.asarray(v)

    def chunks(w):
        return w.reshape(KC, P, -1).transpose(1, 0, 2)

    def attention_weights(wq, wk, wv, wo):
        q, k = (chunks(w).reshape(P, KC, HEADS, P).transpose(2, 0, 1, 3) for w in (wq, wk))
        qk = np.concatenate([q, k], axis=3).reshape(HEADS, P, KC * 2 * P)
        v = chunks(wv).reshape(P, KC, PAIRS, 2 * P).transpose(2, 0, 1, 3).reshape(PAIRS, P, KC * 2 * P)
        o = wo.reshape(PAIRS, 2, P, D).transpose(0, 2, 1, 3).reshape(PAIRS, P, 2 * D)
        return qk, v, o

    HD = HEADS * P
    qkv = a(L0_attn_w_qkv)
    layer0 = attention_weights(qkv[:, 0:HD], qkv[:, HD:2 * HD], qkv[:, 2 * HD:3 * HD], a(L0_attn_w_out))
    layer1 = attention_weights(a(L1_attn_Wq).T, a(L1_attn_Wk).T, a(L1_attn_Wv).T, a(L1_attn_Wo).T)
    router0 = chunks(np.concatenate([a(L0_ffn_router_weight).T, a(L0_attn_w_gates)], axis=1))
    router1 = chunks(a(L1_ffn_router_w).T)
    ups = np.concatenate([a(L0_ffn_w_up), a(L0_ffn_shared_up).reshape(D, SHARED, P).transpose(1, 0, 2)])
    ups = ups.reshape(UNITS, KC, P, P).transpose(0, 2, 1, 3).reshape(UNITS, P, KC * P)
    downs = np.concatenate([a(L0_ffn_w_down), a(L0_ffn_shared_down).reshape(SHARED, P, D)])
    wide = FULL * P

    def inner(w):
        w = w.transpose(0, 2, 1).reshape(E1, KC, P, -1).transpose(0, 2, 1, 3)
        return w[..., 0:wide].reshape(E1, P, KC, FULL, P).transpose(0, 1, 3, 2, 4), w[..., wide:]

    (g, g_tail), (u, u_tail) = inner(a(L1_ffn_gate_w)), inner(a(L1_ffn_up_w))
    gu = np.concatenate([np.concatenate([g, u], axis=4).reshape(E1, P, -1),
                         np.concatenate([g_tail, u_tail], axis=3).reshape(E1, P, -1)], axis=2)
    d1 = np.zeros((E1, CH * P, D), np.float32)
    d1[:, 0:wide + TAIL, :] = a(L1_ffn_down_w).transpose(0, 2, 1)
    d1 = d1.reshape(E1, CH, P, D).transpose(0, 2, 1, 3).reshape(E1 * P, CH * D)
    gu = gu.reshape(E1 * P, GU)

    def before(n):
        return np.broadcast_to(np.tril(np.ones((n, n), np.float32), -1).reshape(1, n * n), (P, n * n))

    const = np.concatenate([np.eye(P, dtype=np.float32), np.broadcast_to(a(L0_ffn_e_bias)[None, :], (P, E0)),
                            before(16), before(4), before(8),
                            np.where(np.arange(P)[None, :] > np.arange(P)[:, None], NEG, 0.0).astype(np.float32)],
                           axis=1)
    row, number = np.arange(P)[:, None], np.arange(15)[None, :]
    route = np.concatenate([row < np.arange(P)[None, :], np.ones((P, P)), np.broadcast_to(number, (P, 15)), row],
                           axis=1).astype(np.float32)
    start = 2.0 ** (-8.0 / HEADS)
    slopes = np.array([start * start ** i for i in range(HEADS)], np.float32).astype(np.float64)
    query, key = np.arange(P)[:, None], np.arange(2 * P)[None, :]
    line = slopes[:, None, None] * key[None] * (P ** 0.5)
    alibi = np.concatenate([np.where(key[None, :, 0:P] > query[None], NEG, line[:, :, 0:P]),
                            np.where(key[None] > query[None] + P, NEG, line)], axis=2).astype(np.float32)

    arrays, args = {}, []
    nc = bacc.Bacc("TRN2", target_bir_lowering=False, num_devices=1)

    def give(name, array):
        arrays[name] = np.ascontiguousarray(array)
        return nc.dram_tensor(name, arrays[name].shape, F32, kind="ExternalInput").ap()

    x_d = give("x", a(L0_attn_x).reshape(TILES, P, D).transpose(1, 0, 2))
    const_d = give("const_in", const)
    alibi_d = give("alibi_in", alibi)
    qk_d, v_d, o_d = ([give(f"{n}{i}", w[k]) for i, w in enumerate((layer0, layer1))]
                      for k, n in enumerate(("w_qk", "w_v", "w_o")))
    router_d = [give("router0", router0), give("router1", router1)]
    up_d, down_d = give("w_up0", ups), give("w_down0", downs)
    gu_d = [give(f"w_gate_up1_{k}", gu[:, JOB_AT[k]:JOB_AT[k] + JOB_COLS[k]]) for k in range(JOBS)]
    down1_d, route_d = give("w_down1", d1), give("route_in", route)
    sorted_d = nc.dram_tensor("sorted_rows", (SLOTS * ROWS, D), F32, kind="Internal").ap()
    outputs_d = nc.dram_tensor("expert_outputs", (SLOTS * ROWS, D), F32, kind="Internal").ap()
    out_d = nc.dram_tensor("out", (P, TILES, D), F32, kind="ExternalOutput").ap()
    bass_two_layers(nc, x_d, const_d, alibi_d, qk_d, v_d, o_d, router_d, up_d, down_d, gu_d, down1_d, route_d,
                    sorted_d, outputs_d, out_d)
    r = run_bass_kernel_spmd(nc, [arrays], core_ids=[0])
    return r.results[0]["out"].transpose(1, 0, 2).reshape(SEQS, 2 * P, D)
```
